# Optimizing a Trainium2 kernel written in Bass

```python
import numpy as np
import jax
import jax.numpy as jnp

def _softmax(x, axis=-1):
    return jax.nn.softmax(x, axis=axis)

def _gelu(x):
    return jax.nn.gelu(x, approximate=True)

def _silu(x):
    return jax.nn.silu(x)

def _sigmoid(x):
    return jax.nn.sigmoid(x)

def _layernorm(x, axis=-1, eps=1e-05):
    m = jnp.mean(x, axis=axis, keepdims=True)
    v = jnp.var(x, axis=axis, keepdims=True)
    return (x - m) / jnp.sqrt(v + eps)

def _scatter_add(tgt, idx, src, axis=0):
    return tgt.at[idx].add(src)

def _segment_sum(src, seg, n):
    return jax.ops.segment_sum(src, seg, n)
kernel_name = 'mk_perceiver_d1_seqx_r2_2c8477'

def setup_inputs(seed: int=0):
    np.random.seed(seed)
    _w = jnp.asarray

    def _rec_inputs():
        import jax
        import jax.numpy as jnp
        _rk = jax.random.key(seed)
        x = 7.22e-05 + 1 * jax.random.normal(jax.random.fold_in(_rk, 1), (1, 512, 512), jnp.float32)
        _lenS = 512 - jax.random.randint(jax.random.fold_in(_rk, 7), (1,), 0, max(1, 512 // 4) + 1, jnp.int32)
        _lenS2 = 8192 - jax.random.randint(jax.random.fold_in(_rk, 8), (1,), 0, max(1, 8192 // 4) + 1, jnp.int32)
        _ctx_1024P = jax.random.normal(jax.random.fold_in(_rk, 11), (1, 16, 512), jnp.float32)
        _ctx_1024c = jax.random.dirichlet(jax.random.fold_in(_rk, 511), 0.3 * jnp.ones((16,), jnp.float32), (1, 8192))
        _ctx_1024t = jnp.einsum('bsk,bkd->bsd', _ctx_1024c, _ctx_1024P)
        _ctx_1024t = _ctx_1024t * jax.lax.rsqrt(jnp.mean(jnp.square(_ctx_1024t)) + 1e-12) * 0.953939
        ctx_1024 = -0.000514642 + 1.00011 * (_ctx_1024t + 0.3 * jax.random.normal(jax.random.fold_in(_rk, 611), (1, 8192, 512), jnp.float32))
        return (x, ctx_1024)
    x, ctx_1024 = _rec_inputs()

    def _L0_xattn_setup():
        import jax, jax.numpy as jnp
        import numpy as np
        B, L_ENC, L_DEC, D = (16, 256, 128, 512)
        key = jax.random.key(seed)
        k1, k2, k3, k4, k5, k6 = jax.random.split(key, 6)
        encoder_hc = jax.random.normal(k1, (B, L_ENC, D), dtype=jnp.float32)
        decoder_hq = jax.random.normal(k2, (B, L_DEC, D), dtype=jnp.float32)
        w_sim = jax.random.normal(k3, (3 * D,), dtype=jnp.float32) * 0.02
        b_sim = jax.random.normal(k4, (1,), dtype=jnp.float32) * 0.02
        W_qv = jax.random.normal(k5, (4 * D, D), dtype=jnp.float32) * 0.02
        b_qv = jax.random.normal(k6, (D,), dtype=jnp.float32) * 0.02
        return {'encoder_hc': encoder_hc, 'decoder_hq': decoder_hq, 'w_sim': w_sim, 'b_sim': b_sim, 'W_qv': W_qv, 'b_qv': b_qv}
    _L0_xattn_all = _L0_xattn_setup()
    _L0_xattn_in = {k: v for k, v in _L0_xattn_all.items() if k in ('w_sim', 'b_sim', 'W_qv', 'b_qv')}
    del _L0_xattn_all

    def _L0_attn_setup():
        import jax, jax.numpy as jnp
        import numpy as np
        EMB = 512
        NQ = 16
        NKV = 4
        D = 64
        B, S = (1, 1024)
        ROPE_BASE = 10000.0

        def _rotary(t):
            d = t.shape[-1]
            inv_freq = 1.0 / ROPE_BASE ** (jnp.arange(0, d, 2, dtype=jnp.float32) / d)
            pos = jnp.arange(t.shape[1], dtype=jnp.float32)
            ang = pos[:, None] * inv_freq[None, :]
            cos = jnp.concatenate([jnp.cos(ang), jnp.cos(ang)], axis=-1)[None, :, None, :]
            sin = jnp.concatenate([jnp.sin(ang), jnp.sin(ang)], axis=-1)[None, :, None, :]
            x1, x2 = (t[..., :d // 2], t[..., d // 2:])
            t_rot = jnp.concatenate([-x2, x1], axis=-1)
            return t * cos + t_rot * sin
        key = jax.random.key(seed)
        ks = jax.random.split(key, 5)
        std = 0.02
        return {'x': jax.random.normal(ks[0], (B, S, EMB), jnp.float32), 'Wq': jax.random.normal(ks[1], (EMB, NQ * D), jnp.float32) * std, 'bq': jnp.zeros((NQ * D,), jnp.float32), 'Wk': jax.random.normal(ks[2], (EMB, NKV * D), jnp.float32) * std, 'bk': jnp.zeros((NKV * D,), jnp.float32), 'Wv': jax.random.normal(ks[3], (EMB, NKV * D), jnp.float32) * std, 'bv': jnp.zeros((NKV * D,), jnp.float32), 'Wo': jax.random.normal(ks[4], (NQ * D, EMB), jnp.float32) * std, 'bo': jnp.zeros((EMB,), jnp.float32)}
    _L0_attn_all = _L0_attn_setup()
    _L0_attn_in = {k: v for k, v in _L0_attn_all.items() if k in ('Wq', 'bq', 'Wk', 'bk', 'Wv', 'bv', 'Wo', 'bo')}
    del _L0_attn_all

    def _L0_ffn_setup():
        import jax, jax.numpy as jnp
        import numpy as np
        H = 512
        I = 1024
        E = 8
        B, S = (2, 512)

        def _swiglu(x, wg, wu, wd):
            return jax.nn.silu(x @ wg) * (x @ wu) @ wd
        key = jax.random.key(seed)
        ks = jax.random.split(key, 8)
        sc_h = 1.0 / np.sqrt(H)
        sc_i = 1.0 / np.sqrt(I)
        return {'hidden_states': jax.random.normal(ks[0], (B, S, H), jnp.float32), 'gate_w': jax.random.normal(ks[1], (H, E), jnp.float32) * sc_h, 'sh_gate': jax.random.normal(ks[2], (H, I), jnp.float32) * sc_h, 'sh_up': jax.random.normal(ks[3], (H, I), jnp.float32) * sc_h, 'sh_down': jax.random.normal(ks[4], (I, H), jnp.float32) * sc_i, 'rt_gate': jax.random.normal(ks[5], (E, H, I), jnp.float32) * sc_h, 'rt_up': jax.random.normal(ks[6], (E, H, I), jnp.float32) * sc_h, 'rt_down': jax.random.normal(ks[7], (E, I, H), jnp.float32) * sc_i}
    _L0_ffn_all = _L0_ffn_setup()
    _L0_ffn_in = {k: v for k, v in _L0_ffn_all.items() if k in ('gate_w', 'sh_gate', 'sh_up', 'sh_down', 'rt_gate', 'rt_up', 'rt_down')}
    del _L0_ffn_all
    return {'x': x, 'ctx_1024': ctx_1024, 'L0_xattn_w_sim': _L0_xattn_in['w_sim'], 'L0_xattn_b_sim': _L0_xattn_in['b_sim'], 'L0_xattn_W_qv': _L0_xattn_in['W_qv'], 'L0_xattn_b_qv': _L0_xattn_in['b_qv'], 'L0_attn_Wq': _L0_attn_in['Wq'], 'L0_attn_bq': _L0_attn_in['bq'], 'L0_attn_Wk': _L0_attn_in['Wk'], 'L0_attn_bk': _L0_attn_in['bk'], 'L0_attn_Wv': _L0_attn_in['Wv'], 'L0_attn_bv': _L0_attn_in['bv'], 'L0_attn_Wo': _L0_attn_in['Wo'], 'L0_attn_bo': _L0_attn_in['bo'], 'L0_ffn_gate_w': _L0_ffn_in['gate_w'], 'L0_ffn_sh_gate': _L0_ffn_in['sh_gate'], 'L0_ffn_sh_up': _L0_ffn_in['sh_up'], 'L0_ffn_sh_down': _L0_ffn_in['sh_down'], 'L0_ffn_rt_gate': _L0_ffn_in['rt_gate'], 'L0_ffn_rt_up': _L0_ffn_in['rt_up'], 'L0_ffn_rt_down': _L0_ffn_in['rt_down']}

def reference(x, ctx_1024, L0_xattn_w_sim, L0_xattn_b_sim, L0_xattn_W_qv, L0_xattn_b_qv, L0_attn_Wq, L0_attn_bq, L0_attn_Wk, L0_attn_bk, L0_attn_Wv, L0_attn_bv, L0_attn_Wo, L0_attn_bo, L0_ffn_gate_w, L0_ffn_sh_gate, L0_ffn_sh_up, L0_ffn_sh_down, L0_ffn_rt_gate, L0_ffn_rt_up, L0_ffn_rt_down):
    import jax
    import jax.numpy as jnp

    def _L0_xattn_ref(encoder_hc, decoder_hq, w_sim, b_sim, W_qv, b_qv):
        import jax, jax.numpy as jnp
        import numpy as np
        B, L_ENC, L_DEC, D = (16, 256, 128, 512)
        d = encoder_hc.shape[-1]
        w1, w2, w3 = (w_sim[:d], w_sim[d:2 * d], w_sim[2 * d:])
        Sim = (encoder_hc @ w1)[:, :, None] + (decoder_hq @ w2)[:, None, :] + jnp.einsum('bid,bjd->bij', encoder_hc * w3, decoder_hq) + b_sim[0]
        A = jax.nn.softmax(Sim, axis=2)
        hq_hat = jnp.einsum('bij,bjd->bid', A, decoder_hq)
        Batt = jax.nn.softmax(jnp.max(Sim, axis=2), axis=1)
        hc_bar = jnp.einsum('bi,bid->bd', Batt, encoder_hc)[:, None, :]
        hc_hat = jnp.broadcast_to(hc_bar, encoder_hc.shape)
        feats = jnp.concatenate([encoder_hc, hq_hat, encoder_hc * hq_hat, encoder_hc * hc_hat], axis=-1)
        hcq = feats @ W_qv + b_qv
        return hcq

    def _L0_attn_ref(x, Wq, bq, Wk, bk, Wv, bv, Wo, bo):
        import jax, jax.numpy as jnp
        import numpy as np
        EMB = 512
        NQ = 16
        NKV = 4
        D = 64
        B, S = (1, 1024)
        ROPE_BASE = 10000.0

        def _rotary(t):
            d = t.shape[-1]
            inv_freq = 1.0 / ROPE_BASE ** (jnp.arange(0, d, 2, dtype=jnp.float32) / d)
            pos = jnp.arange(t.shape[1], dtype=jnp.float32)
            ang = pos[:, None] * inv_freq[None, :]
            cos = jnp.concatenate([jnp.cos(ang), jnp.cos(ang)], axis=-1)[None, :, None, :]
            sin = jnp.concatenate([jnp.sin(ang), jnp.sin(ang)], axis=-1)[None, :, None, :]
            x1, x2 = (t[..., :d // 2], t[..., d // 2:])
            t_rot = jnp.concatenate([-x2, x1], axis=-1)
            return t * cos + t_rot * sin
        b, s, _ = x.shape
        g = NQ // NKV
        q = (x @ Wq + bq).reshape(b, s, NQ, D)
        k = (x @ Wk + bk).reshape(b, s, NKV, D)
        v = (x @ Wv + bv).reshape(b, s, NKV, D)
        q = _rotary(q)
        k = _rotary(k)
        qg = q.reshape(b, s, NKV, g, D)
        scale = 1.0 / jnp.sqrt(jnp.float32(D))
        logits = jnp.einsum('bqhgd,bkhd->bhgqk', qg, k) * scale
        causal = jnp.tril(jnp.ones((s, s), bool))
        logits = jnp.where(causal, logits, jnp.float32(-1e+30))
        w = jax.nn.softmax(logits, axis=-1)
        out = jnp.einsum('bhgqk,bkhd->bqhgd', w, v).reshape(b, s, NQ * D)
        return out @ Wo + bo

    def _L0_ffn_ref(hidden_states, gate_w, sh_gate, sh_up, sh_down, rt_gate, rt_up, rt_down):
        import jax, jax.numpy as jnp
        import numpy as np
        H = 512
        I = 1024
        E = 8
        B, S = (2, 512)

        def _swiglu(x, wg, wu, wd):
            return jax.nn.silu(x @ wg) * (x @ wu) @ wd
        b, s, h = hidden_states.shape
        x = hidden_states.reshape(-1, h)
        logits = x @ gate_w
        top_val = jnp.max(logits, axis=-1, keepdims=True)
        top_id = jnp.argmax(logits, axis=-1)
        score = jax.nn.sigmoid(top_val)
        xs = x * score
        g = jnp.einsum('th,ehi->eti', xs, rt_gate)
        u = jnp.einsum('th,ehi->eti', xs, rt_up)
        act = jax.nn.silu(g) * u
        y = jnp.einsum('eti,eih->eth', act, rt_down)
        onehot = jax.nn.one_hot(top_id, E, dtype=x.dtype)
        routed = jnp.einsum('eth,te->th', y, onehot)
        shared = _swiglu(x, sh_gate, sh_up, sh_down)
        return (shared + routed).reshape(b, s, h)
    x = x + _L0_xattn_ref(_layernorm(x, axis=-1), ctx_1024, L0_xattn_w_sim, L0_xattn_b_sim, L0_xattn_W_qv, L0_xattn_b_qv)
    x = x + _L0_attn_ref(_layernorm(x, axis=-1), L0_attn_Wq, L0_attn_bq, L0_attn_Wk, L0_attn_bk, L0_attn_Wv, L0_attn_bv, L0_attn_Wo, L0_attn_bo)
    x = x + _L0_ffn_ref(_layernorm(x, axis=-1), L0_ffn_gate_w, L0_ffn_sh_gate, L0_ffn_sh_up, L0_ffn_sh_down, L0_ffn_rt_gate, L0_ffn_rt_up, L0_ffn_rt_down)
    return x

_drawn_inputs = setup_inputs


def setup_inputs(seed=0):
    import zlib

    import numpy as np

    out = dict(_drawn_inputs(seed))
    spreads = {'L0_attn_bq': (0.0, 0.8),
     'L0_attn_bk': (0.0, 0.8),
     'L0_attn_bv': (0.0, 0.1),
     'L0_attn_bo': (0.0, 0.1)}
    factors = {'L0_attn_Wk': 3.537}
    for name, (base, spread) in spreads.items():
        noise = np.random.default_rng([zlib.crc32(name.encode()), seed]).standard_normal(out[name].shape)
        drawn = base * np.exp(spread * noise) if base else spread * noise
        out[name] = jnp.asarray(drawn.astype(out[name].dtype))
    for name, factor in factors.items():
        out[name] = (out[name] * factor).astype(out[name].dtype)
    return out
```

```python
from contextlib import ExitStack

import numpy as np

import concourse.bass as bass
from concourse import mybir

F32 = mybir.dt.float32
F32R = mybir.dt.float32r
I32 = mybir.dt.int32
ALU = mybir.AluOpType
ACT = mybir.ActivationFunctionType
AX = mybir.AxisListType.X

P = 128
N = 512
D = 512
NT = N // P
DC = D // P
CTX = 8192
CB = 512
JT = CB // P
BLOCKS = CTX // CB
UNITS = BLOCKS * NT
STEP = 2 * NT
HEADS, KV, HD = 16, 4, 64
QT = HEADS * HD // P
INNER = 1024
IC = INNER // P
E = 8
EPS = 1e-5
FAR = 3e38
HIDDEN = -1e30
ATT_SCALE = HD ** -0.5

C_IDENT, C_ROT, C_MASK, C_TRI, C_ONES, C_IOTA = (k * P for k in range(6))
C_COS = 6 * P
C_SIN = C_COS + N
C_PREF = C_SIN + N
C_EPS = C_PREF + E
C_ZERO = C_EPS + 1
C_ALL = C_ZERO + 1

R_W1, R_W2, R_W3, R_BQ, R_BK = 0, DC, 2 * DC, 3 * DC, 3 * DC + QT
ROWS = R_BK + 2


def constants():
    c = np.zeros((P, C_ALL), np.float32)
    i = np.arange(P)
    c[i, C_IDENT + i] = 1.0
    first = i % HD < HD // 2
    c[i[first] + HD // 2, C_ROT + i[first]] = -1.0
    c[i[~first] - HD // 2, C_ROT + i[~first]] = 1.0
    c[:, C_MASK:C_MASK + P] = np.where(i[None, :] > i[:, None], HIDDEN, 0.0)
    c[:, C_TRI:C_TRI + P] = i[:, None] < i[None, :]
    c[:, C_ONES:C_ONES + P] = 1.0
    c[:, C_IOTA:C_IOTA + P] = i[None, :]
    freq = np.float32(1.0) / np.float32(10000.0) ** (np.arange(0, HD, 2, dtype=np.float32) / np.float32(HD))
    angle = np.arange(N, dtype=np.float32)[None, :] * freq[i % (HD // 2)][:, None]
    c[:, C_COS:C_COS + N] = np.cos(angle)
    c[:, C_SIN:C_SIN + N] = np.sin(angle)
    c[:, C_PREF:C_PREF + E] = E - np.arange(E)[None, :]
    c[:, C_EPS] = EPS
    return c


class Memory:

    def __init__(self, nc, ctx):
        base = (nc.sbuf_base + 31) // 32 * 32
        self.nc = nc

        def at(name, kb, shape, dt=F32):
            return nc.alloc_sbuf_tensor_at(name, shape, dt, offset=base + int(kb * 1024))

        self.ps = ctx.enter_context(nc.psum_tensor("banks", [P, 8, 512], F32))
        self.x = at("x_res", 0, [P, NT, D])
        self.h = at("h_norm", 8, [P, NT, D])
        self.hT = at("hT", 16, [P, DC, N])
        self.c = at("consts", 40, [P, C_ALL])
        self.small_at = 47.5 * 1024

        def small(name, shape, dt=F32):
            size = int(np.prod(shape[1:])) * 4
            t = nc.alloc_sbuf_tensor_at(name, shape, dt, offset=base + int(self.small_at))
            self.small_at += (size + 31) // 32 * 32
            assert self.small_at <= 50 * 1024
            return t

        self.wT = small("wT", [P, ROWS])
        self.stats = small("ln_stats", [P, NT, 6])
        self.mv = small("ln_mean_var", [P, NT, 2])
        self.sd = small("ln_sd", [P, NT])
        self.rstd = small("ln_rstd", [P, NT])
        self.e1 = small("enc_w1", [P, NT])
        self.negm = small("neg_max", [P, 2, NT])
        self.mx = small("block_max", [P, 2 * NT])
        self.alpha = small("alpha", [P, 2 * NT])
        self.rowsum = small("row_sum", [P, 2 * NT])
        self.den = small("denominator", [P, NT])
        self.rden = small("inv_denominator", [P, NT])
        self.bsim = small("b_sim", [P, 1])
        self.mcol = small("token_max", [P, NT])
        self.r1 = small("row_scalars", [1, 4])
        self.batt = small("batt_col", [P, NT])
        self.hc = small("hc_bar", [P, DC])
        self.amx = small("att_max", [P, 4, 2])
        self.anb = small("att_bias", [P, 4, 2])
        self.ars = small("att_sum", [P, 4, 2])
        self.arl = small("att_inv", [P, 4, 2])
        self.gw = small("gate_w", [P, DC, E])
        self.lg = small("logits", [P, NT, E])
        self.top = small("top", [P, NT])
        self.eq = small("is_top", [P, NT, E])
        self.first = small("first_top", [P, NT])
        self.onehot = small("onehot", [P, NT, E])
        self.score = small("score", [P, NT])
        self.tmp8 = small("rank_of_own", [P, NT, E])
        self.rank = small("rank", [P, NT])
        self.cnt = small("counts", [P, E])
        self.over = small("overflow", [P, 1])
        self.over_i = small("overflow_int", [P, 1], I32)
        self.bqv = at("b_qv_all", 198, [P, D])
        self.bo = at("b_o_all", 200, [P, D])
        self.bv = at("b_v_all", 202, [P, KV * HD])
        self.rows = at("rows", 203, [ROWS, P])
        self.mrow = at("token_max_row", 204, [1, N])
        self.gh = at("g_hi", 24, [P, DC, N], F32R)
        self.gl = at("g_lo", 32, [P, DC, N], F32R)
        self.raw = [at(f"ctx_raw{s}", 50 + 8 * s, [P, JT, D]) for s in range(2)]
        self.nh = [at(f"ctx_hi{s}", 66 + 8 * s, [P, JT, D], F32R) for s in range(2)]
        self.nl = [at(f"ctx_lo{s}", 82 + 8 * s, [P, JT, D], F32R) for s in range(2)]
        self.th = [at(f"ctxT_hi{s}", 98 + 8 * s, [P, DC, CB], F32R) for s in range(2)]
        self.tl = [at(f"ctxT_lo{s}", 114 + 8 * s, [P, DC, CB], F32R) for s in range(2)]
        self.p = [at(f"probs{s}", 130 + 2 * s, [P, CB]) for s in range(2)]
        self.pth = [at(f"probsT_hi{s}", 134 + 2 * s, [P, CB], F32R) for s in range(2)]
        self.ptl = [at(f"probsT_lo{s}", 138 + 2 * s, [P, CB], F32R) for s in range(2)]
        self.o = at("attended", 142, [P, NT, D])
        self.g = at("g_whole", 142, [P, DC, N])
        self.wqv = at("w_qv", 150, [P, 4, DC, D])
        self.hqT = at("hqT", 66, [P, DC, N])
        self.ehT = at("enc_hqT", 74, [P, DC, N])
        self.wq = at("w_q", 182, [P, DC, HEADS * HD])
        self.wk = at("w_k", 98, [P, DC, KV * HD])
        self.wv = at("w_v", 102, [P, DC, KV * HD])
        self.wo = at("w_o", 106, [P, QT, D])
        self.k2h = at("k_hi_twice", 24, [P, KV, N], F32R)
        self.k2l = at("k_lo_twice", 32, [P, KV, N], F32R)
        self.q2 = at("q_hi_lo", 50, [P, HEADS, N], F32R)
        self.v = at("values", 82, [P, NT, (KV + 1) * HD])
        self.ap = [at(f"att_probs{s}", 88 + 4 * s, [P, 2, N]) for s in range(2)]
        self.apt = [at(f"att_probsT{s}", 122 + 4 * s, [P, 2, N]) for s in range(2)]
        self.qb = [at(f"q_biased{s}", 130 + 2 * s, [P, N]) for s in range(2)]
        self.qc = [at(f"q_cos{s}", 134 + 2 * s, [P, N]) for s in range(2)]
        self.qs = [at(f"q_sin{s}", 138 + 2 * s, [P, N]) for s in range(2)]
        self.ao = at("att_out", 130, [P, NT, HEADS * HD])
        self.aoT = [at(f"att_outT{s}", 88 + 4 * s, [P, QT, P]) for s in range(2)]
        self.sg = at("sh_gate", 150, [P, DC, INNER])
        self.su = at("sh_up", 166, [P, DC, INNER])
        self.sdn = at("sh_down", 182, [P, IC, D])
        self.sil = [at(f"silu{s}", 146 + 2 * s, [P, 512]) for s in range(2)]
        self.sact = at("sh_act", 130, [P, IC, N])
        self.wg = [at(f"rt_gate{s}", 50 + 32 * s, [P, DC, INNER]) for s in range(2)]
        self.wu = [at(f"rt_up{s}", 66 + 32 * s, [P, DC, INNER]) for s in range(2)]
        self.wd = [at("rt_down0", 114, [P, IC, D]), at("rt_down1", 8, [P, IC, D])]
        self.xsh = at("xs_hi", 24, [P, NT, D], F32R)
        self.xsl = at("xs_lo", 32, [P, NT, D], F32R)
        self.sel = at("select", 198, [P, NT, 4, P], F32R)
        self.selT = at("selectT", 130, [P, E, N], F32R)
        self.xg = at("gatheredT", 150, [P, DC, E * P])
        self.yh = at("y_hi", 166, [P, 4, D], F32R)
        self.yl = at("y_lo", 174, [P, 4, D], F32R)
        self.act = [at(f"act{s}", 182 + 4 * s, [P, INNER]) for s in range(2)]
        self.actT = [at(f"actT{s}", 190 + 4 * s, [P, INNER]) for s in range(2)]
        self.lgt = at("logits_turned", 146, [E, N])
        self.osel = at("over_select", 198, [P, NT, P], F32R)
        self.oselT = at("over_selectT", 130, [P, N], F32R)
        self.oxg = at("over_gatheredT", 150, [P, DC, P])

    def const(self, col, n=1, rows=P):
        return self.c[0:rows, col:col + n]


class Norm:

    def __init__(self, m, sem, tag):
        self.m = m
        self.stats = sem(f"{tag}_stats")
        self.var = sem(f"{tag}_var")
        self.sd = sem(f"{tag}_sd")
        self.rstd = sem(f"{tag}_rstd")
        self.h = sem(f"{tag}_h")
        self.turned = sem(f"{tag}_turned")
        self.hT = sem(f"{tag}_hT")

    def vector_stats(self, dve, t):
        dve.bn_stats(self.m.stats[:, t, :], self.m.x[:, t, :]).then_inc(self.stats, 1)

    def vector(self, dve):
        m = self.m
        for t in range(NT):
            dve.wait_ge(self.stats, t + 1)
            dve.bn_aggr(m.mv[:, t, :], m.stats[:, t, :]).then_inc(self.var, 1)
        dve.wait_ge(self.sd, 1)
        dve.reciprocal(m.rstd[:, :], m.sd[:, :]).then_inc(self.rstd, 1)
        dve.wait_ge(self.rstd, 1)
        for t in range(NT):
            dve.tensor_scalar(m.h[:, t, :], m.x[:, t, :], m.mv[:, t, 0:1], m.rstd[:, t:t + 1],
                              ALU.subtract, ALU.mult).then_inc(self.h, 1)

    def scalar(self, act):
        m = self.m
        act.wait_ge(self.var, NT)
        act.activation(m.sd[:, :], m.mv[:, :, 1], ACT.Sqrt, bias=m.const(C_EPS)).then_inc(self.sd, 1)
        for t in range(NT):
            act.wait_ge(self.turned, t + 1)
            act.activation(m.hT[:, :, t * P:(t + 1) * P], m.ps[:, t, :].rearrange("p (c n) -> p c n", c=DC),
                           ACT.Copy).then_inc(self.hT, 1)

    def tensor(self, pe):
        m = self.m
        for t in range(NT):
            pe.wait_ge(self.h, t + 1)
            for c in range(DC):
                last = pe.transpose(m.ps[:, t, c * P:(c + 1) * P], m.h[:, t, c * P:(c + 1) * P],
                                    m.const(C_IDENT, P))
            last.then_inc(self.turned, 1)


def need(eng, sem, base, n):
    if not isinstance(base, int) or base + n > 0:
        eng.wait_ge(sem, base + n)


def setup(nc, m, d, sem, s):
    ln = Norm(m, sem, "ln0")
    s_consts, s_x, s_rows, s_bias = sem("consts_loaded"), sem("x_loaded"), sem("rows_loaded"), sem("bias_loaded")
    rows_turned, wT_ready, g_whole, g_hi, e1_made = (sem("rows_turned"), sem("wT_ready"), sem("g_whole_made"),
                                                     sem("g_hi_made"), sem("e1_made"))
    g_lo = sem("g_lo_made")
    s.ctx_loaded = [sem(f"ctx_loaded{k}") for k in range(2)]
    s.wqv_loaded, s.wq_loaded = sem("wqv_loaded"), sem("wq_loaded")
    s.bias_loaded = s_bias
    s.ctx = d["ctx"].rearrange("o (b p t) d -> (o b) p t d", p=P, t=JT)

    with nc.Block() as block:
        @block.sync
        def _(sp):
            sp.dma_start(m.x[:, :, :], d["x"].rearrange("o (t p) d -> p (o t) d", p=P)).then_inc(s_x, 16)
            sp.dma_start(m.c[:, :], d["consts"]).then_inc(s_consts, 16)
            sp.dma_start(m.rows[0:3 * DC, :], d["w_sim"].rearrange("(a p) -> a p", p=P)).then_inc(s_rows, 16)
            sp.dma_start(m.rows[R_BQ:R_BK, :], d["bq"].rearrange("(a p) -> a p", p=P)).then_inc(s_rows, 16)
            sp.dma_start(m.rows[R_BK:ROWS, :], d["bk"].rearrange("(a p) -> a p", p=P)).then_inc(s_rows, 16)
            for k in range(2):
                sp.dma_start(m.raw[k][:, :, :], s.ctx[k]).then_inc(s.ctx_loaded[k], 16)
            sp.dma_start(m.bqv[:, :], d["b_qv"].partition_broadcast(P)).then_inc(s_bias, 16)
            sp.dma_start(m.bo[:, :], d["bo"].partition_broadcast(P)).then_inc(s_bias, 16)
            sp.dma_start(m.bv[:, :], d["bv"].partition_broadcast(P)).then_inc(s_bias, 16)
            sp.dma_start(m.bsim[:, :], d["b_sim"].partition_broadcast(P)).then_inc(s_bias, 16)
            sp.dma_start(m.gw[:, :, :], d["gate_w"].rearrange("(c p) e -> p c e", p=P)).then_inc(s_bias, 16)
            sp.dma_start(m.wqv[:, :, :, :], d["W_qv"].rearrange("(a c p) n -> p a c n", p=P, a=4)).then_inc(s.wqv_loaded, 16)
            sp.dma_start(m.wq[:, :, :], d["Wq"].rearrange("(c p) n -> p c n", p=P)).then_inc(s.wq_loaded, 16)

        @block.tensor
        def _(pe):
            pe.wait_ge(s_consts, 16)
            pe.wait_ge(s_rows, 48)
            pe.transpose(m.ps[:, 7, 0:ROWS], m.rows[:, :], m.const(C_IDENT, ROWS, ROWS)).then_inc(rows_turned, 1)
            ln.tensor(pe)
            pe.wait_ge(ln.hT, NT)
            pe.wait_ge(wT_ready, 1)
            for t in range(NT):
                for c in range(DC):
                    last = pe.matmul(m.ps[:, 6, t:t + 1], m.hT[:, c, t * P:(t + 1) * P], m.wT[:, R_W1 + c:R_W1 + c + 1],
                                     start=c == 0, stop=c == DC - 1)
            last.then_inc(e1_made, 1)

        @block.scalar
        def _(act):
            act.wait_ge(rows_turned, 1)
            act.activation(m.wT[:, :], m.ps[:, 7, 0:ROWS], ACT.Copy).then_inc(wT_ready, 1)
            act.wait_ge(s_consts, 16)
            ln.scalar(act)

        @block.vector
        def _(dve):
            dve.memset(m.den[:, :], 0.0)
            dve.memset(m.negm[:, 1, :], FAR)
            dve.wait_ge(s_x, 16)
            for t in range(NT):
                ln.vector_stats(dve, t)
            ln.vector(dve)
            dve.wait_ge(wT_ready, 1)
            dve.wait_ge(ln.hT, NT)
            for c in range(DC):
                dve.tensor_scalar(m.g[:, c, :], m.hT[:, c, :], m.wT[:, R_W3 + c:R_W3 + c + 1],
                                  m.wT[:, R_W2 + c:R_W2 + c + 1], ALU.mult, ALU.add).then_inc(g_whole, 1)
            for c in range(DC):
                dve.wait_ge(g_whole, c + 1)
                dve.tensor_copy(m.gh[:, c, :], m.g[:, c, :]).then_inc(g_hi, 1)
            for c in range(DC):
                dve.wait_ge(g_hi, c + 1)
                dve.tensor_tensor(m.gl[:, c, :], m.g[:, c, :], m.gh[:, c, :].bitcast(F32), ALU.subtract).then_inc(g_lo, 1)
            dve.wait_ge(e1_made, 1)
            dve.tensor_copy(m.e1[:, :], m.ps[:, 6, 0:NT])
            dve.wait_ge(g_lo, DC)
            dve.memset(m.o[:, :, :], 0.0)


def cross_attention(nc, m, sem, s):
    ct_turned, ct_hi, ct_lo = sem("ctxT_turned"), sem("ctxT_hi_made"), sem("ctxT_lo_made")
    n_hi, n_lo = sem("ctx_hi_made"), sem("ctx_lo_made")
    scored, maxed, negm_made = sem("scored"), sem("block_maxed"), sem("negm_made")
    alpha_made, exp_made = sem("alpha_made"), sem("exp_made")
    pt_turned, pt_hi, pt_lo = sem("probsT_turned"), sem("probsT_hi_made"), sem("probsT_lo_made")
    attended, den_made, merged = sem("attended_made"), sem("den_made"), sem("merged")
    S_BANK, PT_BANK, CT_BANK, O_BANK = 0, 2, 4, 6
    AHEAD_S, AHEAD_CT, AHEAD_N = 2, 6, 4
    ps = m.ps
    ident = m.const(C_IDENT, P)
    loops = UNITS // STEP

    def loaded(eng, base, n):
        slot, use = n // JT % 2, n // JT // 2 + 1
        eng.wait_ge(s.ctx_loaded[slot], base * 2 + 16 * use)

    def turns(eng, unit, prologue):
        prologue()
        for k in range(STEP):
            unit(0, k, False)
        with eng.Fori(STEP, UNITS - STEP, STEP) as base:
            for k in range(STEP):
                unit(base, k, False)
        for k in range(STEP):
            unit(UNITS - STEP, k, True)

    with nc.Block() as block:
        @block.sync
        def _(sp):
            def load(base, block_index, slot, k):
                need(sp, ct_turned, base, JT * (k + 1))
                need(sp, n_lo, base, JT * (k + 1))
                sp.dma_start(m.raw[slot][:, :, :], s.ctx[block_index]).then_inc(s.ctx_loaded[slot], 16)

            for k in range(2):
                load(0, 2 + k, k, k)
            with sp.Fori(1, loops - 1) as turn:
                for k in range(2):
                    load(turn * STEP, turn * 2 + 2 + k, k, k)

        @block.gpsimd
        def _(pool):
            zeros = m.const(C_ZERO).to_broadcast([P, D])

            def split(base, n):
                slot = n // JT % 2
                loaded(pool, base, n)
                need(pool, attended, base, n // JT * JT - JT)
                raw, hi, lo = m.raw[slot][:, n % JT, :], m.nh[slot][:, n % JT, :], m.nl[slot][:, n % JT, :]
                pool.tensor_tensor(hi, raw, zeros, ALU.add).then_inc(n_hi, 1)
                need(pool, n_hi, base, n + 1)
                pool.tensor_tensor(lo, raw, hi.bitcast(F32), ALU.subtract).then_inc(n_lo, 1)

            def unit(base, k, last):
                if not last or k + AHEAD_N < STEP:
                    split(base, k + AHEAD_N)

            def prologue():
                for n in range(AHEAD_N):
                    split(0, n)

            turns(pool, unit, prologue)

        @block.tensor
        def _(pe):
            def turn_ctx(base, n):
                slot, bank = n // JT % 2, CT_BANK + n % 2
                loaded(pe, base, n)
                need(pe, ct_lo, base, n - 1)
                for c in range(DC):
                    last = pe.transpose(ps[:, bank, c * P:(c + 1) * P], m.raw[slot][:, n % JT, c * P:(c + 1) * P], ident)
                last.then_inc(ct_turned, 1)

            def score(base, v):
                slot, i, bank = v // NT % 2, v % NT, S_BANK + v % 2
                need(pe, ct_lo, base, v // NT * JT + JT)
                need(pe, exp_made, base, v - 1)
                tok = slice(i * P, (i + 1) * P)
                for c in range(DC):
                    pe.matmul(ps[:, bank, :], m.gh[:, c, tok], m.th[slot][:, c, :], start=c == 0, stop=False)
                    pe.matmul(ps[:, bank, :], m.gh[:, c, tok], m.tl[slot][:, c, :], start=False, stop=False)
                    last = pe.matmul(ps[:, bank, :], m.gl[:, c, tok], m.th[slot][:, c, :], start=False, stop=c == DC - 1)
                last.then_inc(scored, 1)

            def turn_probs(base, u):
                need(pe, exp_made, base, u + 1)
                need(pe, pt_lo, base, u - 1)
                for j in range(JT):
                    last = pe.transpose(ps[:, PT_BANK + u % 2, j * P:(j + 1) * P], m.p[u % 2][:, j * P:(j + 1) * P], ident)
                last.then_inc(pt_turned, 1)

            def attend(base, u):
                slot, bank, b = u // NT % 2, O_BANK + u % 2, u % 2
                need(pe, pt_lo, base, u + 1)
                need(pe, n_lo, base, u // NT * JT + JT)
                need(pe, merged, base, u - 1)
                for j in range(JT):
                    col = slice(j * P, (j + 1) * P)
                    pe.matmul(ps[:, bank, :], m.pth[b][:, col], m.nh[slot][:, j, :], start=j == 0, stop=False)
                    pe.matmul(ps[:, bank, :], m.pth[b][:, col], m.nl[slot][:, j, :], start=False, stop=False)
                    last = pe.matmul(ps[:, bank, :], m.ptl[b][:, col], m.nh[slot][:, j, :], start=False, stop=j == JT - 1)
                last.then_inc(attended, 1)

            def unit(base, k, last):
                turn_probs(base, k)
                if not last or k + AHEAD_CT < STEP:
                    turn_ctx(base, k + AHEAD_CT)
                if not last or k + AHEAD_S < STEP:
                    score(base, k + AHEAD_S)
                attend(base, k)

            def prologue():
                for n in range(AHEAD_CT):
                    turn_ctx(0, n)
                    if n == JT:
                        score(0, 0)
                score(0, 1)

            turns(pe, unit, prologue)

        @block.scalar
        def _(act):
            def ctx_hi(base, n):
                need(act, ct_turned, base, n + 1)
                need(act, scored, base, n // JT * NT - NT)
                act.activation(m.th[n // JT % 2][:, :, n % JT * P:(n % JT + 1) * P],
                               ps[:, CT_BANK + n % 2, :].rearrange("p (c n) -> p c n", c=DC),
                               ACT.Copy).then_inc(ct_hi, 1)

            def exps(base, v):
                i, new, b = v % NT, v // NT % 2, v % STEP
                need(act, negm_made, base, v + 1)
                act.activation(m.alpha[:, b:b + 1], m.negm[:, 1 - new, i:i + 1], ACT.Exp, scale=-1.0,
                               bias=m.negm[:, new, i:i + 1]).then_inc(alpha_made, 1)
                need(act, pt_turned, base, v - 1)
                act.activation(m.p[v % 2][:, :], ps[:, S_BANK + v % 2, :], ACT.Exp, bias=m.negm[:, new, i:i + 1],
                               accum_out=m.rowsum[:, b:b + 1]).then_inc(exp_made, 1)

            def probs_hi(base, u):
                need(act, pt_turned, base, u + 1)
                need(act, attended, base, u - 1)
                act.activation(m.pth[u % 2][:, :], ps[:, PT_BANK + u % 2, :], ACT.Copy).then_inc(pt_hi, 1)

            def unit(base, k, last):
                probs_hi(base, k)
                if not last or k + AHEAD_CT < STEP:
                    ctx_hi(base, k + AHEAD_CT)
                if not last or k + AHEAD_S < STEP:
                    exps(base, k + AHEAD_S)

            def prologue():
                for n in range(AHEAD_CT):
                    ctx_hi(0, n)
                exps(0, 0)
                exps(0, 1)

            turns(act, unit, prologue)

        @block.vector
        def _(dve):
            def ctx_lo(base, n):
                slot, col = n // JT % 2, slice(n % JT * P, (n % JT + 1) * P)
                need(dve, ct_hi, base, n + 1)
                dve.tensor_tensor(m.tl[slot][:, :, col], ps[:, CT_BANK + n % 2, :].rearrange("p (c n) -> p c n", c=DC),
                                  m.th[slot][:, :, col].bitcast(F32), ALU.subtract).then_inc(ct_lo, 1)

            def maxes(base, v):
                i, new, b = v % NT, v // NT % 2, v % STEP
                need(dve, scored, base, v + 1)
                dve.tensor_reduce(m.mx[:, b:b + 1], ps[:, S_BANK + v % 2, :], AX, ALU.max).then_inc(maxed, 1)
                need(dve, maxed, base, v + 1)
                dve.scalar_tensor_tensor(m.negm[:, new, i:i + 1], m.mx[:, b:b + 1], -1.0, m.negm[:, 1 - new, i:i + 1],
                                         ALU.mult, ALU.min).then_inc(negm_made, 1)

            def probs_lo(base, u):
                need(dve, pt_hi, base, u + 1)
                dve.tensor_tensor(m.ptl[u % 2][:, :], ps[:, PT_BANK + u % 2, :], m.pth[u % 2][:, :].bitcast(F32),
                                  ALU.subtract).then_inc(pt_lo, 1)

            def merge(base, u):
                i, b = u % NT, u % STEP
                need(dve, attended, base, u + 1)
                need(dve, exp_made, base, u + 1)
                need(dve, merged, base, u - NT + 1)
                dve.scalar_tensor_tensor(m.o[:, i, :], m.o[:, i, :], m.alpha[:, b:b + 1], ps[:, O_BANK + u % 2, :],
                                         ALU.mult, ALU.add).then_inc(merged, 1)
                need(dve, den_made, base, u - NT + 1)
                dve.scalar_tensor_tensor(m.den[:, i:i + 1], m.den[:, i:i + 1], m.alpha[:, b:b + 1],
                                         m.rowsum[:, b:b + 1], ALU.mult, ALU.add).then_inc(den_made, 1)

            def unit(base, k, last):
                probs_lo(base, k)
                if not isinstance(base, int) or base + k > 0:
                    merge(base, k - 1) if k else merge(base, -1)
                if not last or k + AHEAD_CT < STEP:
                    ctx_lo(base, k + AHEAD_CT)
                if not last or k + AHEAD_S < STEP:
                    maxes(base, k + AHEAD_S)

            def prologue():
                for n in range(AHEAD_CT):
                    ctx_lo(0, n)
                    if n == JT:
                        maxes(0, 0)
                maxes(0, 1)

            turns(dve, unit, prologue)
            merge(UNITS - STEP, STEP - 1)


def cross_output(nc, m, d, sem, s):
    ln = s.ln1 = Norm(m, sem, "ln1")
    mcol0, mcol, mrow, rmax, rexp, rinv, brow, bcol_ps, bcol, hc_ps, hc = (sem(x) for x in (
        "mcol_sum", "mcol_made", "mrow_turned", "row_max", "row_exp", "row_inv", "batt_row", "batt_turned",
        "batt_col_made", "hc_summed", "hc_made"))
    rden, hq, hq_turned, hqT, ehT, w14, fed, xb, x1 = (sem(x) for x in (
        "rden_made", "hq_made", "hq_turned", "hqT_made", "ehT_made", "w14_made", "fed", "x_biased", "x1_made"))
    s.wkv_loaded, s.wo_loaded = sem("wkv_loaded"), sem("wo_loaded")
    ROW_BANK = 4
    ps = m.ps
    out_bank = [5, 6, 7, 4]

    with nc.Block() as block:
        @block.sync
        def _(sp):
            sp.dma_start(m.wk[:, :, :], d["Wk"].rearrange("(c p) n -> p c n", p=P)).then_inc(s.wkv_loaded, 16)
            sp.dma_start(m.wv[:, :, :], d["Wv"].rearrange("(c p) n -> p c n", p=P)).then_inc(s.wkv_loaded, 16)
            sp.dma_start(m.wo[:, :, :], d["Wo"].rearrange("(c p) n -> p c n", p=P)).then_inc(s.wo_loaded, 16)

        @block.tensor
        def _(pe):
            pe.wait_ge(mcol, 1)
            for t in range(NT):
                last = pe.matmul(ps[0:1, ROW_BANK, t * P:(t + 1) * P], m.mcol[:, t:t + 1], m.const(C_IDENT, P),
                                 start=True, stop=True)
            last.then_inc(mrow, 1)
            for t in range(NT):
                pe.wait_ge(hq, t + 1)
                for c in range(DC):
                    last = pe.transpose(ps[:, t, c * P:(c + 1) * P], m.o[:, t, c * P:(c + 1) * P], m.const(C_IDENT, P))
                last.then_inc(hq_turned, 1)

            def feed(t, part, lhsT, start, stop):
                for c in range(DC):
                    last = pe.matmul(ps[:, out_bank[t], :], lhsT[:, c, t * P:(t + 1) * P], m.wqv[:, part, c, :],
                                     start=start and c == 0, stop=stop and c == DC - 1)
                return last

            pe.wait_ge(s.wqv_loaded, 16)
            pe.wait_ge(hqT, NT)
            for t in range(3):
                feed(t, 1, m.hqT, True, False)
            pe.wait_ge(ehT, DC)
            for t in range(3):
                feed(t, 2, m.ehT, False, False)
            pe.wait_ge(brow, 1)
            for t in range(NT):
                last = pe.matmul(ps[:, ROW_BANK, t:t + 1], m.mrow[0:1, t * P:(t + 1) * P], m.const(C_ONES, 1, 1),
                                 start=True, stop=True)
            last.then_inc(bcol_ps, 1)
            pe.wait_ge(bcol, 1)
            for c in range(DC):
                for t in range(NT):
                    last = pe.matmul(ps[:, ROW_BANK, 8 + c:9 + c], m.h[:, t, c * P:(c + 1) * P], m.batt[:, t:t + 1],
                                     start=t == 0, stop=t == NT - 1)
            last.then_inc(hc_ps, 1)
            pe.wait_ge(w14, DC)
            for t in range(3):
                feed(t, 0, m.hT, False, True).then_inc(fed, 1)
            feed(3, 1, m.hqT, True, False)
            feed(3, 2, m.ehT, False, False)
            feed(3, 0, m.hT, False, True).then_inc(fed, 1)
            ln.tensor(pe)

        @block.scalar
        def _(act):
            for t in range(NT):
                act.wait_ge(hq_turned, t + 1)
                act.activation(m.hqT[:, :, t * P:(t + 1) * P], ps[:, t, :].rearrange("p (c n) -> p c n", c=DC),
                               ACT.Copy).then_inc(hqT, 1)
            act.wait_ge(rmax, 2)
            act.activation(m.mrow[:, :], ps[0:1, ROW_BANK, :], ACT.Exp, bias=m.r1[:, 1:2],
                           accum_out=m.r1[:, 2:3]).then_inc(rexp, 1)
            ln.scalar(act)

        @block.vector
        def _(dve):
            dve.scalar_tensor_tensor(m.mcol[:, :], m.negm[:, 1, :], -1.0, m.e1[:, :], ALU.mult, ALU.add).then_inc(mcol0, 1)
            dve.wait_ge(mcol0, 1)
            dve.wait_ge(s.bias_loaded, 80)
            dve.tensor_scalar(m.mcol[:, :], m.mcol[:, :], m.bsim[:, 0:1], None, ALU.add).then_inc(mcol, 1)
            dve.reciprocal(m.rden[:, :], m.den[:, :]).then_inc(rden, 1)
            dve.wait_ge(rden, 1)
            for t in range(NT):
                dve.tensor_scalar(m.o[:, t, :], m.o[:, t, :], m.rden[:, t:t + 1], None, ALU.mult).then_inc(hq, 1)
            dve.wait_ge(mrow, 1)
            dve.tensor_reduce(m.r1[:, 0:1], ps[0:1, ROW_BANK, :], AX, ALU.max).then_inc(rmax, 1)
            dve.wait_ge(rmax, 1)
            dve.tensor_scalar(m.r1[:, 1:2], m.r1[:, 0:1], -1.0, None, ALU.mult).then_inc(rmax, 1)
            for t in range(NT):
                dve.tensor_tensor(m.x[:, t, :], m.x[:, t, :], m.bqv[:, :], ALU.add).then_inc(xb, 1)
            dve.wait_ge(hqT, NT)
            for c in range(DC):
                dve.tensor_tensor(m.ehT[:, c, :], m.hT[:, c, :], m.hqT[:, c, :], ALU.mult).then_inc(ehT, 1)
            dve.wait_ge(rexp, 1)
            dve.reciprocal(m.r1[:, 3:4], m.r1[:, 2:3]).then_inc(rinv, 1)
            dve.wait_ge(rinv, 1)
            dve.tensor_scalar(m.mrow[:, :], m.mrow[:, :], m.r1[:, 3:4], None, ALU.mult).then_inc(brow, 1)
            dve.wait_ge(bcol_ps, 1)
            dve.tensor_copy(m.batt[:, :], ps[:, ROW_BANK, 0:NT]).then_inc(bcol, 1)
            dve.wait_ge(hc_ps, 1)
            dve.tensor_copy(m.hc[:, :], ps[:, ROW_BANK, 8:8 + DC]).then_inc(hc, 1)
            dve.wait_ge(hc, 1)
            dve.wait_ge(s.wqv_loaded, 16)
            for c in range(DC):
                dve.scalar_tensor_tensor(m.wqv[:, 0, c, :], m.wqv[:, 3, c, :], m.hc[:, c:c + 1], m.wqv[:, 0, c, :],
                                         ALU.mult, ALU.add).then_inc(w14, 1)
            for t in range(NT):
                dve.wait_ge(fed, t + 1)
                dve.wait_ge(xb, t + 1)
                dve.tensor_tensor(m.x[:, t, :], m.x[:, t, :], ps[:, out_bank[t], :], ALU.add).then_inc(x1, 1)
                dve.wait_ge(x1, t + 1)
                ln.vector_stats(dve, t)
            ln.vector(dve)


def self_attention(nc, m, d, sem, s):
    ln = Norm(m, sem, "ln2")
    projected, biased, rotated, cosed, sined, summed, q_hi, k_hi, split_done = (sem(x) for x in (
        "projected", "q_biased_made", "q_rotated", "q_cosed", "q_sined", "rotary_made", "q_hi_made", "k_hi_made",
        "qk_lo_made"))
    v_ps, v_made, v_pad = sem("v_projected"), sem("v_made"), sem("v_padded")
    scored, masked, maxed, bias_made, exped = (sem(x) for x in (
        "att_scored", "att_masked", "att_maxed", "att_bias_made", "att_exp_made"))
    turned, pt0, pt1, valued, inv, out_made = (sem(x) for x in (
        "att_turned", "att_pt0_made", "att_pt1_made", "att_valued", "att_inv_made", "att_out_made"))
    o_turned, oT0, oT1, wo_done, xb, x2 = (sem(x) for x in (
        "out_turned", "outT0_made", "outT1_made", "wo_done", "x1_biased", "x2_made"))
    s.sh_loaded, s.shd_loaded = sem("sh_loaded"), sem("sh_down_loaded")
    ps = m.ps
    ident = m.const(C_IDENT, P)
    PAIRS = HEADS // 2
    AU = NT * PAIRS
    tiles = [("k", c) for c in range(KV * HD // P)] + [("q", c) for c in range(QT)]

    with nc.Block() as block:
        @block.sync
        def _(sp):
            sp.dma_start(m.sg[:, :, :], d["sh_gate"].rearrange("(c p) n -> p c n", p=P)).then_inc(s.sh_loaded, 16)
            sp.dma_start(m.su[:, :, :], d["sh_up"].rearrange("(c p) n -> p c n", p=P)).then_inc(s.sh_loaded, 16)
            sp.wait_ge(projected, len(tiles))
            sp.dma_start(m.sdn[:, :, :], d["sh_down"].rearrange("(c p) n -> p c n", p=P)).then_inc(s.shd_loaded, 16)

        @block.tensor
        def _(pe):
            pe.wait_ge(s.wkv_loaded, 32)
            pe.wait_ge(s.wq_loaded, 16)
            pe.wait_ge(s.ln1.hT, NT)

            def rotate(j):
                pe.wait_ge(biased, j + 1)
                if j >= 2:
                    pe.wait_ge(sined, j - 1)
                pe.matmul(ps[:, 2 + j % 2, :], m.const(C_ROT, P), m.qb[j % 2][:, :], start=True, stop=True).then_inc(rotated, 1)

            for j, (kind, c) in enumerate(tiles):
                w = m.wk if kind == "k" else m.wq
                if j >= 2:
                    pe.wait_ge(biased, j - 1)
                for dc in range(DC):
                    last = pe.matmul(ps[:, j % 2, :], w[:, dc, c * P:(c + 1) * P], m.hT[:, dc, :],
                                     start=dc == 0, stop=dc == DC - 1)
                last.then_inc(projected, 1)
                if j:
                    rotate(j - 1)
                if 1 <= j <= NT:
                    t = j - 1
                    for dc in range(DC):
                        last = pe.matmul(ps[:, 4 + t, 0:KV * HD], m.hT[:, dc, t * P:(t + 1) * P], m.wv[:, dc, :],
                                         start=dc == 0, stop=dc == DC - 1)
                    last.then_inc(v_ps, 1)
            rotate(len(tiles) - 1)

            def score(u):
                t, pair = u // PAIRS, u % PAIRS
                if u >= 2:
                    pe.wait_ge(exped, 2 * (u - 1))
                for i in range(2):
                    head = 2 * pair + i
                    g, bank = head // (HEADS // KV), u % 2 * 2 + i
                    q, w = m.q2[:, head, t * P:(t + 1) * P], (t + 1) * P
                    pe.matmul(ps[:, bank, 0:w], q, m.k2h[:, g, 0:w], start=True, stop=False)
                    last = pe.matmul(ps[:, bank, 0:w], q, m.k2l[:, g, 0:w], start=False, stop=True)
                last.then_inc(scored, 1)

            def turn(u):
                t = u // PAIRS
                pe.wait_ge(exped, 2 * (u + 1))
                if u >= 1:
                    pe.wait_ge(pt0, u)
                    pe.wait_ge(pt1, u)
                for i in range(2):
                    for k in range(t + 1):
                        last = pe.transpose(ps[:, 4 + i, k * P:(k + 1) * P], m.ap[u % 2][:, i, k * P:(k + 1) * P], ident)
                last.then_inc(turned, 1)

            def value(u):
                t, pair = u // PAIRS, u % PAIRS
                pe.wait_ge(pt0, u + 1)
                pe.wait_ge(pt1, u + 1)
                if u >= 2:
                    pe.wait_ge(out_made, u - 1)
                for i in range(2):
                    g = (2 * pair + i) // (HEADS // KV)
                    for k in range(t + 1):
                        last = pe.matmul(ps[:, 6 + u % 2, i * P:(i + 1) * P], m.apt[u % 2][:, i, k * P:(k + 1) * P],
                                         m.v[:, k, g * HD:g * HD + P], start=k == 0, stop=k == t)
                last.then_inc(valued, 1)

            pe.wait_ge(split_done, len(tiles))
            pe.wait_ge(v_made, NT)
            pe.wait_ge(v_pad, 1)
            score(0)
            score(1)
            for u in range(AU):
                turn(u)
                if u + 2 < AU:
                    score(u + 2)
                if u >= 1:
                    value(u - 1)
            value(AU - 1)
            pe.wait_ge(s.wo_loaded, 16)

            def turn_out(t):
                pe.wait_ge(out_made, PAIRS * (t + 1))
                pe.wait_ge(out_made, AU)
                if t >= 1:
                    pe.wait_ge(oT0, t)
                    pe.wait_ge(oT1, t)
                for c in range(QT):
                    last = pe.transpose(ps[:, 4 + c // 4, c % 4 * P:(c % 4 + 1) * P], m.ao[:, t, c * P:(c + 1) * P], ident)
                last.then_inc(o_turned, 1)

            turn_out(0)
            for t in range(NT):
                pe.wait_ge(oT0, t + 1)
                pe.wait_ge(oT1, t + 1)
                if t + 1 < NT:
                    turn_out(t + 1)
                for c in range(QT):
                    last = pe.matmul(ps[:, t, :], m.aoT[t % 2][:, c, :], m.wo[:, c, :], start=c == 0, stop=c == QT - 1)
                last.then_inc(wo_done, 1)
            pe.wait_ge(x2, NT)
            ln.tensor(pe)

        @block.scalar
        def _(act):
            def bias(j):
                kind, c = tiles[j]
                col = (R_BK if kind == "k" else R_BQ) + c
                act.wait_ge(projected, j + 1)
                if j >= 2:
                    act.wait_ge(rotated, j - 1)
                    act.wait_ge(cosed, j - 1)
                act.activation(m.qb[j % 2][:, :], ps[:, j % 2, :], ACT.Identity, bias=m.wT[:, col:col + 1]).then_inc(biased, 1)

            def split_hi(j):
                kind, c = tiles[j]
                act.wait_ge(summed, j + 1)
                src = m.qc[j % 2]
                for i in range(2):
                    own = slice(i * HD, (i + 1) * HD)
                    other = slice((1 - i) * HD, (2 - i) * HD)
                    if kind == "q":
                        act.activation(m.q2[own, 2 * c + i, :], src[own, :], ACT.Copy).then_inc(q_hi, 1)
                    else:
                        act.activation(m.k2h[own, 2 * c + i, :], src[own, :], ACT.Copy).then_inc(k_hi, 1)
                        act.activation(m.k2h[other, 2 * c + i, :], src[own, :], ACT.Copy).then_inc(k_hi, 1)

            for j in range(len(tiles)):
                bias(j)
                if j:
                    split_hi(j - 1)
            split_hi(len(tiles) - 1)

            def exps(u):
                t = u // PAIRS
                act.wait_ge(bias_made, u + 1)
                if u >= 2:
                    act.wait_ge(turned, u - 1)
                    act.wait_ge(inv, u // 4 * 4 - 4 + 1 + u % 4 if u >= 4 else 1)
                for i in range(2):
                    w = (t + 1) * P
                    act.activation(m.ap[u % 2][:, i, 0:w], ps[:, u % 2 * 2 + i, 0:w], ACT.Exp, scale=ATT_SCALE,
                                   bias=m.anb[:, u % 4, i:i + 1],
                                   accum_out=m.ars[:, u % 4, i:i + 1]).then_inc(exped, 1)

            def move0(u):
                w = (u // PAIRS + 1) * P
                act.wait_ge(turned, u + 1)
                if u >= 2:
                    act.wait_ge(valued, u - 1)
                act.activation(m.apt[u % 2][:, 0, 0:w], ps[:, 4, 0:w], ACT.Copy).then_inc(pt0, 1)

            exps(0)
            exps(1)
            for u in range(AU):
                move0(u)
                if u + 2 < AU:
                    exps(u + 2)
            for t in range(NT):
                act.wait_ge(o_turned, t + 1)
                if t >= 2:
                    act.wait_ge(wo_done, t - 1)
                act.activation(m.aoT[t % 2][:, 0:4, :], ps[:, 4, :].rearrange("p (c n) -> p c n", c=4),
                               ACT.Copy).then_inc(oT0, 1)
            ln.scalar(act)

        @block.vector
        def _(dve):
            dve.memset(m.v[:, :, KV * HD:], 0.0).then_inc(v_pad, 1)

            def rotary(j):
                b = j % 2
                dve.wait_ge(biased, j + 1)
                if j >= 2:
                    dve.wait_ge(split_done, j - 1)
                    dve.wait_ge(q_hi if tiles[j - 2][0] == "q" else k_hi, 2 * (j - 3) if tiles[j - 2][0] == "q" else 4 * (j - 1))
                dve.tensor_tensor(m.qc[b][:, :], m.qb[b][:, :], m.const(C_COS, N), ALU.mult).then_inc(cosed, 1)
                dve.wait_ge(rotated, j + 1)
                dve.tensor_tensor(m.qs[b][:, :], ps[:, 2 + b, :], m.const(C_SIN, N), ALU.mult).then_inc(sined, 1)
                dve.wait_ge(cosed, j + 1)
                dve.wait_ge(sined, j + 1)
                dve.tensor_tensor(m.qc[b][:, :], m.qc[b][:, :], m.qs[b][:, :], ALU.add).then_inc(summed, 1)

            def split_lo(j):
                kind, c = tiles[j]
                src = m.qc[j % 2]
                dve.wait_ge(summed, j + 1)
                for i in range(2):
                    own = slice(i * HD, (i + 1) * HD)
                    other = slice((1 - i) * HD, (2 - i) * HD)
                    if kind == "q":
                        dve.wait_ge(q_hi, 2 * (j - 2) + i + 1)
                        last = dve.tensor_tensor(m.q2[other, 2 * c + i, :], src[own, :],
                                                 m.q2[own, 2 * c + i, :].bitcast(F32), ALU.subtract)
                    else:
                        dve.wait_ge(k_hi, 4 * j + 2 * i + 2)
                        hi = m.k2h[own, 2 * c + i, :].bitcast(F32)
                        dve.tensor_tensor(m.k2l[own, 2 * c + i, :], src[own, :], hi, ALU.subtract)
                        last = dve.tensor_tensor(m.k2l[other, 2 * c + i, :], src[own, :], hi, ALU.subtract)
                last.then_inc(split_done, 1)

            for j in range(len(tiles)):
                rotary(j)
                if j:
                    split_lo(j - 1)
                if 1 <= j <= NT:
                    t = j - 1
                    dve.wait_ge(v_ps, t + 1)
                    dve.tensor_tensor(m.v[:, t, 0:KV * HD], ps[:, 4 + t, 0:KV * HD], m.bv[:, :], ALU.add).then_inc(v_made, 1)
            split_lo(len(tiles) - 1)
            for t in range(NT):
                dve.tensor_tensor(m.x[:, t, :], m.x[:, t, :], m.bo[:, :], ALU.add).then_inc(xb, 1)

            def maxes(u):
                t, bank, slot = u // PAIRS, u % 2 * 2, u % 4
                w = (t + 1) * P
                dve.wait_ge(scored, u + 1)
                diag = ps[:, bank:bank + 2, t * P:w]
                dve.tensor_tensor(diag, diag, m.const(C_MASK, P).unsqueeze(1).to_broadcast([P, 2, P]), ALU.add).then_inc(masked, 1)
                dve.wait_ge(masked, u + 1)
                if u >= 4:
                    dve.wait_ge(exped, 2 * (u - 3))
                    dve.wait_ge(bias_made, u - 3)
                dve.tensor_reduce(m.amx[:, slot, :], ps[:, bank:bank + 2, 0:w], AX, ALU.max).then_inc(maxed, 1)
                dve.wait_ge(maxed, u + 1)
                dve.tensor_scalar(m.anb[:, slot, :], m.amx[:, slot, :], -ATT_SCALE, None, ALU.mult).then_inc(bias_made, 1)

            def move1(u):
                w = (u // PAIRS + 1) * P
                dve.wait_ge(turned, u + 1)
                if u >= 2:
                    dve.wait_ge(valued, u - 1)
                dve.tensor_copy(m.apt[u % 2][:, 1, 0:w], ps[:, 5, 0:w]).then_inc(pt1, 1)

            def invert(u):
                dve.wait_ge(exped, 2 * (u + 1))
                if u >= 4:
                    dve.wait_ge(out_made, u - 3)
                dve.reciprocal(m.arl[:, u % 4, :], m.ars[:, u % 4, :]).then_inc(inv, 1)

            def output(u):
                t, pair = u // PAIRS, u % PAIRS
                dve.wait_ge(valued, u + 1)
                dve.wait_ge(inv, u + 1)
                dve.tensor_tensor(m.ao[:, t, pair * P:(pair + 1) * P].rearrange("p (i n) -> p i n", i=2),
                                  ps[:, 6 + u % 2, 0:2 * P].rearrange("p (i n) -> p i n", i=2)[:, :, 0:HD],
                                  m.arl[:, u % 4, :].unsqueeze(2).to_broadcast([P, 2, HD]), ALU.mult).then_inc(out_made, 1)

            maxes(0)
            maxes(1)
            for u in range(AU):
                invert(u)
                move1(u)
                if u + 2 < AU:
                    maxes(u + 2)
                if u >= 1:
                    output(u - 1)
            output(AU - 1)
            for t in range(NT):
                dve.wait_ge(o_turned, t + 1)
                if t >= 2:
                    dve.wait_ge(wo_done, t - 1)
                dve.tensor_copy(m.aoT[t % 2][:, 4:8, :], ps[:, 5, :].rearrange("p (c n) -> p c n", c=4)).then_inc(oT1, 1)
            for t in range(NT):
                dve.wait_ge(wo_done, t + 1)
                dve.wait_ge(xb, t + 1)
                dve.tensor_tensor(m.x[:, t, :], m.x[:, t, :], ps[:, t, :], ALU.add).then_inc(x2, 1)
                dve.wait_ge(x2, t + 1)
                ln.vector_stats(dve, t)
            ln.vector(dve)
    s.ln2 = ln


def feed_forward(nc, m, d, sem, s):
    lgT_ps, lgT, lg_ps, lg, top, eq, cand, first, onehot, th, score, rank_ps, own, rank, cnt, over, over_i = (
        sem(x) for x in ("lgT_summed", "lgT_made", "lg_turned", "lg_made", "top_made", "eq_made", "cand_made",
                         "first_made", "onehot_made", "tanh_made", "score_made", "rank_summed", "own_rank_made",
                         "rank_made", "counts_made", "over_made", "over_int_made"))
    xs, xs_hi, xs_lo = sem("xs_made"), sem("xs_hi_made"), sem("xs_lo_made")
    sh_in, sh_sil, sh_act, sh_out, x3 = (sem(x) for x in ("sh_projected", "sh_silu_made", "sh_act_made", "sh_down_done", "x3_made"))
    sel, selT_ps, selT, xg_ps, xg = (sem(x) for x in ("sel_made", "sel_turned", "selT_made", "gathered", "xg_made"))
    gu, sil, act_made, a_ps, actT, y_ps, y_hi, y_lo, put, added = (sem(x) for x in (
        "gu_done", "silu_made", "act_made", "act_turned", "actT_made", "y_done", "y_hi_made", "y_lo_made",
        "put_back", "put_added"))
    gu_loaded = [sem(f"gu_loaded{k}") for k in range(2)]
    d_loaded = [sem(f"down_loaded{k}") for k in range(2)]
    ps = m.ps
    ident = m.const(C_IDENT, P)
    HALF = INNER // 2

    with nc.Block() as block:
        @block.sync
        def _(sp):
            for e in range(E):
                b = e % 2
                if e >= 2:
                    sp.wait_ge(gu, 2 * (e - 1))
                for w, name in ((m.wg, "rt_gate"), (m.wu, "rt_up")):
                    sp.dma_start(w[b][:, :, :], d[name][e].rearrange("(c p) n -> p c n", p=P)).then_inc(gu_loaded[b], 16)
                if e == 1:
                    sp.wait_ge(xg_ps, 2 * DC)
                if e >= 2:
                    sp.wait_ge(y_ps, e - 1)
                sp.dma_start(m.wd[b][:, :, :], d["rt_down"][e].rearrange("(c p) n -> p c n", p=P)).then_inc(d_loaded[b], 16)

        @block.tensor
        def _(pe):
            pe.wait_ge(s.ln2.hT, NT)
            for c in range(DC):
                last = pe.matmul(ps[0:E, 4, :], m.gw[:, c, :], m.hT[:, c, :], start=c == 0, stop=c == DC - 1)
            last.then_inc(lgT_ps, 1)

            def shared_in(k):
                if k >= 2:
                    pe.wait_ge(sh_act, k - 1)
                    pe.wait_ge(sh_sil, k - 1)
                for w, bank in ((m.sg, k % 2), (m.su, 2 + k % 2)):
                    for c in range(DC):
                        last = pe.matmul(ps[:, bank, :], w[:, c, k * P:(k + 1) * P], m.hT[:, c, :],
                                         start=c == 0, stop=c == DC - 1)
                last.then_inc(sh_in, 1)

            pe.wait_ge(s.sh_loaded, 32)
            shared_in(0)
            pe.wait_ge(lgT, 1)
            for t in range(NT):
                last = pe.transpose(ps[:, 5, t * E:(t + 1) * E], m.lgt[:, t * P:(t + 1) * P], m.const(C_IDENT, E, E))
            last.then_inc(lg_ps, 1)
            shared_in(1)
            shared_in(2)
            pe.wait_ge(onehot, 1)
            for t in range(NT):
                for q in range(t + 1):
                    pe.matmul(ps[:, 6, t * E:(t + 1) * E], m.const(C_TRI if q == t else C_ONES, P), m.onehot[:, q, :],
                              start=q == 0, stop=q == t)
            for q in range(NT):
                last = pe.matmul(ps[:, 6, NT * E:(NT + 1) * E], m.const(C_ONES, P), m.onehot[:, q, :],
                                 start=q == 0, stop=q == NT - 1)
            last.then_inc(rank_ps, 1)
            for k in range(3, IC):
                shared_in(k)
            pe.wait_ge(sh_act, IC)
            pe.wait_ge(s.shd_loaded, 16)
            pe.wait_ge(cnt, 1)
            for t in range(NT):
                for k in range(IC):
                    last = pe.matmul(ps[:, 4 + t, :], m.sact[:, k, t * P:(t + 1) * P], m.sdn[:, k, :],
                                     start=k == 0, stop=k == IC - 1)
                last.then_inc(sh_out, 1)
            pe.wait_ge(xs_lo, NT)
            for half in range(2):
                pe.wait_ge(sel, 16 * (half + 1))
                for c in range(DC):
                    if half:
                        pe.wait_ge(xg, c + 1)
                    for t in range(NT):
                        for part in (m.xsh, m.xsl):
                            last = pe.matmul(ps[:, c, :], part[:, t, c * P:(c + 1) * P], m.sel[:, t, :, :],
                                             start=t == 0 and part is m.xsh, stop=t == NT - 1 and part is m.xsl)
                    last.then_inc(xg_ps, 1)
                for q in range(4):
                    e, bank = 4 * half + q, 4 + q
                    pe.wait_ge(x3, q + 1)
                    if half:
                        pe.wait_ge(selT, q + 1)
                    for t in range(NT):
                        last = pe.transpose(ps[:, bank, t * P:(t + 1) * P], m.sel[:, t, q, :].bitcast(F32), ident)
                    last.then_inc(selT_ps, 1)

            def gate_up(e, half):
                b = e % 2
                if half == 0:
                    pe.wait_ge(gu_loaded[b], 32 * (e // 2 + 1))
                if e:
                    pe.wait_ge(act_made, 2 * (e - 1) + half + 1)
                for w, bank in ((m.wg[b], 2 * half), (m.wu[b], 2 * half + 1)):
                    for c in range(DC):
                        last = pe.matmul(ps[:, bank, :], m.xg[:, c, e * P:(e + 1) * P], w[:, c, half * HALF:(half + 1) * HALF],
                                         start=c == 0, stop=c == DC - 1)
                last.then_inc(gu, 1)

            def turn_act(e, half):
                n = 2 * e + half
                pe.wait_ge(act_made, n + 1)
                if n:
                    pe.wait_ge(actT, n)
                for k in range(4):
                    last = pe.transpose(ps[:, 4, k * P:(k + 1) * P], m.act[e % 2][:, (4 * half + k) * P:(4 * half + k + 1) * P], ident)
                last.then_inc(a_ps, 1)

            def down(e):
                pe.wait_ge(actT, 2 * e + 2)
                pe.wait_ge(d_loaded[e % 2], 16 * (e // 2 + 1))
                if e:
                    pe.wait_ge(y_lo, e)
                for k in range(IC):
                    last = pe.matmul(ps[:, 5, :], m.actT[e % 2][:, k * P:(k + 1) * P], m.wd[e % 2][:, k, :],
                                     start=k == 0, stop=k == IC - 1)
                last.then_inc(y_ps, 1)

            def put_back(half):
                pe.wait_ge(y_lo, 4 * (half + 1))
                for t in range(NT):
                    n = 4 * half + t
                    if n >= 2:
                        pe.wait_ge(added, n - 1)
                    for q in range(4):
                        for part in (m.yh, m.yl):
                            last = pe.matmul(ps[:, 6 + t % 2, :], m.selT[:, 4 * half + q, t * P:(t + 1) * P], part[:, q, :],
                                             start=q == 0 and part is m.yh, stop=q == 3 and part is m.yl)
                    last.then_inc(put, 1)

            pe.wait_ge(xg, 2 * DC)
            pe.wait_ge(selT, E)
            for e in range(E):
                gate_up(e, 0)
                if e:
                    turn_act(e - 1, 1)
                gate_up(e, 1)
                turn_act(e, 0)
                if e == 5:
                    put_back(0)
                if e:
                    down(e - 1)
            turn_act(E - 1, 1)
            down(E - 1)
            put_back(1)

        @block.scalar
        def _(act):
            def move_act(n):
                e, half = n // 2, n % 2
                act.wait_ge(a_ps, n + 1)
                if e >= 2:
                    act.wait_ge(y_ps, e - 1)
                act.activation(m.actT[e % 2][:, half * HALF:(half + 1) * HALF], ps[:, 4, :], ACT.Copy).then_inc(actT, 1)

            def hi_of_y(e):
                act.wait_ge(y_ps, e + 1)
                if e >= 4:
                    act.wait_ge(put, NT)
                act.activation(m.yh[:, e % 4, :], ps[:, 5, :], ACT.Copy).then_inc(y_hi, 1)

            act.wait_ge(lgT_ps, 1)
            act.activation(m.lgt[:, :], ps[0:E, 4, :], ACT.Copy).then_inc(lgT, 1)

            def shared_silu(k):
                act.wait_ge(sh_in, k + 1)
                if k >= 2:
                    act.wait_ge(sh_act, k - 1)
                if k < 2:
                    act.wait_ge(lg_ps, 1)
                act.activation(m.sil[k % 2][:, :], ps[:, k % 2, :], ACT.Silu).then_inc(sh_sil, 1)

            shared_silu(0)
            shared_silu(1)
            act.wait_ge(top, 1)
            act.activation(m.score[:, :], m.top[:, :], ACT.Tanh, scale=0.5).then_inc(th, 1)
            for k in range(2, IC):
                shared_silu(k)

            for t in range(NT):
                act.wait_ge(xs, t + 1)
                act.activation(m.xsh[:, t, :], m.h[:, t, :], ACT.Copy).then_inc(xs_hi, 1)
            for half in range(2):
                for c in range(DC):
                    act.wait_ge(xg_ps, half * DC + c + 1)
                    act.activation(m.xg[:, c, half * N:(half + 1) * N], ps[:, c, :], ACT.Copy).then_inc(xg, 1)
            for e in range(E):
                for half in range(2):
                    n = 2 * e + half
                    act.wait_ge(gu, n + 1)
                    if e >= 2:
                        act.wait_ge(a_ps, 2 * (e - 2) + half + 1)
                    act.activation(m.act[e % 2][:, half * HALF:(half + 1) * HALF], ps[:, 2 * half, :], ACT.Silu).then_inc(sil, 1)
                    if n:
                        move_act(n - 1)
                    if half and e:
                        hi_of_y(e - 1)
            move_act(2 * E - 1)
            hi_of_y(E - 1)

        @block.vector
        def _(dve):
            def shared_act(k):
                dve.wait_ge(sh_sil, k + 1)
                dve.tensor_tensor(m.sact[:, k, :], m.sil[k % 2][:, :], ps[:, 2 + k % 2, :], ALU.mult).then_inc(sh_act, 1)

            dve.wait_ge(lg_ps, 1)
            dve.tensor_copy(m.lg[:, :, :], ps[:, 5, 0:NT * E].rearrange("p (t e) -> p t e", t=NT)).then_inc(lg, 1)
            dve.wait_ge(lg, 1)
            dve.tensor_reduce(m.top[:, :], m.lg[:, :, :], AX, ALU.max).then_inc(top, 1)
            dve.wait_ge(top, 1)
            wide = [P, NT, E]
            dve.tensor_tensor(m.eq[:, :, :], m.lg[:, :, :], m.top[:, :].unsqueeze(2).to_broadcast(wide), ALU.is_equal).then_inc(eq, 1)
            dve.wait_ge(eq, 1)
            dve.tensor_tensor(m.tmp8[:, :, :], m.eq[:, :, :], m.const(C_PREF, E).unsqueeze(1).to_broadcast(wide), ALU.mult).then_inc(cand, 1)
            dve.wait_ge(cand, 1)
            dve.tensor_reduce(m.first[:, :], m.tmp8[:, :, :], AX, ALU.max).then_inc(first, 1)
            dve.wait_ge(first, 1)
            dve.tensor_tensor(m.onehot[:, :, :], m.tmp8[:, :, :], m.first[:, :].unsqueeze(2).to_broadcast(wide), ALU.is_equal).then_inc(onehot, 1)
            shared_act(0)
            dve.wait_ge(th, 1)
            dve.tensor_scalar(m.score[:, :], m.score[:, :], 0.5, 0.5, ALU.mult, ALU.add).then_inc(score, 1)
            dve.wait_ge(score, 1)
            for t in range(NT):
                dve.tensor_scalar(m.h[:, t, :], m.h[:, t, :], m.score[:, t:t + 1], None, ALU.mult).then_inc(xs, 1)
            shared_act(1)
            shared_act(2)
            dve.wait_ge(rank_ps, 1)
            dve.wait_ge(onehot, 1)
            dve.tensor_tensor(m.tmp8[:, :, :], ps[:, 6, 0:NT * E].rearrange("p (t e) -> p t e", t=NT), m.onehot[:, :, :], ALU.mult).then_inc(own, 1)
            dve.tensor_reduce(m.over[:, :], ps[:, 6, NT * E:(NT + 1) * E], AX, ALU.max).then_inc(cnt, 1)
            dve.wait_ge(own, 1)
            dve.tensor_reduce(m.rank[:, :], m.tmp8[:, :, :], AX, ALU.add).then_inc(rank, 1)
            dve.wait_ge(cnt, 1)
            dve.tensor_scalar(m.over[:, :], m.over[:, :], -float(P), 0.0, ALU.add, ALU.max).then_inc(over, 1)
            dve.wait_ge(over, 1)
            dve.tensor_copy(m.over_i[:, :], m.over[:, :]).then_inc(over_i, 1)
            for k in range(3, IC):
                shared_act(k)

            def select(half):
                if half:
                    dve.wait_ge(xg_ps, DC)
                    dve.wait_ge(selT_ps, 4)
                for t in range(NT):
                    for q in range(4):
                        dve.tensor_scalar(m.sel[:, t, q, :], m.const(C_IOTA, P), m.rank[:, t:t + 1],
                                          m.onehot[:, t, 4 * half + q:4 * half + q + 1], ALU.is_equal, ALU.mult).then_inc(sel, 1)

            def move_sel(half):
                for q in range(4):
                    e = 4 * half + q
                    dve.wait_ge(selT_ps, e + 1)
                    dve.tensor_copy(m.selT[:, e, :], ps[:, 4 + q, :]).then_inc(selT, 1)

            dve.wait_ge(rank, 1)
            select(0)
            for t in range(NT):
                dve.wait_ge(xs_hi, t + 1)
                dve.tensor_tensor(m.xsl[:, t, :], m.h[:, t, :], m.xsh[:, t, :].bitcast(F32), ALU.subtract).then_inc(xs_lo, 1)
            for t in range(NT):
                dve.wait_ge(sh_out, t + 1)
                dve.tensor_tensor(m.x[:, t, :], m.x[:, t, :], ps[:, 4 + t, :], ALU.add).then_inc(x3, 1)
            move_sel(0)
            select(1)
            move_sel(1)

            def act_of(n):
                e, half = n // 2, n % 2
                a = m.act[e % 2][:, half * HALF:(half + 1) * HALF]
                dve.wait_ge(sil, n + 1)
                dve.tensor_tensor(a, a, ps[:, 2 * half + 1, :], ALU.mult).then_inc(act_made, 1)

            def lo_of_y(e):
                dve.wait_ge(y_hi, e + 1)
                dve.tensor_tensor(m.yl[:, e % 4, :], ps[:, 5, :], m.yh[:, e % 4, :].bitcast(F32), ALU.subtract).then_inc(y_lo, 1)

            def add_back(half):
                for t in range(NT):
                    n = 4 * half + t
                    dve.wait_ge(put, n + 1)
                    dve.wait_ge(added, n - 3) if n >= 4 else dve.wait_ge(x3, t + 1)
                    dve.tensor_tensor(m.x[:, t, :], m.x[:, t, :], ps[:, 6 + t % 2, :], ALU.add).then_inc(added, 1)

            for e in range(E):
                act_of(2 * e)
                act_of(2 * e + 1)
                if e == 5:
                    add_back(0)
                if e:
                    lo_of_y(e - 1)
            lo_of_y(E - 1)
            add_back(1)


def overflow(nc, m, d, sem):
    loaded, moved, sel, selT_ps, selT, xg_ps, xg, gu, sil, act_made, a_ps, actT, y_ps, y_hi, y_lo, put, added = (
        sem("over_" + x) for x in ("loaded", "rank_moved", "sel", "selT_ps", "selT", "xg_ps", "xg", "gu", "silu", "act",
                                   "act_turned", "actT", "y", "y_hi", "y_lo", "put", "added"))
    ps = m.ps
    ident = m.const(C_IDENT, P)
    ROUNDS = (N - 1) // P
    HALF = INNER // 2

    def rounds(eng, body):
        with eng.Fori(0, ROUNDS) as tile:
            with eng.Fori(0, E) as e:
                body(tile, e, tile * E + e)

    with nc.Block() as block:
        @block.gpsimd
        def _(pool):
            pool.memset(m.over[:, :], 0.0).then_inc(added, 1)

        @block.sync
        def _(sp):
            def body(tile, e, n):
                sp.wait_ge(added, n * NT + 1)
                for w, name in ((m.wg[0], "rt_gate"), (m.wu[0], "rt_up"), (m.wd[0], "rt_down")):
                    sp.dma_start(w[:, :, :], d[name][e].rearrange("(c p) n -> p c n", p=P)).then_inc(loaded, 16)

            rounds(sp, body)

        @block.tensor
        def _(pe):
            def body(tile, e, n):
                pe.wait_ge(sel, n * NT + NT)
                for t in range(NT):
                    last = pe.transpose(ps[:, 0, t * P:(t + 1) * P], m.osel[:, t, :].bitcast(F32), ident)
                last.then_inc(selT_ps, 1)
                for c in range(DC):
                    for t in range(NT):
                        for part in (m.xsh, m.xsl):
                            last = pe.matmul(ps[:, 1, c * P:(c + 1) * P], part[:, t, c * P:(c + 1) * P], m.osel[:, t, :],
                                             start=t == 0 and part is m.xsh, stop=t == NT - 1 and part is m.xsl)
                last.then_inc(xg_ps, 1)
                pe.wait_ge(xg, n + 1)
                pe.wait_ge(loaded, n * 48 + 48)
                for half in range(2):
                    for w, bank in ((m.wg[0], 2 + 2 * half), (m.wu[0], 3 + 2 * half)):
                        for c in range(DC):
                            last = pe.matmul(ps[:, bank, :], m.oxg[:, c, :], w[:, c, half * HALF:(half + 1) * HALF],
                                             start=c == 0, stop=c == DC - 1)
                    last.then_inc(gu, 1)
                pe.wait_ge(act_made, n * 2 + 2)
                for k in range(IC):
                    last = pe.transpose(ps[:, 6 + k // 4, k % 4 * P:(k % 4 + 1) * P], m.act[0][:, k * P:(k + 1) * P], ident)
                last.then_inc(a_ps, 1)
                pe.wait_ge(actT, n + 1)
                for k in range(IC):
                    last = pe.matmul(ps[:, 0, :], m.actT[0][:, k * P:(k + 1) * P], m.wd[0][:, k, :], start=k == 0, stop=k == IC - 1)
                last.then_inc(y_ps, 1)
                pe.wait_ge(y_lo, n + 1)
                for t in range(NT):
                    for part in (m.yh, m.yl):
                        last = pe.matmul(ps[:, 2 + t, :], m.oselT[:, t * P:(t + 1) * P], part[:, 0, :],
                                         start=part is m.yh, stop=part is m.yl)
                last.then_inc(put, 1)

            rounds(pe, body)

        @block.scalar
        def _(act):
            def body(tile, e, n):
                act.wait_ge(selT_ps, n + 1)
                act.activation(m.oselT[:, :], ps[:, 0, :], ACT.Copy).then_inc(selT, 1)
                act.wait_ge(xg_ps, n + 1)
                act.activation(m.oxg[:, :, :], ps[:, 1, :].rearrange("p (c n) -> p c n", c=DC), ACT.Copy).then_inc(xg, 1)
                for half in range(2):
                    act.wait_ge(gu, n * 2 + half + 1)
                    act.activation(m.act[0][:, half * HALF:(half + 1) * HALF], ps[:, 2 + 2 * half, :], ACT.Silu).then_inc(sil, 1)
                act.wait_ge(a_ps, n + 1)
                act.activation(m.actT[0][:, :], ps[:, 6:8, :], ACT.Copy).then_inc(actT, 1)
                act.wait_ge(y_ps, n + 1)
                act.activation(m.yh[:, 0, :], ps[:, 0, :], ACT.Copy).then_inc(y_hi, 1)

            rounds(act, body)

        @block.vector
        def _(dve):
            dve.tensor_scalar(m.rank[:, :], m.rank[:, :], -float(P), None, ALU.add).then_inc(moved, 1)

            def body(tile, e, n):
                dve.wait_ge(added, n * NT + 1)
                dve.wait_ge(moved, tile + 1)
                for t in range(NT):
                    dve.tensor_scalar(m.osel[:, t, :], m.const(C_IOTA, P), m.rank[:, t:t + 1], m.onehot[:, t, bass.ds(e, 1)],
                                      ALU.is_equal, ALU.mult).then_inc(sel, 1)
                for half in range(2):
                    dve.wait_ge(sil, n * 2 + half + 1)
                    a = m.act[0][:, half * HALF:(half + 1) * HALF]
                    dve.tensor_tensor(a, a, ps[:, 3 + 2 * half, :], ALU.mult).then_inc(act_made, 1)
                dve.wait_ge(y_hi, n + 1)
                dve.tensor_tensor(m.yl[:, 0, :], ps[:, 0, :], m.yh[:, 0, :].bitcast(F32), ALU.subtract).then_inc(y_lo, 1)
                dve.wait_ge(put, n + 1)
                for t in range(NT):
                    dve.tensor_tensor(m.x[:, t, :], m.x[:, t, :], ps[:, 2 + t, :], ALU.add).then_inc(added, 1)

            with dve.Fori(0, ROUNDS) as tile:
                with dve.Fori(0, E) as e:
                    body(tile, e, tile * E + e)
                dve.wait_ge(sel, (tile + 1) * E * NT)
                dve.tensor_scalar(m.rank[:, :], m.rank[:, :], -float(P), None, ALU.add).then_inc(moved, 1)


def store(nc, m, out, stored):
    with nc.Block() as block:
        @block.sync
        def _(sp):
            sp.dma_start(out.rearrange("o (t p) d -> p (o t) d", p=P), m.x[:, :, :]).then_inc(stored, 16)
            sp.wait_ge(stored, 16)


class Signals:
    pass


def perceiver_block(nc, d, out, phases=6):
    with ExitStack() as ctx:
        m = Memory(nc, ctx)
        s = Signals()

        made = []

        def sem(name):
            made.append(nc.alloc_semaphore(name))
            return made[-1]

        stored = nc.alloc_semaphore("stored")
        setup(nc, m, d, sem, s)
        if phases > 1:
            cross_attention(nc, m, sem, s)
            cross_output(nc, m, d, sem, s)
        if phases > 2:
            self_attention(nc, m, d, sem, s)
        if phases > 3:
            feed_forward(nc, m, d, sem, s)
        if phases > 4:
            beyond = nc.values_load(m.over_i[0:1, 0:1], min_val=0, max_val=N,
                                    skip_runtime_bounds_check_because="a count of tokens less 128, not below 0")
            with nc.If(beyond > 0):
                nc.clear_and_free_semaphores(made[:])
                nc.all_engine_barrier()
                overflow(nc, m, d, sem)
        store(nc, m, out, stored)


_NAMES = {"x": "x", "ctx_1024": "ctx", "L0_xattn_w_sim": "w_sim", "L0_xattn_b_sim": "b_sim", "L0_xattn_W_qv": "W_qv",
          "L0_xattn_b_qv": "b_qv", "L0_attn_Wq": "Wq", "L0_attn_bq": "bq", "L0_attn_Wk": "Wk", "L0_attn_bk": "bk",
          "L0_attn_Wv": "Wv", "L0_attn_bv": "bv", "L0_attn_Wo": "Wo", "L0_attn_bo": "bo", "L0_ffn_gate_w": "gate_w",
          "L0_ffn_sh_gate": "sh_gate", "L0_ffn_sh_up": "sh_up", "L0_ffn_sh_down": "sh_down",
          "L0_ffn_rt_gate": "rt_gate", "L0_ffn_rt_up": "rt_up", "L0_ffn_rt_down": "rt_down"}


def kernel(**inputs):
    import concourse.bacc as bacc
    from concourse.bass_utils import run_bass_kernel_spmd

    nc = bacc.Bacc("TRN2", target_bir_lowering=False, num_devices=1)
    arrays = {_NAMES[k]: np.ascontiguousarray(v) for k, v in inputs.items()}
    arrays["consts"] = constants()
    arrays = {f"in_{k}": v for k, v in arrays.items()}
    d = {k[3:]: nc.dram_tensor(k, v.shape, mybir.dt.from_np(v.dtype), kind="ExternalInput").ap() for k, v in arrays.items()}
    out = nc.dram_tensor("out", (1, N, D), F32, kind="ExternalOutput").ap()
    perceiver_block(nc, d, out)
    r = run_bass_kernel_spmd(nc, [arrays], core_ids=[0])
    return r.results[0]["out"]
```

```python
from contextlib import ExitStack

import numpy as np

import concourse.bass as bass
from concourse import mybir

F32 = mybir.dt.float32
F32R = mybir.dt.float32r
I32 = mybir.dt.int32
ALU = mybir.AluOpType
ACT = mybir.ActivationFunctionType
AX = mybir.AxisListType.X

P = 128
N = 512
D = 512
NT = N // P
DC = D // P
CTX = 8192
CB = 512
JT = CB // P
BLOCKS = CTX // CB
UNITS = BLOCKS * NT
STEP = 2 * NT
HEADS, KV, HD = 16, 4, 64
QT = HEADS * HD // P
INNER = 1024
IC = INNER // P
E = 8
EPS = 1e-5
FAR = 3e38
HIDDEN = -1e30
ATT_SCALE = HD ** -0.5

C_IDENT, C_ROT, C_MASK, C_TRI, C_ONES, C_IOTA = (k * P for k in range(6))
C_COS = 6 * P
C_SIN = C_COS + N
C_PREF = C_SIN + N
C_EPS = C_PREF + E
C_ZERO = C_EPS + 1
C_ALL = C_ZERO + 1

R_W1, R_W2, R_W3, R_BQ, R_BK = 0, DC, 2 * DC, 3 * DC, 3 * DC + QT
ROWS = R_BK + 2


def constants():
    c = np.zeros((P, C_ALL), np.float32)
    i = np.arange(P)
    c[i, C_IDENT + i] = 1.0
    first = i % HD < HD // 2
    c[i[first] + HD // 2, C_ROT + i[first]] = -1.0
    c[i[~first] - HD // 2, C_ROT + i[~first]] = 1.0
    c[:, C_MASK:C_MASK + P] = np.where(i[None, :] > i[:, None], HIDDEN, 0.0)
    c[:, C_TRI:C_TRI + P] = i[:, None] < i[None, :]
    c[:, C_ONES:C_ONES + P] = 1.0
    c[:, C_IOTA:C_IOTA + P] = i[None, :]
    freq = np.float32(1.0) / np.float32(10000.0) ** (np.arange(0, HD, 2, dtype=np.float32) / np.float32(HD))
    angle = np.arange(N, dtype=np.float32)[None, :] * freq[i % (HD // 2)][:, None]
    c[:, C_COS:C_COS + N] = np.cos(angle)
    c[:, C_SIN:C_SIN + N] = np.sin(angle)
    c[:, C_PREF:C_PREF + E] = E - np.arange(E)[None, :]
    c[:, C_EPS] = EPS
    return c


class Memory:

    def __init__(self, nc, ctx):
        base = (nc.sbuf_base + 31) // 32 * 32
        self.nc = nc

        def at(name, kb, shape, dt=F32):
            return nc.alloc_sbuf_tensor_at(name, shape, dt, offset=base + int(kb * 1024))

        self.ps = ctx.enter_context(nc.psum_tensor("banks", [P, 8, 512], F32))
        self.x = at("x_res", 0, [P, NT, D])
        self.h = at("h_norm", 8, [P, NT, D])
        self.hT = at("hT", 16, [P, DC, N])
        self.c = at("consts", 40, [P, C_ALL])
        self.small_at = 47.5 * 1024

        def small(name, shape, dt=F32):
            size = int(np.prod(shape[1:])) * 4
            t = nc.alloc_sbuf_tensor_at(name, shape, dt, offset=base + int(self.small_at))
            self.small_at += (size + 31) // 32 * 32
            assert self.small_at <= 50 * 1024
            return t

        self.wT = small("wT", [P, ROWS])
        self.stats = small("ln_stats", [P, NT, 6])
        self.mv = small("ln_mean_var", [P, NT, 2])
        self.sd = small("ln_sd", [P, NT])
        self.rstd = small("ln_rstd", [P, NT])
        self.e1 = small("enc_w1", [P, NT])
        self.negm = small("neg_max", [P, 2, NT])
        self.mx = small("block_max", [P, 2 * NT])
        self.alpha = small("alpha", [P, 2 * NT])
        self.rowsum = small("row_sum", [P, 2 * NT])
        self.den = small("denominator", [P, NT])
        self.rden = small("inv_denominator", [P, NT])
        self.bsim = small("b_sim", [P, 1])
        self.mcol = small("token_max", [P, NT])
        self.r1 = small("row_scalars", [1, 4])
        self.batt = small("batt_col", [P, NT])
        self.hc = small("hc_bar", [P, DC])
        self.amx = small("att_max", [P, 4, 2])
        self.anb = small("att_bias", [P, 4, 2])
        self.ars = small("att_sum", [P, 4, 2])
        self.arl = small("att_inv", [P, 4, 2])
        self.gw = small("gate_w", [P, DC, E])
        self.lg = small("logits", [P, NT, E])
        self.top = small("top", [P, NT])
        self.eq = small("is_top", [P, NT, E])
        self.first = small("first_top", [P, NT])
        self.onehot = small("onehot", [P, NT, E])
        self.score = small("score", [P, NT])
        self.tmp8 = small("rank_of_own", [P, NT, E])
        self.rank = small("rank", [P, NT])
        self.cnt = small("counts", [P, E])
        self.over = small("overflow", [P, 1])
        self.over_i = small("overflow_int", [P, 1], I32)
        self.bqv = at("b_qv_all", 198, [P, D])
        self.bo = at("b_o_all", 200, [P, D])
        self.bv = at("b_v_all", 202, [P, KV * HD])
        self.rows = at("rows", 203, [ROWS, P])
        self.mrow = at("token_max_row", 204, [1, N])
        self.hTh = at("hT_hi", 24, [P, DC, N], F32R)
        self.hTl = at("hT_lo", 32, [P, DC, N], F32R)
        self.gh = at("g_hi", 24, [P, DC, N], F32R)
        self.gl = at("g_lo", 32, [P, DC, N], F32R)
        self.raw = [at(f"ctx_raw{s}", 50 + 8 * s, [P, JT, D]) for s in range(2)]
        self.nh = [at(f"ctx_hi{s}", 66 + 8 * s, [P, JT, D], F32R) for s in range(2)]
        self.nl = [at(f"ctx_lo{s}", 82 + 8 * s, [P, JT, D], F32R) for s in range(2)]
        self.th = [at(f"ctxT_hi{s}", 98 + 8 * s, [P, DC, CB], F32R) for s in range(2)]
        self.tl = [at(f"ctxT_lo{s}", 114 + 8 * s, [P, DC, CB], F32R) for s in range(2)]
        self.p = [at(f"probs{s}", 130 + 2 * s, [P, CB]) for s in range(2)]
        self.pth = [at(f"probsT_hi{s}", 134 + 2 * s, [P, CB], F32R) for s in range(2)]
        self.ptl = [at(f"probsT_lo{s}", 138 + 2 * s, [P, CB], F32R) for s in range(2)]
        self.o = at("attended", 142, [P, NT, D])
        self.g = at("g_whole", 142, [P, DC, N])

        def weight(name, kb, shape, hi_kb=None):
            hi_kb = kb + int(np.prod(shape[1:])) * 4 // 1024 if hi_kb is None else hi_kb
            return at(name, kb, shape), at(name + "_hi", hi_kb, shape, F32R), at(name + "_lo", kb, shape, F32R)

        self.w23, self.w23h, self.w23l = weight("w_qv23", 150, [P, 2, DC, D])
        self.w1, self.w1h, self.w1l = weight("w_qv1", 182, [P, DC, D], 82)
        self.w4 = at("w_qv4", 190, [P, DC, D])
        self.hqTh = at("hqT_hi", 50, [P, DC, N], F32R)
        self.hqTl = at("hqT_lo", 58, [P, DC, N], F32R)
        self.ehTh = at("enc_hqT_hi", 66, [P, DC, N], F32R)
        self.ehTl = at("enc_hqT_lo", 74, [P, DC, N], F32R)
        self.ehT = at("enc_hqT", 90, [P, DC, N])
        self.wq, self.wqh, self.wql = weight("w_q", 98, [P, DC, HEADS * HD])
        self.wkv, self.wkvh, self.wkvl = weight("w_kv", 130, [P, 2, DC, KV * HD])
        self.wo, self.woh, self.wol = weight("w_o", 154, [P, QT, D])
        self.k2h = at("k_hi_twice", 8, [P, KV, N], F32R)
        self.k2l = at("k_lo_twice", 16, [P, KV, N], F32R)
        self.q2 = at("q_hi_lo", 50, [P, HEADS, N], F32R)
        self.qb = [at(f"q_biased{s}", 82 + 2 * s, [P, N]) for s in range(2)]
        self.qc = [at(f"q_cos{s}", 86 + 2 * s, [P, N]) for s in range(2)]
        self.qs = [at(f"q_sin{s}", 90 + 2 * s, [P, N]) for s in range(2)]
        self.v = at("values", 186, [P, NT, (KV + 1) * HD])
        self.ap = [at(f"att_probs{s}", 191 + 4 * s, [P, 2, N]) for s in range(2)]
        self.apt = [at(f"att_probsT{s}", 199 + 4 * s, [P, 2, N]) for s in range(2)]
        self.ao = at("att_out", 24, [P, NT, HEADS * HD])
        self.aoTh = [at(f"att_outT_hi{s}", 191 + 8 * s, [P, QT, P], F32R) for s in range(2)]
        self.aoTl = [at(f"att_outT_lo{s}", 195 + 8 * s, [P, QT, P], F32R) for s in range(2)]
        self.piece = [weight(f"piece{s}", kb, [P, 4, 512]) for s, kb in enumerate((82, 98, 114, 130, 50, 66))]
        self.sacth = at("sh_act_hi", 154, [P, IC, N], F32R)
        self.sactl = at("sh_act_lo", 170, [P, IC, N], F32R)
        self.sil = [at(f"silu{s}", 186 + 2 * s, [P, 512]) for s in range(2)]
        self.lgt = at("logits_turned", 190, [E, N])
        self.xsh = at("xs_hi", 24, [P, NT, D], F32R)
        self.xsl = at("xs_lo", 32, [P, NT, D], F32R)
        self.sel = at("select", 146, [P, NT, 4, P], F32R)
        self.xg = at("gatheredT", 154, [P, DC, E * P])
        self.selT = at("selectT", 170, [P, E, N], F32R)
        self.act = at("act", 186, [P, INNER])
        self.actTh = [at("actT_hi0", 190, [P, INNER], F32R), at("actT_hi1", 16, [P, INNER], F32R)]
        self.actTl = [at("actT_lo0", 194, [P, INNER], F32R), at("actT_lo1", 20, [P, INNER], F32R)]
        self.xgh = [at(f"gatheredT_hi{s}", 198 + 4 * s, [P, DC, P], F32R) for s in range(2)]
        self.xgl = [at(f"gatheredT_lo{s}", 200 + 4 * s, [P, DC, P], F32R) for s in range(2)]
        self.yh = at("y_hi", 24, [P, 4, D], F32R)
        self.yl = at("y_lo", 32, [P, 4, D], F32R)
        self.wg = at("over_gate", 50, [P, DC, INNER])
        self.wu = at("over_up", 66, [P, DC, INNER])
        self.wd = at("over_down", 82, [P, IC, D])
        self.osel = at("over_select", 146, [P, NT, P], F32R)
        self.oselT = at("over_selectT", 170, [P, N], F32R)
        self.oxg = at("over_gatheredT", 154, [P, DC, P])
        self.oact = at("over_act", 98, [P, INNER])
        self.oactT = at("over_actT", 102, [P, INNER])
        self.oyh = at("over_y_hi", 106, [P, D], F32R)
        self.oyl = at("over_y_lo", 108, [P, D], F32R)

    def const(self, col, n=1, rows=P):
        return self.c[0:rows, col:col + n]


class Norm:

    def __init__(self, m, sem, tag, whole, parts):
        self.m, self.whole, self.parts = m, whole, parts
        self.stats = sem(f"{tag}_stats")
        self.var = sem(f"{tag}_var")
        self.sd = sem(f"{tag}_sd")
        self.rstd = sem(f"{tag}_rstd")
        self.h = sem(f"{tag}_h")
        self.turned = sem(f"{tag}_turned")
        self.hT = sem(f"{tag}_hT")
        self.hTl = sem(f"{tag}_hT_lo") if parts else None

    def turned_tile(self, t):
        return self.m.ps[:, t, :].rearrange("p (c n) -> p c n", c=DC)

    def vector_stats(self, dve, t):
        dve.bn_stats(self.m.stats[:, t, :], self.m.x[:, t, :]).then_inc(self.stats, 1)

    def vector(self, dve):
        m = self.m
        for t in range(NT):
            dve.wait_ge(self.stats, t + 1)
            dve.bn_aggr(m.mv[:, t, :], m.stats[:, t, :]).then_inc(self.var, 1)
        dve.wait_ge(self.sd, 1)
        dve.reciprocal(m.rstd[:, :], m.sd[:, :]).then_inc(self.rstd, 1)
        dve.wait_ge(self.rstd, 1)
        for t in range(NT):
            dve.tensor_scalar(m.h[:, t, :], m.x[:, t, :], m.mv[:, t, 0:1], m.rstd[:, t:t + 1],
                              ALU.subtract, ALU.mult).then_inc(self.h, 1)
        if self.parts:
            for t in range(NT):
                dve.wait_ge(self.hT, t + 1)
                dve.tensor_tensor(m.hTl[:, :, t * P:(t + 1) * P], self.turned_tile(t),
                                  m.hTh[:, :, t * P:(t + 1) * P].bitcast(F32), ALU.subtract).then_inc(self.hTl, 1)

    def scalar(self, act):
        m = self.m
        act.wait_ge(self.var, NT)
        act.activation(m.sd[:, :], m.mv[:, :, 1], ACT.Sqrt, bias=m.const(C_EPS)).then_inc(self.sd, 1)
        for t in range(NT):
            act.wait_ge(self.turned, t + 1)
            kept = [m.hT] * self.whole + [m.hTh] * self.parts
            for dst in kept:
                last = act.activation(dst[:, :, t * P:(t + 1) * P], self.turned_tile(t), ACT.Copy)
            last.then_inc(self.hT, 1)

    def tensor(self, pe):
        m = self.m
        for t in range(NT):
            pe.wait_ge(self.h, t + 1)
            for c in range(DC):
                last = pe.transpose(m.ps[:, t, c * P:(c + 1) * P], m.h[:, t, c * P:(c + 1) * P],
                                    m.const(C_IDENT, P))
            last.then_inc(self.turned, 1)


def product(pe, out, lhs, rhs, first, last):
    pe.matmul(out, lhs[0], rhs[0], start=first, stop=False)
    pe.matmul(out, lhs[0], rhs[1], start=False, stop=False)
    return pe.matmul(out, lhs[1], rhs[0], start=False, stop=last)


def need(eng, sem, base, n):
    if not isinstance(base, int) or base + n > 0:
        eng.wait_ge(sem, base + n)


def setup(nc, m, d, sem, s):
    ln = Norm(m, sem, "ln0", True, False)
    s_consts, s_x, s_rows, s_bias = sem("consts_loaded"), sem("x_loaded"), sem("rows_loaded"), sem("bias_loaded")
    rows_turned, wT_ready, g_whole, g_hi, e1_made = (sem("rows_turned"), sem("wT_ready"), sem("g_whole_made"),
                                                     sem("g_hi_made"), sem("e1_made"))
    g_lo = sem("g_lo_made")
    s.ctx_loaded = [sem(f"ctx_loaded{k}") for k in range(2)]
    s.w23_loaded, s.w14_loaded = sem("w23_loaded"), sem("w14_loaded")
    s.bias_loaded = s_bias
    s.ctx = d["ctx"].rearrange("o (b p t) d -> (o b) p t d", p=P, t=JT)

    with nc.Block() as block:
        @block.sync
        def _(sp):
            sp.dma_start(m.x[:, :, :], d["x"].rearrange("o (t p) d -> p (o t) d", p=P)).then_inc(s_x, 16)
            sp.dma_start(m.c[:, :], d["consts"]).then_inc(s_consts, 16)
            sp.dma_start(m.rows[0:3 * DC, :], d["w_sim"].rearrange("(a p) -> a p", p=P)).then_inc(s_rows, 16)
            sp.dma_start(m.rows[R_BQ:R_BK, :], d["bq"].rearrange("(a p) -> a p", p=P)).then_inc(s_rows, 16)
            sp.dma_start(m.rows[R_BK:ROWS, :], d["bk"].rearrange("(a p) -> a p", p=P)).then_inc(s_rows, 16)
            for k in range(2):
                sp.dma_start(m.raw[k][:, :, :], s.ctx[k]).then_inc(s.ctx_loaded[k], 16)
            sp.dma_start(m.bqv[:, :], d["b_qv"].partition_broadcast(P)).then_inc(s_bias, 16)
            sp.dma_start(m.bo[:, :], d["bo"].partition_broadcast(P)).then_inc(s_bias, 16)
            sp.dma_start(m.bv[:, :], d["bv"].partition_broadcast(P)).then_inc(s_bias, 16)
            sp.dma_start(m.bsim[:, :], d["b_sim"].partition_broadcast(P)).then_inc(s_bias, 16)
            sp.dma_start(m.gw[:, :, :], d["gate_w"].rearrange("(c p) e -> p c e", p=P)).then_inc(s_bias, 16)
            wqv = d["W_qv"].rearrange("(a c p) n -> a p c n", p=P, a=4)
            for k in range(2):
                sp.dma_start(m.w23[:, k, :, :], wqv[1 + k]).then_inc(s.w23_loaded, 16)
            sp.dma_start(m.w1[:, :, :], wqv[0]).then_inc(s.w14_loaded, 16)
            sp.dma_start(m.w4[:, :, :], wqv[3]).then_inc(s.w14_loaded, 16)

        @block.tensor
        def _(pe):
            pe.wait_ge(s_consts, 16)
            pe.wait_ge(s_rows, 48)
            pe.transpose(m.ps[:, 7, 0:ROWS], m.rows[:, :], m.const(C_IDENT, ROWS, ROWS)).then_inc(rows_turned, 1)
            ln.tensor(pe)
            pe.wait_ge(ln.hT, NT)
            pe.wait_ge(wT_ready, 1)
            for t in range(NT):
                for c in range(DC):
                    last = pe.matmul(m.ps[:, 6, t:t + 1], m.hT[:, c, t * P:(t + 1) * P], m.wT[:, R_W1 + c:R_W1 + c + 1],
                                     start=c == 0, stop=c == DC - 1)
            last.then_inc(e1_made, 1)

        @block.scalar
        def _(act):
            act.wait_ge(rows_turned, 1)
            act.activation(m.wT[:, :], m.ps[:, 7, 0:ROWS], ACT.Copy).then_inc(wT_ready, 1)
            act.wait_ge(s_consts, 16)
            ln.scalar(act)

        @block.vector
        def _(dve):
            dve.memset(m.den[:, :], 0.0)
            dve.memset(m.negm[:, 1, :], FAR)
            dve.wait_ge(s_x, 16)
            for t in range(NT):
                ln.vector_stats(dve, t)
            ln.vector(dve)
            dve.wait_ge(wT_ready, 1)
            dve.wait_ge(ln.hT, NT)
            for c in range(DC):
                dve.tensor_scalar(m.g[:, c, :], m.hT[:, c, :], m.wT[:, R_W3 + c:R_W3 + c + 1],
                                  m.wT[:, R_W2 + c:R_W2 + c + 1], ALU.mult, ALU.add).then_inc(g_whole, 1)
            for c in range(DC):
                dve.wait_ge(g_whole, c + 1)
                dve.tensor_copy(m.gh[:, c, :], m.g[:, c, :]).then_inc(g_hi, 1)
            for c in range(DC):
                dve.wait_ge(g_hi, c + 1)
                dve.tensor_tensor(m.gl[:, c, :], m.g[:, c, :], m.gh[:, c, :].bitcast(F32), ALU.subtract).then_inc(g_lo, 1)
            dve.wait_ge(e1_made, 1)
            dve.tensor_copy(m.e1[:, :], m.ps[:, 6, 0:NT])
            dve.wait_ge(g_lo, DC)
            dve.memset(m.o[:, :, :], 0.0)


def cross_attention(nc, m, sem, s):
    ct_turned, ct_hi, ct_lo = sem("ctxT_turned"), sem("ctxT_hi_made"), sem("ctxT_lo_made")
    n_hi, n_lo = sem("ctx_hi_made"), sem("ctx_lo_made")
    scored, maxed, negm_made = sem("scored"), sem("block_maxed"), sem("negm_made")
    alpha_made, exp_made = sem("alpha_made"), sem("exp_made")
    pt_turned, pt_hi, pt_lo = sem("probsT_turned"), sem("probsT_hi_made"), sem("probsT_lo_made")
    attended, den_made, merged = sem("attended_made"), sem("den_made"), sem("merged")
    w23_hi = sem("w23_hi_made")
    S_BANK, PT_BANK, CT_BANK, O_BANK = 0, 2, 4, 6
    AHEAD_S, AHEAD_CT, AHEAD_N = 2, 6, 4
    ps = m.ps
    ident = m.const(C_IDENT, P)
    loops = UNITS // STEP

    def loaded(eng, base, n):
        slot, use = n // JT % 2, n // JT // 2 + 1
        eng.wait_ge(s.ctx_loaded[slot], base * 2 + 16 * use)

    def turns(eng, unit, prologue):
        prologue()
        for k in range(STEP):
            unit(0, k, False)
        with eng.Fori(STEP, UNITS - STEP, STEP) as base:
            for k in range(STEP):
                unit(base, k, False)
        for k in range(STEP):
            unit(UNITS - STEP, k, True)

    with nc.Block() as block:
        @block.sync
        def _(sp):
            def load(base, block_index, slot, k):
                need(sp, ct_turned, base, JT * (k + 1))
                need(sp, n_lo, base, JT * (k + 1))
                sp.dma_start(m.raw[slot][:, :, :], s.ctx[block_index]).then_inc(s.ctx_loaded[slot], 16)

            for k in range(2):
                load(0, 2 + k, k, k)
            with sp.Fori(1, loops - 1) as turn:
                for k in range(2):
                    load(turn * STEP, turn * 2 + 2 + k, k, k)

        @block.gpsimd
        def _(pool):
            zeros = m.const(C_ZERO).to_broadcast([P, D])

            def split(base, n):
                slot = n // JT % 2
                loaded(pool, base, n)
                need(pool, attended, base, n // JT * JT - JT)
                raw, hi, lo = m.raw[slot][:, n % JT, :], m.nh[slot][:, n % JT, :], m.nl[slot][:, n % JT, :]
                pool.tensor_tensor(hi, raw, zeros, ALU.add).then_inc(n_hi, 1)
                need(pool, n_hi, base, n + 1)
                pool.tensor_tensor(lo, raw, hi.bitcast(F32), ALU.subtract).then_inc(n_lo, 1)

            def split_weights(part, c):
                raw, hi, lo = m.w23[:, part, c, :], m.w23h[:, part, c, :], m.w23l[:, part, c, :]
                n = part * DC + c
                pool.tensor_tensor(hi, raw, zeros, ALU.add).then_inc(w23_hi, 1)
                pool.wait_ge(w23_hi, n + 1)
                pool.tensor_tensor(lo, raw, hi.bitcast(F32), ALU.subtract)

            def unit(base, k, last):
                if not last or k + AHEAD_N < STEP:
                    split(base, k + AHEAD_N)
                if last:
                    if k == 0:
                        pool.wait_ge(s.w23_loaded, 32)
                    split_weights(k // DC, k % DC)

            def prologue():
                for n in range(AHEAD_N):
                    split(0, n)

            turns(pool, unit, prologue)

        @block.tensor
        def _(pe):
            def turn_ctx(base, n):
                slot, bank = n // JT % 2, CT_BANK + n % 2
                loaded(pe, base, n)
                need(pe, ct_lo, base, n - 1)
                for c in range(DC):
                    last = pe.transpose(ps[:, bank, c * P:(c + 1) * P], m.raw[slot][:, n % JT, c * P:(c + 1) * P], ident)
                last.then_inc(ct_turned, 1)

            def score(base, v):
                slot, i, bank = v // NT % 2, v % NT, S_BANK + v % 2
                need(pe, ct_lo, base, v // NT * JT + JT)
                need(pe, exp_made, base, v - 1)
                tok = slice(i * P, (i + 1) * P)
                for c in range(DC):
                    pe.matmul(ps[:, bank, :], m.gh[:, c, tok], m.th[slot][:, c, :], start=c == 0, stop=False)
                    pe.matmul(ps[:, bank, :], m.gh[:, c, tok], m.tl[slot][:, c, :], start=False, stop=False)
                    last = pe.matmul(ps[:, bank, :], m.gl[:, c, tok], m.th[slot][:, c, :], start=False, stop=c == DC - 1)
                last.then_inc(scored, 1)

            def turn_probs(base, u):
                need(pe, exp_made, base, u + 1)
                need(pe, pt_lo, base, u - 1)
                for j in range(JT):
                    last = pe.transpose(ps[:, PT_BANK + u % 2, j * P:(j + 1) * P], m.p[u % 2][:, j * P:(j + 1) * P], ident)
                last.then_inc(pt_turned, 1)

            def attend(base, u):
                slot, bank, b = u // NT % 2, O_BANK + u % 2, u % 2
                need(pe, pt_lo, base, u + 1)
                need(pe, n_lo, base, u // NT * JT + JT)
                need(pe, merged, base, u - 1)
                for j in range(JT):
                    col = slice(j * P, (j + 1) * P)
                    pe.matmul(ps[:, bank, :], m.pth[b][:, col], m.nh[slot][:, j, :], start=j == 0, stop=False)
                    pe.matmul(ps[:, bank, :], m.pth[b][:, col], m.nl[slot][:, j, :], start=False, stop=False)
                    last = pe.matmul(ps[:, bank, :], m.ptl[b][:, col], m.nh[slot][:, j, :], start=False, stop=j == JT - 1)
                last.then_inc(attended, 1)

            def unit(base, k, last):
                turn_probs(base, k)
                if not last or k + AHEAD_CT < STEP:
                    turn_ctx(base, k + AHEAD_CT)
                if not last or k + AHEAD_S < STEP:
                    score(base, k + AHEAD_S)
                attend(base, k)

            def prologue():
                for n in range(AHEAD_CT):
                    turn_ctx(0, n)
                    if n == JT:
                        score(0, 0)
                score(0, 1)

            turns(pe, unit, prologue)

        @block.scalar
        def _(act):
            def ctx_hi(base, n):
                need(act, ct_turned, base, n + 1)
                need(act, scored, base, n // JT * NT - NT)
                act.activation(m.th[n // JT % 2][:, :, n % JT * P:(n % JT + 1) * P],
                               ps[:, CT_BANK + n % 2, :].rearrange("p (c n) -> p c n", c=DC),
                               ACT.Copy).then_inc(ct_hi, 1)

            def exps(base, v):
                i, new, b = v % NT, v // NT % 2, v % STEP
                need(act, negm_made, base, v + 1)
                act.activation(m.alpha[:, b:b + 1], m.negm[:, 1 - new, i:i + 1], ACT.Exp, scale=-1.0,
                               bias=m.negm[:, new, i:i + 1]).then_inc(alpha_made, 1)
                need(act, pt_turned, base, v - 1)
                act.activation(m.p[v % 2][:, :], ps[:, S_BANK + v % 2, :], ACT.Exp, bias=m.negm[:, new, i:i + 1],
                               accum_out=m.rowsum[:, b:b + 1]).then_inc(exp_made, 1)

            def probs_hi(base, u):
                need(act, pt_turned, base, u + 1)
                need(act, attended, base, u - 1)
                act.activation(m.pth[u % 2][:, :], ps[:, PT_BANK + u % 2, :], ACT.Copy).then_inc(pt_hi, 1)

            def unit(base, k, last):
                probs_hi(base, k)
                if not last or k + AHEAD_CT < STEP:
                    ctx_hi(base, k + AHEAD_CT)
                if not last or k + AHEAD_S < STEP:
                    exps(base, k + AHEAD_S)

            def prologue():
                for n in range(AHEAD_CT):
                    ctx_hi(0, n)
                exps(0, 0)
                exps(0, 1)

            turns(act, unit, prologue)

        @block.vector
        def _(dve):
            def ctx_lo(base, n):
                slot, col = n // JT % 2, slice(n % JT * P, (n % JT + 1) * P)
                need(dve, ct_hi, base, n + 1)
                dve.tensor_tensor(m.tl[slot][:, :, col], ps[:, CT_BANK + n % 2, :].rearrange("p (c n) -> p c n", c=DC),
                                  m.th[slot][:, :, col].bitcast(F32), ALU.subtract).then_inc(ct_lo, 1)

            def maxes(base, v):
                i, new, b = v % NT, v // NT % 2, v % STEP
                need(dve, scored, base, v + 1)
                dve.tensor_reduce(m.mx[:, b:b + 1], ps[:, S_BANK + v % 2, :], AX, ALU.max).then_inc(maxed, 1)
                need(dve, maxed, base, v + 1)
                dve.scalar_tensor_tensor(m.negm[:, new, i:i + 1], m.mx[:, b:b + 1], -1.0, m.negm[:, 1 - new, i:i + 1],
                                         ALU.mult, ALU.min).then_inc(negm_made, 1)

            def probs_lo(base, u):
                need(dve, pt_hi, base, u + 1)
                dve.tensor_tensor(m.ptl[u % 2][:, :], ps[:, PT_BANK + u % 2, :], m.pth[u % 2][:, :].bitcast(F32),
                                  ALU.subtract).then_inc(pt_lo, 1)

            def merge(base, u):
                i, b = u % NT, u % STEP
                need(dve, attended, base, u + 1)
                need(dve, exp_made, base, u + 1)
                need(dve, merged, base, u - NT + 1)
                dve.scalar_tensor_tensor(m.o[:, i, :], m.o[:, i, :], m.alpha[:, b:b + 1], ps[:, O_BANK + u % 2, :],
                                         ALU.mult, ALU.add).then_inc(merged, 1)
                need(dve, den_made, base, u - NT + 1)
                dve.scalar_tensor_tensor(m.den[:, i:i + 1], m.den[:, i:i + 1], m.alpha[:, b:b + 1],
                                         m.rowsum[:, b:b + 1], ALU.mult, ALU.add).then_inc(den_made, 1)

            def unit(base, k, last):
                probs_lo(base, k)
                if not isinstance(base, int) or base + k > 0:
                    merge(base, k - 1) if k else merge(base, -1)
                if not last or k + AHEAD_CT < STEP:
                    ctx_lo(base, k + AHEAD_CT)
                if not last or k + AHEAD_S < STEP:
                    maxes(base, k + AHEAD_S)

            def prologue():
                for n in range(AHEAD_CT):
                    ctx_lo(0, n)
                    if n == JT:
                        maxes(0, 0)
                maxes(0, 1)

            turns(dve, unit, prologue)
            merge(UNITS - STEP, STEP - 1)


def cross_output(nc, m, d, sem, s):
    ln = Norm(m, sem, "ln1", False, True)
    mcol0, mcol, mrow, rmax, rexp, rinv, brow, bcol_ps, bcol, hc_ps, hc = (sem(x) for x in (
        "mcol_sum", "mcol_made", "mrow_turned", "row_max", "row_exp", "row_inv", "batt_row", "batt_turned",
        "batt_col_made", "hc_summed", "hc_made"))
    rden, hq, hq_turned, xb, fed, x1 = (sem(x) for x in (
        "rden_made", "hq_made", "hq_turned", "x_biased", "fed", "x1_made"))
    enc_hi, enc_lo, hqT_hi, hqT_lo, eh_whole, eh_hi, eh_lo, w14, w14_hi, w14_lo = (sem(x) for x in (
        "encT_hi_made", "encT_lo_made", "hqT_hi_made", "hqT_lo_made", "ehT_made", "ehT_hi_made", "ehT_lo_made",
        "w14_made", "w14_hi_made", "w14_lo_made"))
    wkv_loaded, wq_loaded, wkv_hi, wq_hi = (sem(x) for x in ("wkv_loaded", "wq_loaded", "wkv_hi_made", "wq_hi_made"))
    ROW_BANK = 4
    ps = m.ps
    out_bank = [5, 6, 7, 0]
    encT, hqT, ehT = (m.hTh, m.hTl), (m.hqTh, m.hqTl), (m.ehTh, m.ehTl)

    def turned_tile(t):
        return ps[:, t, :].rearrange("p (c n) -> p c n", c=DC)

    with nc.Block() as block:
        @block.sync
        def _(sp):
            sp.dma_start(m.wkv[:, 0, :, :], d["Wk"].rearrange("(c p) n -> p c n", p=P)).then_inc(wkv_loaded, 16)
            sp.dma_start(m.wkv[:, 1, :, :], d["Wv"].rearrange("(c p) n -> p c n", p=P)).then_inc(wkv_loaded, 16)
            sp.dma_start(m.wq[:, :, :], d["Wq"].rearrange("(c p) n -> p c n", p=P)).then_inc(wq_loaded, 16)

        @block.tensor
        def _(pe):
            pe.wait_ge(mcol, 1)
            for t in range(NT):
                last = pe.matmul(ps[0:1, ROW_BANK, t * P:(t + 1) * P], m.mcol[:, t:t + 1], m.const(C_IDENT, P),
                                 start=True, stop=True)
            last.then_inc(mrow, 1)
            for t in range(NT):
                pe.wait_ge(hq, t + 1)
                for c in range(DC):
                    last = pe.transpose(ps[:, t, c * P:(c + 1) * P], m.o[:, t, c * P:(c + 1) * P], m.const(C_IDENT, P))
                last.then_inc(hq_turned, 1)

            def feed(t, lhs, rhs, start, stop):
                tok = slice(t * P, (t + 1) * P)
                for c in range(DC):
                    last = product(pe, ps[:, out_bank[t], :], (lhs[0][:, c, tok], lhs[1][:, c, tok]),
                                   (rhs[0][:, c, :], rhs[1][:, c, :]), start and c == 0, stop and c == DC - 1)
                return last

            for t in range(NT):
                pe.wait_ge(hqT_hi, t + 1)
                pe.wait_ge(hqT_lo, t + 1)
                if t == NT - 1:
                    pe.wait_ge(eh_whole, 1)
                feed(t, hqT, (m.w23h[:, 0, :, :], m.w23l[:, 0, :, :]), True, False)
            for t in range(NT):
                pe.wait_ge(eh_hi, t + 1)
                pe.wait_ge(eh_lo, t + 1)
                feed(t, ehT, (m.w23h[:, 1, :, :], m.w23l[:, 1, :, :]), False, False)
                if t == 0:
                    pe.wait_ge(brow, 1)
                    for q in range(NT):
                        last = pe.matmul(ps[:, ROW_BANK, q:q + 1], m.mrow[0:1, q * P:(q + 1) * P],
                                         m.const(C_ONES, 1, 1), start=True, stop=True)
                    last.then_inc(bcol_ps, 1)
                if t == 1:
                    pe.wait_ge(bcol, 1)
                    for c in range(DC):
                        for q in range(NT):
                            last = pe.matmul(ps[:, ROW_BANK, 8 + c:9 + c], m.h[:, q, c * P:(c + 1) * P],
                                             m.batt[:, q:q + 1], start=q == 0, stop=q == NT - 1)
                    last.then_inc(hc_ps, 1)
            pe.wait_ge(enc_hi, NT)
            pe.wait_ge(enc_lo, NT)
            pe.wait_ge(w14_hi, DC)
            pe.wait_ge(w14_lo, DC)
            for t in range(NT):
                feed(t, encT, (m.w1h, m.w1l), False, True).then_inc(fed, 1)
            ln.tensor(pe)

        @block.scalar
        def _(act):
            for c in range(DC):
                act.activation(m.hTh[:, c, :], m.hT[:, c, :], ACT.Copy).then_inc(enc_hi, 1)
            for t in range(NT):
                act.wait_ge(hq_turned, t + 1)
                act.activation(m.hqTh[:, :, t * P:(t + 1) * P], turned_tile(t), ACT.Copy).then_inc(hqT_hi, 1)
            act.wait_ge(rmax, 2)
            act.activation(m.mrow[:, :], ps[0:1, ROW_BANK, :], ACT.Exp, bias=m.r1[:, 1:2],
                           accum_out=m.r1[:, 2:3]).then_inc(rexp, 1)
            for t in range(NT):
                act.wait_ge(eh_whole, t + 1)
                act.activation(m.ehTh[:, :, t * P:(t + 1) * P], m.ehT[:, :, t * P:(t + 1) * P], ACT.Copy).then_inc(eh_hi, 1)
            act.wait_ge(wkv_loaded, 32)
            for k in range(2):
                act.activation(m.wkvh[:, k, :, :], m.wkv[:, k, :, :], ACT.Copy).then_inc(wkv_hi, 1)
            for c in range(DC):
                act.wait_ge(w14, c + 1)
                act.activation(m.w1h[:, c, :], m.w1[:, c, :], ACT.Copy).then_inc(w14_hi, 1)
            act.wait_ge(wq_loaded, 16)
            for c in range(DC):
                act.activation(m.wqh[:, c, :], m.wq[:, c, :], ACT.Copy).then_inc(wq_hi, 1)
            ln.scalar(act)

        @block.gpsimd
        def _(pool):
            for c in range(DC):
                pool.wait_ge(enc_hi, c + 1)
                pool.tensor_tensor(m.hTl[:, c, :], m.hT[:, c, :], m.hTh[:, c, :].bitcast(F32), ALU.subtract).then_inc(enc_lo, 1)
            pool.wait_ge(s.bias_loaded, 80)
            for t in range(NT):
                pool.tensor_tensor(m.x[:, t, :], m.x[:, t, :], m.bqv[:, :], ALU.add).then_inc(xb, 1)
            for k in range(2):
                pool.wait_ge(wkv_hi, k + 1)
                pool.tensor_tensor(m.wkvl[:, k, :, :], m.wkv[:, k, :, :], m.wkvh[:, k, :, :].bitcast(F32), ALU.subtract)
            for c in range(DC):
                pool.wait_ge(wq_hi, c + 1)
                pool.tensor_tensor(m.wql[:, c, :], m.wq[:, c, :], m.wqh[:, c, :].bitcast(F32), ALU.subtract)

        @block.vector
        def _(dve):
            dve.scalar_tensor_tensor(m.mcol[:, :], m.negm[:, 1, :], -1.0, m.e1[:, :], ALU.mult, ALU.add).then_inc(mcol0, 1)
            dve.reciprocal(m.rden[:, :], m.den[:, :]).then_inc(rden, 1)
            dve.wait_ge(mcol0, 1)
            dve.wait_ge(s.bias_loaded, 80)
            dve.tensor_scalar(m.mcol[:, :], m.mcol[:, :], m.bsim[:, 0:1], None, ALU.add).then_inc(mcol, 1)
            dve.wait_ge(rden, 1)
            for t in range(NT):
                dve.tensor_scalar(m.o[:, t, :], m.o[:, t, :], m.rden[:, t:t + 1], None, ALU.mult).then_inc(hq, 1)
            dve.wait_ge(mrow, 1)
            dve.tensor_reduce(m.r1[:, 0:1], ps[0:1, ROW_BANK, :], AX, ALU.max).then_inc(rmax, 1)
            dve.wait_ge(rmax, 1)
            dve.tensor_scalar(m.r1[:, 1:2], m.r1[:, 0:1], -1.0, None, ALU.mult).then_inc(rmax, 1)
            for t in range(NT):
                tok = slice(t * P, (t + 1) * P)
                dve.wait_ge(hqT_hi, t + 1)
                dve.tensor_tensor(m.hqTl[:, :, tok], turned_tile(t), m.hqTh[:, :, tok].bitcast(F32), ALU.subtract).then_inc(hqT_lo, 1)
            dve.wait_ge(rexp, 1)
            dve.reciprocal(m.r1[:, 3:4], m.r1[:, 2:3]).then_inc(rinv, 1)
            dve.wait_ge(rinv, 1)
            dve.tensor_scalar(m.mrow[:, :], m.mrow[:, :], m.r1[:, 3:4], None, ALU.mult).then_inc(brow, 1)
            for t in range(NT):
                tok = slice(t * P, (t + 1) * P)
                dve.tensor_tensor(m.ehT[:, :, tok], m.hT[:, :, tok], turned_tile(t), ALU.mult).then_inc(eh_whole, 1)
            for t in range(NT):
                tok = slice(t * P, (t + 1) * P)
                dve.wait_ge(eh_hi, t + 1)
                dve.tensor_tensor(m.ehTl[:, :, tok], m.ehT[:, :, tok], m.ehTh[:, :, tok].bitcast(F32), ALU.subtract).then_inc(eh_lo, 1)
            dve.wait_ge(bcol_ps, 1)
            dve.tensor_copy(m.batt[:, :], ps[:, ROW_BANK, 0:NT]).then_inc(bcol, 1)
            dve.wait_ge(hc_ps, 1)
            dve.tensor_copy(m.hc[:, :], ps[:, ROW_BANK, 8:8 + DC]).then_inc(hc, 1)
            dve.wait_ge(hc, 1)
            dve.wait_ge(s.w14_loaded, 32)
            for c in range(DC):
                dve.scalar_tensor_tensor(m.w1[:, c, :], m.w4[:, c, :], m.hc[:, c:c + 1], m.w1[:, c, :],
                                         ALU.mult, ALU.add).then_inc(w14, 1)
            for c in range(DC):
                dve.wait_ge(w14_hi, c + 1)
                dve.tensor_tensor(m.w1l[:, c, :], m.w1[:, c, :], m.w1h[:, c, :].bitcast(F32), ALU.subtract).then_inc(w14_lo, 1)
            for t in range(NT):
                dve.wait_ge(fed, t + 1)
                dve.wait_ge(xb, t + 1)
                dve.tensor_tensor(m.x[:, t, :], m.x[:, t, :], ps[:, out_bank[t], :], ALU.add).then_inc(x1, 1)
                dve.wait_ge(x1, t + 1)
                ln.vector_stats(dve, t)
            ln.vector(dve)


class Pieces:
    SLOTS = 6
    SHARED = -1

    def __init__(self, m, d, sem):
        self.m, self.d = m, d
        self.order = [(self.SHARED, name, half) for name, half in (
            ("gate", 0), ("up", 0), ("gate", 1), ("up", 1), ("down", 0), ("down", 1))]
        for e in range(E):
            self.order += [(e, "gate", 0), (e, "up", 0), (e, "gate", 1), (e, "up", 1)]
            if e:
                self.order += [(e - 1, "down", 0), (e - 1, "down", 1)]
        self.order += [(E - 1, "down", 0), (E - 1, "down", 1)]
        self.loaded = [sem(f"piece_loaded{k}") for k in range(self.SLOTS)]
        self.hi_made = [sem(f"piece_hi_made{k}") for k in range(self.SLOTS)]
        self.lo_made = [sem(f"piece_lo_made{k}") for k in range(self.SLOTS)]

    def number(self, e, name, half):
        return self.order.index((e, name, half))

    def load(self, sp, n):
        e, name, half = self.order[n]
        w = self.d["sh_" + name] if e == self.SHARED else self.d["rt_" + name][e]
        if name == "down":
            w = w[half * 4 * P:(half + 1) * 4 * P, :].rearrange("(c p) n -> p c n", p=P)
        else:
            w = w[:, half * 512:(half + 1) * 512].rearrange("(c p) n -> p c n", p=P)
        sp.dma_start(self.m.piece[n % self.SLOTS][0][:, :, :], w).then_inc(self.loaded[n % self.SLOTS], 16)

    def raw_loaded(self, eng, n):
        eng.wait_ge(self.loaded[n % self.SLOTS], 16 * (n // self.SLOTS + 1))
        return self.m.piece[n % self.SLOTS][0], self.m.piece[n % self.SLOTS][1]

    def scalar_hi(self, act, n):
        raw, hi = self.raw_loaded(act, n)
        act.activation(hi[:, :, :], raw[:, :, :], ACT.Copy).then_inc(self.hi_made[n % self.SLOTS], 4)

    def vector_hi(self, dve, n):
        raw, hi = self.raw_loaded(dve, n)
        dve.tensor_copy(hi[:, :, :], raw[:, :, :]).then_inc(self.hi_made[n % self.SLOTS], 4)

    def pool_hi(self, pool, n, zeros):
        raw, hi = self.raw_loaded(pool, n)
        for c in range(4):
            pool.tensor_tensor(hi[:, c, :], raw[:, c, :], zeros, ALU.add).then_inc(self.hi_made[n % self.SLOTS], 1)

    def lo(self, eng, n):
        raw, hi, lo = self.m.piece[n % self.SLOTS]
        eng.wait_ge(self.hi_made[n % self.SLOTS], 4 * (n // self.SLOTS + 1))
        eng.tensor_tensor(lo[:, :, :], raw[:, :, :], hi[:, :, :].bitcast(F32),
                          ALU.subtract).then_inc(self.lo_made[n % self.SLOTS], 1)

    def wait(self, pe, n):
        raw, hi, lo = self.m.piece[n % self.SLOTS]
        pe.wait_ge(self.lo_made[n % self.SLOTS], n // self.SLOTS + 1)
        return hi, lo


def self_attention(nc, m, d, sem, s):
    ln = Norm(m, sem, "ln2", True, True)
    projected, biased, rotated, cosed, sined, summed, q_hi, k_hi, split_done = (sem(x) for x in (
        "projected", "q_biased_made", "q_rotated", "q_cosed", "q_sined", "rotary_made", "q_hi_made", "k_hi_made",
        "qk_lo_made"))
    v_ps, v_made, v_pad = sem("v_projected"), sem("v_made"), sem("v_padded")
    scored, masked, maxed, bias_made, exped = (sem(x) for x in (
        "att_scored", "att_masked", "att_maxed", "att_bias_made", "att_exp_made"))
    turned, pt0, pt1, valued, inv, out_made = (sem(x) for x in (
        "att_turned", "att_pt0_made", "att_pt1_made", "att_valued", "att_inv_made", "att_out_made"))
    o_turned, oT_hi, oT_lo, wo_done, xb, x2 = (sem(x) for x in (
        "out_turned", "outT_hi_made", "outT_lo_made", "wo_done", "x1_biased", "x2_made"))
    wo_loaded, wo_hi, wo_lo = sem("wo_loaded"), sem("wo_hi_made"), sem("wo_lo_made")
    ps = m.ps
    ident = m.const(C_IDENT, P)
    PAIRS = HEADS // 2
    AU = NT * PAIRS
    tiles = [("k", c) for c in range(KV * HD // P)] + [("q", c) for c in range(QT)]
    pieces = s.pieces = Pieces(m, d, sem)

    def out_turned():
        return ps[:, 4:6, :].rearrange("p a (c n) -> p (a c) n", c=4)

    with nc.Block() as block:
        @block.sync
        def _(sp):
            sp.dma_start(m.wo[:, :, :], d["Wo"].rearrange("(c p) n -> p c n", p=P)).then_inc(wo_loaded, 16)
            sp.wait_ge(projected, len(tiles))
            sp.wait_ge(v_ps, NT)
            for n in (1, 2, 3):
                pieces.load(sp, n)
            sp.wait_ge(split_done, len(tiles))
            pieces.load(sp, 0)
            sp.wait_ge(scored, AU)
            for n in (4, 5):
                pieces.load(sp, n)

        @block.gpsimd
        def _(pool):
            zeros = m.const(C_ZERO).to_broadcast([P, D])
            pool.wait_ge(wo_loaded, 16)
            for c in range(QT):
                pool.tensor_tensor(m.woh[:, c, :], m.wo[:, c, :], zeros, ALU.add).then_inc(wo_hi, 1)
            for c in range(QT):
                pool.wait_ge(wo_hi, c + 1)
                pool.tensor_tensor(m.wol[:, c, :], m.wo[:, c, :], m.woh[:, c, :].bitcast(F32), ALU.subtract).then_inc(wo_lo, 1)
            for n in (1, 2, 3, 0, 4, 5):
                pieces.pool_hi(pool, n, zeros)
                pieces.lo(pool, n)

        @block.tensor
        def _(pe):
            def rotate(j):
                pe.wait_ge(biased, j + 1)
                if j >= 2:
                    pe.wait_ge(sined, j - 1)
                pe.matmul(ps[:, 2 + j % 2, :], m.const(C_ROT, P), m.qb[j % 2][:, :], start=True, stop=True).then_inc(rotated, 1)

            for j, (kind, c) in enumerate(tiles):
                hi, lo = (m.wkvh[:, 0, :, :], m.wkvl[:, 0, :, :]) if kind == "k" else (m.wqh, m.wql)
                if j >= 2:
                    pe.wait_ge(biased, j - 1)
                for dc in range(DC):
                    last = product(pe, ps[:, j % 2, :], (hi[:, dc, c * P:(c + 1) * P], lo[:, dc, c * P:(c + 1) * P]),
                                   (m.hTh[:, dc, :], m.hTl[:, dc, :]), dc == 0, dc == DC - 1)
                last.then_inc(projected, 1)
                if j:
                    rotate(j - 1)
                if 1 <= j <= NT:
                    t = j - 1
                    for dc in range(DC):
                        tok = slice(t * P, (t + 1) * P)
                        last = product(pe, ps[:, 4 + t, 0:KV * HD], (m.hTh[:, dc, tok], m.hTl[:, dc, tok]),
                                       (m.wkvh[:, 1, dc, :], m.wkvl[:, 1, dc, :]), dc == 0, dc == DC - 1)
                    last.then_inc(v_ps, 1)
            rotate(len(tiles) - 1)

            def score(u):
                t, pair = u // PAIRS, u % PAIRS
                if u >= 2:
                    pe.wait_ge(exped, 2 * (u - 1))
                for i in range(2):
                    head = 2 * pair + i
                    g, bank = head // (HEADS // KV), u % 2 * 2 + i
                    q, w = m.q2[:, head, t * P:(t + 1) * P], (t + 1) * P
                    pe.matmul(ps[:, bank, 0:w], q, m.k2h[:, g, 0:w], start=True, stop=False)
                    last = pe.matmul(ps[:, bank, 0:w], q, m.k2l[:, g, 0:w], start=False, stop=True)
                last.then_inc(scored, 1)

            def turn(u):
                t = u // PAIRS
                pe.wait_ge(exped, 2 * (u + 1))
                if u >= 1:
                    pe.wait_ge(pt0, u)
                    pe.wait_ge(pt1, u)
                for i in range(2):
                    for k in range(t + 1):
                        last = pe.transpose(ps[:, 4 + i, k * P:(k + 1) * P], m.ap[u % 2][:, i, k * P:(k + 1) * P], ident)
                last.then_inc(turned, 1)

            def value(u):
                t, pair = u // PAIRS, u % PAIRS
                pe.wait_ge(pt0, u + 1)
                pe.wait_ge(pt1, u + 1)
                if u >= 2:
                    pe.wait_ge(out_made, u - 1)
                for i in range(2):
                    g = (2 * pair + i) // (HEADS // KV)
                    for k in range(t + 1):
                        last = pe.matmul(ps[:, 6 + u % 2, i * P:(i + 1) * P], m.apt[u % 2][:, i, k * P:(k + 1) * P],
                                         m.v[:, k, g * HD:g * HD + P], start=k == 0, stop=k == t)
                last.then_inc(valued, 1)

            pe.wait_ge(split_done, len(tiles))
            pe.wait_ge(v_made, NT)
            pe.wait_ge(v_pad, 1)
            score(0)
            score(1)
            for u in range(AU):
                turn(u)
                if u + 2 < AU:
                    score(u + 2)
                if u >= 1:
                    value(u - 1)
            value(AU - 1)
            pe.wait_ge(wo_lo, QT)

            def turn_out(t):
                pe.wait_ge(out_made, PAIRS * (t + 1))
                pe.wait_ge(out_made, AU)
                if t >= 1:
                    pe.wait_ge(oT_lo, t)
                for c in range(QT):
                    last = pe.transpose(ps[:, 4 + c // 4, c % 4 * P:(c % 4 + 1) * P], m.ao[:, t, c * P:(c + 1) * P], ident)
                last.then_inc(o_turned, 1)

            turn_out(0)
            for t in range(NT):
                pe.wait_ge(oT_lo, t + 1)
                if t + 1 < NT:
                    turn_out(t + 1)
                for c in range(QT):
                    last = product(pe, ps[:, t, :], (m.aoTh[t % 2][:, c, :], m.aoTl[t % 2][:, c, :]),
                                   (m.woh[:, c, :], m.wol[:, c, :]), c == 0, c == QT - 1)
                last.then_inc(wo_done, 1)
            pe.wait_ge(x2, NT)
            ln.tensor(pe)

        @block.scalar
        def _(act):
            def bias(j):
                kind, c = tiles[j]
                col = (R_BK if kind == "k" else R_BQ) + c
                act.wait_ge(projected, j + 1)
                if j >= 2:
                    act.wait_ge(rotated, j - 1)
                    act.wait_ge(cosed, j - 1)
                act.activation(m.qb[j % 2][:, :], ps[:, j % 2, :], ACT.Identity, bias=m.wT[:, col:col + 1]).then_inc(biased, 1)

            def split_hi(j):
                kind, c = tiles[j]
                act.wait_ge(summed, j + 1)
                src = m.qc[j % 2]
                for i in range(2):
                    own = slice(i * HD, (i + 1) * HD)
                    other = slice((1 - i) * HD, (2 - i) * HD)
                    if kind == "q":
                        act.activation(m.q2[own, 2 * c + i, :], src[own, :], ACT.Copy).then_inc(q_hi, 1)
                    else:
                        act.activation(m.k2h[own, 2 * c + i, :], src[own, :], ACT.Copy).then_inc(k_hi, 1)
                        act.activation(m.k2h[other, 2 * c + i, :], src[own, :], ACT.Copy).then_inc(k_hi, 1)

            for j in range(len(tiles)):
                bias(j)
                if j:
                    split_hi(j - 1)
            split_hi(len(tiles) - 1)

            def exps(u):
                t = u // PAIRS
                act.wait_ge(bias_made, u + 1)
                if u >= 2:
                    act.wait_ge(turned, u - 1)
                    act.wait_ge(inv, u // 4 * 4 - 4 + 1 + u % 4 if u >= 4 else 1)
                for i in range(2):
                    w = (t + 1) * P
                    act.activation(m.ap[u % 2][:, i, 0:w], ps[:, u % 2 * 2 + i, 0:w], ACT.Exp, scale=ATT_SCALE,
                                   bias=m.anb[:, u % 4, i:i + 1],
                                   accum_out=m.ars[:, u % 4, i:i + 1]).then_inc(exped, 1)

            def move0(u):
                w = (u // PAIRS + 1) * P
                act.wait_ge(turned, u + 1)
                if u >= 2:
                    act.wait_ge(valued, u - 1)
                act.activation(m.apt[u % 2][:, 0, 0:w], ps[:, 4, 0:w], ACT.Copy).then_inc(pt0, 1)

            exps(0)
            exps(1)
            for u in range(AU):
                move0(u)
                if u + 2 < AU:
                    exps(u + 2)
            for t in range(NT):
                act.wait_ge(o_turned, t + 1)
                if t >= 2:
                    act.wait_ge(wo_done, t - 1)
                act.activation(m.aoTh[t % 2][:, :, :], out_turned(), ACT.Copy).then_inc(oT_hi, 1)
            ln.scalar(act)

        @block.vector
        def _(dve):
            dve.memset(m.v[:, :, KV * HD:], 0.0).then_inc(v_pad, 1)

            def rotary(j):
                b = j % 2
                dve.wait_ge(biased, j + 1)
                if j >= 2:
                    dve.wait_ge(split_done, j - 1)
                    dve.wait_ge(q_hi if tiles[j - 2][0] == "q" else k_hi, 2 * (j - 3) if tiles[j - 2][0] == "q" else 4 * (j - 1))
                dve.tensor_tensor(m.qc[b][:, :], m.qb[b][:, :], m.const(C_COS, N), ALU.mult).then_inc(cosed, 1)
                dve.wait_ge(rotated, j + 1)
                dve.tensor_tensor(m.qs[b][:, :], ps[:, 2 + b, :], m.const(C_SIN, N), ALU.mult).then_inc(sined, 1)
                dve.wait_ge(cosed, j + 1)
                dve.wait_ge(sined, j + 1)
                dve.tensor_tensor(m.qc[b][:, :], m.qc[b][:, :], m.qs[b][:, :], ALU.add).then_inc(summed, 1)

            def split_lo(j):
                kind, c = tiles[j]
                src = m.qc[j % 2]
                dve.wait_ge(summed, j + 1)
                for i in range(2):
                    own = slice(i * HD, (i + 1) * HD)
                    other = slice((1 - i) * HD, (2 - i) * HD)
                    if kind == "q":
                        dve.wait_ge(q_hi, 2 * (j - 2) + i + 1)
                        last = dve.tensor_tensor(m.q2[other, 2 * c + i, :], src[own, :],
                                                 m.q2[own, 2 * c + i, :].bitcast(F32), ALU.subtract)
                    else:
                        dve.wait_ge(k_hi, 4 * j + 2 * i + 2)
                        hi = m.k2h[own, 2 * c + i, :].bitcast(F32)
                        dve.tensor_tensor(m.k2l[own, 2 * c + i, :], src[own, :], hi, ALU.subtract)
                        last = dve.tensor_tensor(m.k2l[other, 2 * c + i, :], src[own, :], hi, ALU.subtract)
                last.then_inc(split_done, 1)

            for j in range(len(tiles)):
                rotary(j)
                if j:
                    split_lo(j - 1)
                if 1 <= j <= NT:
                    t = j - 1
                    dve.wait_ge(v_ps, t + 1)
                    dve.tensor_tensor(m.v[:, t, 0:KV * HD], ps[:, 4 + t, 0:KV * HD], m.bv[:, :], ALU.add).then_inc(v_made, 1)
            split_lo(len(tiles) - 1)
            for t in range(NT):
                dve.tensor_tensor(m.x[:, t, :], m.x[:, t, :], m.bo[:, :], ALU.add).then_inc(xb, 1)

            def maxes(u):
                t, bank, slot = u // PAIRS, u % 2 * 2, u % 4
                w = (t + 1) * P
                dve.wait_ge(scored, u + 1)
                diag = ps[:, bank:bank + 2, t * P:w]
                dve.tensor_tensor(diag, diag, m.const(C_MASK, P).unsqueeze(1).to_broadcast([P, 2, P]), ALU.add).then_inc(masked, 1)
                dve.wait_ge(masked, u + 1)
                if u >= 4:
                    dve.wait_ge(exped, 2 * (u - 3))
                    dve.wait_ge(bias_made, u - 3)
                dve.tensor_reduce(m.amx[:, slot, :], ps[:, bank:bank + 2, 0:w], AX, ALU.max).then_inc(maxed, 1)
                dve.wait_ge(maxed, u + 1)
                dve.tensor_scalar(m.anb[:, slot, :], m.amx[:, slot, :], -ATT_SCALE, None, ALU.mult).then_inc(bias_made, 1)

            def move1(u):
                w = (u // PAIRS + 1) * P
                dve.wait_ge(turned, u + 1)
                if u >= 2:
                    dve.wait_ge(valued, u - 1)
                dve.tensor_copy(m.apt[u % 2][:, 1, 0:w], ps[:, 5, 0:w]).then_inc(pt1, 1)

            def invert(u):
                dve.wait_ge(exped, 2 * (u + 1))
                if u >= 4:
                    dve.wait_ge(out_made, u - 3)
                dve.reciprocal(m.arl[:, u % 4, :], m.ars[:, u % 4, :]).then_inc(inv, 1)

            def output(u):
                t, pair = u // PAIRS, u % PAIRS
                dve.wait_ge(valued, u + 1)
                dve.wait_ge(inv, u + 1)
                dve.tensor_tensor(m.ao[:, t, pair * P:(pair + 1) * P].rearrange("p (i n) -> p i n", i=2),
                                  ps[:, 6 + u % 2, 0:2 * P].rearrange("p (i n) -> p i n", i=2)[:, :, 0:HD],
                                  m.arl[:, u % 4, :].unsqueeze(2).to_broadcast([P, 2, HD]), ALU.mult).then_inc(out_made, 1)

            maxes(0)
            maxes(1)
            for u in range(AU):
                invert(u)
                move1(u)
                if u + 2 < AU:
                    maxes(u + 2)
                if u >= 1:
                    output(u - 1)
            output(AU - 1)
            for t in range(NT):
                dve.wait_ge(oT_hi, t + 1)
                dve.tensor_tensor(m.aoTl[t % 2][:, :, :], out_turned(), m.aoTh[t % 2][:, :, :].bitcast(F32),
                                  ALU.subtract).then_inc(oT_lo, 1)
            for t in range(NT):
                dve.wait_ge(wo_done, t + 1)
                dve.wait_ge(xb, t + 1)
                dve.tensor_tensor(m.x[:, t, :], m.x[:, t, :], ps[:, t, :], ALU.add).then_inc(x2, 1)
                dve.wait_ge(x2, t + 1)
                ln.vector_stats(dve, t)
            ln.vector(dve)


def feed_forward(nc, m, d, sem, s):
    lgT_ps, lgT, lg_ps, lg, top, eq, cand, first, onehot, th, score, rank_ps, own, rank, cnt, over, over_i = (
        sem(x) for x in ("lgT_summed", "lgT_made", "lg_turned", "lg_made", "top_made", "eq_made", "cand_made",
                         "first_made", "onehot_made", "tanh_made", "score_made", "rank_summed", "own_rank_made",
                         "rank_made", "counts_made", "over_made", "over_int_made"))
    xs, xs_hi, xs_lo = sem("xs_made"), sem("xs_hi_made"), sem("xs_lo_made")
    sh_in, sh_sil, sh_act, sh_hi, sh_lo, sh_out, x3 = (sem(x) for x in (
        "sh_projected", "sh_silu_made", "sh_act_made", "sh_act_hi_made", "sh_act_lo_made", "sh_down_done", "x3_made"))
    sel, selT_ps, selT, xg_ps, xg = (sem(x) for x in ("sel_made", "sel_turned", "selT_made", "gathered", "xg_made"))
    xg_hi, xg_lo = sem("xg_hi_made"), sem("xg_lo_made")
    gu, sil, act_made, a_ps, actT_hi, actT_lo, y_ps, y_hi, y_lo, put, added = (sem(x) for x in (
        "gu_done", "silu_made", "act_made", "act_turned", "actT_hi_made", "actT_lo_made", "y_done", "y_hi_made",
        "y_lo_made", "put_back", "put_added"))
    first_used = sem("first_of_pair_used")
    pieces = s.pieces
    count = len(pieces.order)
    BY_POOL = 3
    BY_VECTOR = 6
    ps = m.ps
    ident = m.const(C_IDENT, P)
    HALF = INNER // 2

    with nc.Block() as block:
        @block.sync
        def _(sp):
            for n in range(pieces.SLOTS, count):
                before = n - pieces.SLOTS
                e, name, half = pieces.order[before]
                if before % 2 == 0:
                    sp.wait_ge(first_used, before // 2 + 1)
                elif e == pieces.SHARED:
                    sp.wait_ge(sh_out if name == "down" else sh_in, 4 * (half + 1) if name == "up" else NT)
                elif name == "up":
                    sp.wait_ge(gu, 2 * e + half + 1)
                else:
                    sp.wait_ge(y_ps, e + 1)
                pieces.load(sp, n)

        @block.gpsimd
        def _(pool):
            zeros = m.const(C_ZERO).to_broadcast([P, DC, P])

            def split_tokens(e):
                own = m.xg[:, :, e * P:(e + 1) * P]
                pool.wait_ge(xg, DC * (e // 4 + 1))
                if e >= 2:
                    pool.wait_ge(gu, 2 * (e - 1))
                pool.tensor_tensor(m.xgh[e % 2][:, :, :], own, zeros, ALU.add).then_inc(xg_hi, 1)
                pool.wait_ge(xg_hi, e + 1)
                pool.tensor_tensor(m.xgl[e % 2][:, :, :], own, m.xgh[e % 2][:, :, :].bitcast(F32),
                                   ALU.subtract).then_inc(xg_lo, 1)

            for n in range(pieces.SLOTS, count):
                if n % BY_POOL == BY_POOL - 1:
                    pieces.lo(pool, n)
                if n == 2 * pieces.SLOTS - 1:
                    split_tokens(0)
                    split_tokens(1)
                for e in range(2, E):
                    if n == pieces.number(e - 1, "gate", 0) + 4:
                        split_tokens(e)

        @block.tensor
        def _(pe):
            for c in range(DC):
                last = pe.matmul(ps[0:E, 4, :], m.gw[:, c, :], m.hT[:, c, :], start=c == 0, stop=c == DC - 1)
            last.then_inc(lgT_ps, 1)

            def shared_in(k):
                if k >= 2:
                    pe.wait_ge(sh_act, k - 1)
                    pe.wait_ge(sh_sil, k - 1)
                for name, bank in (("gate", k % 2), ("up", 2 + k % 2)):
                    n = pieces.number(pieces.SHARED, name, k // 4)
                    hi, lo = pieces.wait(pe, n)
                    col = slice(k % 4 * P, (k % 4 + 1) * P)
                    for c in range(DC):
                        last = product(pe, ps[:, bank, :], (hi[:, c, col], lo[:, c, col]), (m.hTh[:, c, :], m.hTl[:, c, :]),
                                       c == 0, c == DC - 1)
                    if k % 4 == 3 and name == "gate":
                        last.then_inc(first_used, 1)
                last.then_inc(sh_in, 1)

            shared_in(0)
            pe.wait_ge(lgT, 1)
            for t in range(NT):
                last = pe.transpose(ps[:, 5, t * E:(t + 1) * E], m.lgt[:, t * P:(t + 1) * P], m.const(C_IDENT, E, E))
            last.then_inc(lg_ps, 1)
            shared_in(1)
            shared_in(2)
            pe.wait_ge(onehot, 1)
            for t in range(NT):
                for q in range(t + 1):
                    pe.matmul(ps[:, 6, t * E:(t + 1) * E], m.const(C_TRI if q == t else C_ONES, P), m.onehot[:, q, :],
                              start=q == 0, stop=q == t)
            for q in range(NT):
                last = pe.matmul(ps[:, 6, NT * E:(NT + 1) * E], m.const(C_ONES, P), m.onehot[:, q, :],
                                 start=q == 0, stop=q == NT - 1)
            last.then_inc(rank_ps, 1)
            for k in range(3, IC):
                shared_in(k)
            pe.wait_ge(cnt, 1)
            for half in range(2):
                n = pieces.number(pieces.SHARED, "down", half)
                hi, lo = pieces.wait(pe, n)
                for t in range(NT):
                    tok = slice(t * P, (t + 1) * P)
                    for k in range(4):
                        row = 4 * half + k
                        pe.wait_ge(sh_hi, row + 1)
                        pe.wait_ge(sh_lo, row + 1)
                        last = product(pe, ps[:, 4 + t, :], (m.sacth[:, row, tok], m.sactl[:, row, tok]),
                                       (hi[:, k, :], lo[:, k, :]), half == 0 and k == 0, half == 1 and k == 3)
                    if half:
                        last.then_inc(sh_out, 1)
                    elif t == NT - 1:
                        last.then_inc(first_used, 1)
            pe.wait_ge(xs_lo, NT)
            for half in range(2):
                pe.wait_ge(sel, 16 * (half + 1))
                for c in range(DC):
                    if half:
                        pe.wait_ge(xg, c + 1)
                    for t in range(NT):
                        for part in (m.xsh, m.xsl):
                            last = pe.matmul(ps[:, c, :], part[:, t, c * P:(c + 1) * P], m.sel[:, t, :, :],
                                             start=t == 0 and part is m.xsh, stop=t == NT - 1 and part is m.xsl)
                    last.then_inc(xg_ps, 1)
                for q in range(4):
                    e, bank = 4 * half + q, 4 + q
                    pe.wait_ge(x3, q + 1)
                    if half:
                        pe.wait_ge(selT, q + 1)
                    for t in range(NT):
                        last = pe.transpose(ps[:, bank, t * P:(t + 1) * P], m.sel[:, t, q, :].bitcast(F32), ident)
                    last.then_inc(selT_ps, 1)

            def gate_up(e, half):
                if half == 0:
                    pe.wait_ge(xg_lo, e + 1)
                if e:
                    pe.wait_ge(act_made, 2 * (e - 1) + half + 1)
                for name, bank in (("gate", 2 * half), ("up", 2 * half + 1)):
                    hi, lo = pieces.wait(pe, pieces.number(e, name, half))
                    for c in range(DC):
                        last = product(pe, ps[:, bank, :], (m.xgh[e % 2][:, c, :], m.xgl[e % 2][:, c, :]),
                                       (hi[:, c, :], lo[:, c, :]), c == 0, c == DC - 1)
                    if name == "gate":
                        last.then_inc(first_used, 1)
                last.then_inc(gu, 1)

            def turn_act(e, half):
                n = 2 * e + half
                pe.wait_ge(act_made, n + 1)
                if n:
                    pe.wait_ge(actT_lo, n)
                for k in range(4):
                    last = pe.transpose(ps[:, 4, k * P:(k + 1) * P], m.act[:, (4 * half + k) * P:(4 * half + k + 1) * P], ident)
                last.then_inc(a_ps, 1)

            def down(e):
                pe.wait_ge(actT_lo, 2 * e + 2)
                if e:
                    pe.wait_ge(y_lo, e)
                for half in range(2):
                    hi, lo = pieces.wait(pe, pieces.number(e, "down", half))
                    for k in range(4):
                        row = slice((4 * half + k) * P, (4 * half + k + 1) * P)
                        last = product(pe, ps[:, 5, :], (m.actTh[e % 2][:, row], m.actTl[e % 2][:, row]),
                                       (hi[:, k, :], lo[:, k, :]), half == 0 and k == 0, half == 1 and k == 3)
                    if half == 0:
                        last.then_inc(first_used, 1)
                last.then_inc(y_ps, 1)

            def put_back(half):
                pe.wait_ge(y_lo, 4 * (half + 1))
                for t in range(NT):
                    n = 4 * half + t
                    if n >= 2:
                        pe.wait_ge(added, n - 1)
                    for q in range(4):
                        for part in (m.yh, m.yl):
                            last = pe.matmul(ps[:, 6 + t % 2, :], m.selT[:, 4 * half + q, t * P:(t + 1) * P], part[:, q, :],
                                             start=q == 0 and part is m.yh, stop=q == 3 and part is m.yl)
                    last.then_inc(put, 1)

            pe.wait_ge(selT, E)
            for e in range(E):
                gate_up(e, 0)
                if e:
                    turn_act(e - 1, 1)
                gate_up(e, 1)
                turn_act(e, 0)
                if e == 5:
                    put_back(0)
                if e:
                    down(e - 1)
            turn_act(E - 1, 1)
            down(E - 1)
            put_back(1)

        @block.scalar
        def _(act):
            def hi_of_act(n):
                e, half = n // 2, n % 2
                act.wait_ge(a_ps, n + 1)
                if e >= 2:
                    act.wait_ge(y_ps, e - 1)
                act.activation(m.actTh[e % 2][:, half * HALF:(half + 1) * HALF], ps[:, 4, :], ACT.Copy).then_inc(actT_hi, 1)

            def hi_of_y(e):
                act.wait_ge(y_ps, e + 1)
                if e >= 4:
                    act.wait_ge(put, NT)
                act.activation(m.yh[:, e % 4, :], ps[:, 5, :], ACT.Copy).then_inc(y_hi, 1)

            def split(before, end):
                for n in range(before, min(end, count)):
                    if n % BY_VECTOR:
                        pieces.scalar_hi(act, n)

            act.wait_ge(lgT_ps, 1)
            act.activation(m.lgt[:, :], ps[0:E, 4, :], ACT.Copy).then_inc(lgT, 1)

            def shared_silu(k):
                act.wait_ge(sh_in, k + 1)
                if k >= 2:
                    act.wait_ge(sh_lo, k - 1)
                if k < 2:
                    act.wait_ge(lg_ps, 1)
                act.activation(m.sil[k % 2][:, :], ps[:, k % 2, :], ACT.Silu).then_inc(sh_sil, 1)

            shared_silu(0)
            shared_silu(1)
            act.wait_ge(top, 1)
            act.activation(m.score[:, :], m.top[:, :], ACT.Tanh, scale=0.5).then_inc(th, 1)
            for k in range(2, IC):
                shared_silu(k)
                if k == 5:
                    split(6, 8)
            split(8, 10)
            act.wait_ge(sh_in, IC)
            for t in range(NT):
                act.wait_ge(xs, t + 1)
                act.activation(m.xsh[:, t, :], m.h[:, t, :], ACT.Copy).then_inc(xs_hi, 1)
            for half in range(2):
                for c in range(DC):
                    act.wait_ge(xg_ps, half * DC + c + 1)
                    act.activation(m.xg[:, c, half * N:(half + 1) * N], ps[:, c, :], ACT.Copy).then_inc(xg, 1)
            split(10, 12)
            for e in range(E):
                for half in range(2):
                    n, q = 2 * e + half, pieces.number(e, "gate", half)
                    if n:
                        split(q + 4, q + 5)
                    act.wait_ge(gu, n + 1)
                    if e:
                        act.wait_ge(a_ps, n - 1)
                    act.activation(m.act[:, half * HALF:(half + 1) * HALF], ps[:, 2 * half, :], ACT.Silu).then_inc(sil, 1)
                    if n:
                        hi_of_act(n - 1)
                        split(q + 5, q + 6)
                if e:
                    q = pieces.number(e - 1, "down", 0)
                    split(q + 4, q + 5)
                    hi_of_y(e - 1)
                    split(q + 5, q + 6)
            hi_of_act(2 * E - 1)
            hi_of_y(E - 1)

        @block.vector
        def _(dve):
            def shared_act(k):
                dve.wait_ge(sh_sil, k + 1)
                own = m.sil[k % 2][:, :]
                dve.tensor_tensor(own, own, ps[:, 2 + k % 2, :], ALU.mult).then_inc(sh_act, 1)
                dve.wait_ge(sh_act, k + 1)
                dve.tensor_copy(m.sacth[:, k, :], own).then_inc(sh_hi, 1)
                dve.wait_ge(sh_hi, k + 1)
                dve.tensor_tensor(m.sactl[:, k, :], own, m.sacth[:, k, :].bitcast(F32), ALU.subtract).then_inc(sh_lo, 1)

            dve.wait_ge(lg_ps, 1)
            dve.tensor_copy(m.lg[:, :, :], ps[:, 5, 0:NT * E].rearrange("p (t e) -> p t e", t=NT)).then_inc(lg, 1)
            dve.wait_ge(lg, 1)
            dve.tensor_reduce(m.top[:, :], m.lg[:, :, :], AX, ALU.max).then_inc(top, 1)
            dve.wait_ge(top, 1)
            wide = [P, NT, E]
            dve.tensor_tensor(m.eq[:, :, :], m.lg[:, :, :], m.top[:, :].unsqueeze(2).to_broadcast(wide), ALU.is_equal).then_inc(eq, 1)
            dve.wait_ge(eq, 1)
            dve.tensor_tensor(m.tmp8[:, :, :], m.eq[:, :, :], m.const(C_PREF, E).unsqueeze(1).to_broadcast(wide), ALU.mult).then_inc(cand, 1)
            dve.wait_ge(cand, 1)
            dve.tensor_reduce(m.first[:, :], m.tmp8[:, :, :], AX, ALU.max).then_inc(first, 1)
            dve.wait_ge(first, 1)
            dve.tensor_tensor(m.onehot[:, :, :], m.tmp8[:, :, :], m.first[:, :].unsqueeze(2).to_broadcast(wide), ALU.is_equal).then_inc(onehot, 1)
            shared_act(0)
            dve.wait_ge(th, 1)
            dve.tensor_scalar(m.score[:, :], m.score[:, :], 0.5, 0.5, ALU.mult, ALU.add).then_inc(score, 1)
            dve.wait_ge(score, 1)
            for t in range(NT):
                dve.tensor_scalar(m.h[:, t, :], m.h[:, t, :], m.score[:, t:t + 1], None, ALU.mult).then_inc(xs, 1)
            shared_act(1)
            shared_act(2)
            dve.wait_ge(rank_ps, 1)
            dve.wait_ge(onehot, 1)
            dve.tensor_tensor(m.tmp8[:, :, :], ps[:, 6, 0:NT * E].rearrange("p (t e) -> p t e", t=NT), m.onehot[:, :, :], ALU.mult).then_inc(own, 1)
            dve.tensor_reduce(m.over[:, :], ps[:, 6, NT * E:(NT + 1) * E], AX, ALU.max).then_inc(cnt, 1)
            dve.wait_ge(own, 1)
            dve.tensor_reduce(m.rank[:, :], m.tmp8[:, :, :], AX, ALU.add).then_inc(rank, 1)
            dve.wait_ge(cnt, 1)
            dve.tensor_scalar(m.over[:, :], m.over[:, :], -float(P), 0.0, ALU.add, ALU.max).then_inc(over, 1)
            dve.wait_ge(over, 1)
            dve.tensor_copy(m.over_i[:, :], m.over[:, :]).then_inc(over_i, 1)
            def split(before, end):
                for n in range(before, min(end, count)):
                    if n % BY_VECTOR == 0:
                        pieces.vector_hi(dve, n)
                    if n % BY_POOL != BY_POOL - 1:
                        pieces.lo(dve, n)

            for k in range(3, IC):
                shared_act(k)
                if k == 5:
                    split(6, 8)
            split(8, 10)

            def select(half):
                if half:
                    dve.wait_ge(xg_ps, DC)
                    dve.wait_ge(selT_ps, 4)
                for t in range(NT):
                    for q in range(4):
                        dve.tensor_scalar(m.sel[:, t, q, :], m.const(C_IOTA, P), m.rank[:, t:t + 1],
                                          m.onehot[:, t, 4 * half + q:4 * half + q + 1], ALU.is_equal, ALU.mult).then_inc(sel, 1)

            def move_sel(half):
                for q in range(4):
                    e = 4 * half + q
                    dve.wait_ge(selT_ps, e + 1)
                    dve.tensor_copy(m.selT[:, e, :], ps[:, 4 + q, :]).then_inc(selT, 1)

            dve.wait_ge(rank, 1)
            select(0)
            for t in range(NT):
                dve.wait_ge(xs_hi, t + 1)
                dve.tensor_tensor(m.xsl[:, t, :], m.h[:, t, :], m.xsh[:, t, :].bitcast(F32), ALU.subtract).then_inc(xs_lo, 1)
            for t in range(NT):
                dve.wait_ge(sh_out, t + 1)
                dve.tensor_tensor(m.x[:, t, :], m.x[:, t, :], ps[:, 4 + t, :], ALU.add).then_inc(x3, 1)
            move_sel(0)
            select(1)
            move_sel(1)
            split(10, 12)

            def act_of(n):
                e, half = n // 2, n % 2
                a = m.act[:, half * HALF:(half + 1) * HALF]
                dve.wait_ge(sil, n + 1)
                dve.tensor_tensor(a, a, ps[:, 2 * half + 1, :], ALU.mult).then_inc(act_made, 1)

            def lo_of_act(n):
                e, half = n // 2, n % 2
                own = slice(half * HALF, (half + 1) * HALF)
                dve.wait_ge(actT_hi, n + 1)
                dve.tensor_tensor(m.actTl[e % 2][:, own], ps[:, 4, :], m.actTh[e % 2][:, own].bitcast(F32),
                                  ALU.subtract).then_inc(actT_lo, 1)

            def lo_of_y(e):
                dve.wait_ge(y_hi, e + 1)
                dve.tensor_tensor(m.yl[:, e % 4, :], ps[:, 5, :], m.yh[:, e % 4, :].bitcast(F32), ALU.subtract).then_inc(y_lo, 1)

            def add_back(half):
                for t in range(NT):
                    n = 4 * half + t
                    dve.wait_ge(put, n + 1)
                    dve.wait_ge(added, n - 3) if n >= 4 else dve.wait_ge(x3, t + 1)
                    dve.tensor_tensor(m.x[:, t, :], m.x[:, t, :], ps[:, 6 + t % 2, :], ALU.add).then_inc(added, 1)

            for e in range(E):
                for half in range(2):
                    n, q = 2 * e + half, pieces.number(e, "gate", half)
                    if n:
                        split(q + 4, q + 5)
                    act_of(n)
                    if n:
                        lo_of_act(n - 1)
                        split(q + 5, q + 6)
                if e:
                    q = pieces.number(e - 1, "down", 0)
                    split(q + 4, q + 5)
                    if e == 5:
                        add_back(0)
                    lo_of_y(e - 1)
                    split(q + 5, q + 6)
            lo_of_act(2 * E - 1)
            lo_of_y(E - 1)
            add_back(1)


def overflow(nc, m, d, sem):
    loaded, moved, sel, selT_ps, selT, xg_ps, xg, gu, sil, act_made, a_ps, actT, y_ps, y_hi, y_lo, put, added, xs_hi, xs_lo = (
        sem("over_" + x) for x in ("loaded", "rank_moved", "sel", "selT_ps", "selT", "xg_ps", "xg", "gu", "silu", "act",
                                   "act_turned", "actT", "y", "y_hi", "y_lo", "put", "added", "xs_hi", "xs_lo"))
    ps = m.ps
    ident = m.const(C_IDENT, P)
    ROUNDS = (N - 1) // P
    HALF = INNER // 2

    def rounds(eng, body):
        with eng.Fori(0, ROUNDS) as tile:
            with eng.Fori(0, E) as e:
                body(tile, e, tile * E + e)

    with nc.Block() as block:
        @block.gpsimd
        def _(pool):
            pool.memset(m.over[:, :], 0.0).then_inc(added, 1)

        @block.sync
        def _(sp):
            def body(tile, e, n):
                sp.wait_ge(added, n * NT + 1)
                for w, name in ((m.wg, "rt_gate"), (m.wu, "rt_up"), (m.wd, "rt_down")):
                    sp.dma_start(w[:, :, :], d[name][e].rearrange("(c p) n -> p c n", p=P)).then_inc(loaded, 16)

            rounds(sp, body)

        @block.tensor
        def _(pe):
            pe.wait_ge(xs_lo, 1)

            def body(tile, e, n):
                pe.wait_ge(sel, n * NT + NT)
                for t in range(NT):
                    last = pe.transpose(ps[:, 0, t * P:(t + 1) * P], m.osel[:, t, :].bitcast(F32), ident)
                last.then_inc(selT_ps, 1)
                for c in range(DC):
                    for t in range(NT):
                        for part in (m.xsh, m.xsl):
                            last = pe.matmul(ps[:, 1, c * P:(c + 1) * P], part[:, t, c * P:(c + 1) * P], m.osel[:, t, :],
                                             start=t == 0 and part is m.xsh, stop=t == NT - 1 and part is m.xsl)
                last.then_inc(xg_ps, 1)
                pe.wait_ge(xg, n + 1)
                pe.wait_ge(loaded, n * 48 + 48)
                for half in range(2):
                    for w, bank in ((m.wg, 2 + 2 * half), (m.wu, 3 + 2 * half)):
                        for c in range(DC):
                            last = pe.matmul(ps[:, bank, :], m.oxg[:, c, :], w[:, c, half * HALF:(half + 1) * HALF],
                                             start=c == 0, stop=c == DC - 1)
                    last.then_inc(gu, 1)
                pe.wait_ge(act_made, n * 2 + 2)
                for k in range(IC):
                    last = pe.transpose(ps[:, 6 + k // 4, k % 4 * P:(k % 4 + 1) * P], m.oact[:, k * P:(k + 1) * P], ident)
                last.then_inc(a_ps, 1)
                pe.wait_ge(actT, n + 1)
                for k in range(IC):
                    last = pe.matmul(ps[:, 0, :], m.oactT[:, k * P:(k + 1) * P], m.wd[:, k, :], start=k == 0, stop=k == IC - 1)
                last.then_inc(y_ps, 1)
                pe.wait_ge(y_lo, n + 1)
                for t in range(NT):
                    for part in (m.oyh, m.oyl):
                        last = pe.matmul(ps[:, 2 + t, :], m.oselT[:, t * P:(t + 1) * P], part[:, :],
                                         start=part is m.oyh, stop=part is m.oyl)
                last.then_inc(put, 1)

            rounds(pe, body)

        @block.scalar
        def _(act):
            act.activation(m.xsh[:, :, :], m.h[:, :, :], ACT.Copy).then_inc(xs_hi, 1)

            def body(tile, e, n):
                act.wait_ge(selT_ps, n + 1)
                act.activation(m.oselT[:, :], ps[:, 0, :], ACT.Copy).then_inc(selT, 1)
                act.wait_ge(xg_ps, n + 1)
                act.activation(m.oxg[:, :, :], ps[:, 1, :].rearrange("p (c n) -> p c n", c=DC), ACT.Copy).then_inc(xg, 1)
                for half in range(2):
                    act.wait_ge(gu, n * 2 + half + 1)
                    act.activation(m.oact[:, half * HALF:(half + 1) * HALF], ps[:, 2 + 2 * half, :], ACT.Silu).then_inc(sil, 1)
                act.wait_ge(a_ps, n + 1)
                act.activation(m.oactT[:, :], ps[:, 6:8, :], ACT.Copy).then_inc(actT, 1)
                act.wait_ge(y_ps, n + 1)
                act.activation(m.oyh[:, :], ps[:, 0, :], ACT.Copy).then_inc(y_hi, 1)

            rounds(act, body)

        @block.vector
        def _(dve):
            dve.tensor_scalar(m.rank[:, :], m.rank[:, :], -float(P), None, ALU.add).then_inc(moved, 1)
            dve.wait_ge(xs_hi, 1)
            dve.tensor_tensor(m.xsl[:, :, :], m.h[:, :, :], m.xsh[:, :, :].bitcast(F32), ALU.subtract).then_inc(xs_lo, 1)

            def body(tile, e, n):
                dve.wait_ge(added, n * NT + 1)
                dve.wait_ge(moved, tile + 1)
                for t in range(NT):
                    dve.tensor_scalar(m.osel[:, t, :], m.const(C_IOTA, P), m.rank[:, t:t + 1], m.onehot[:, t, bass.ds(e, 1)],
                                      ALU.is_equal, ALU.mult).then_inc(sel, 1)
                for half in range(2):
                    dve.wait_ge(sil, n * 2 + half + 1)
                    a = m.oact[:, half * HALF:(half + 1) * HALF]
                    dve.tensor_tensor(a, a, ps[:, 3 + 2 * half, :], ALU.mult).then_inc(act_made, 1)
                dve.wait_ge(y_hi, n + 1)
                dve.tensor_tensor(m.oyl[:, :], ps[:, 0, :], m.oyh[:, :].bitcast(F32), ALU.subtract).then_inc(y_lo, 1)
                dve.wait_ge(put, n + 1)
                for t in range(NT):
                    dve.tensor_tensor(m.x[:, t, :], m.x[:, t, :], ps[:, 2 + t, :], ALU.add).then_inc(added, 1)

            with dve.Fori(0, ROUNDS) as tile:
                with dve.Fori(0, E) as e:
                    body(tile, e, tile * E + e)
                dve.wait_ge(sel, (tile + 1) * E * NT)
                dve.tensor_scalar(m.rank[:, :], m.rank[:, :], -float(P), None, ALU.add).then_inc(moved, 1)


def store(nc, m, out, stored):
    with nc.Block() as block:
        @block.sync
        def _(sp):
            sp.dma_start(out.rearrange("o (t p) d -> p (o t) d", p=P), m.x[:, :, :]).then_inc(stored, 16)
            sp.wait_ge(stored, 16)


class Signals:
    pass


def perceiver_block(nc, d, out, phases=6):
    with ExitStack() as ctx:
        m = Memory(nc, ctx)
        s = Signals()

        made = []

        def sem(name):
            made.append(nc.alloc_semaphore(name))
            return made[-1]

        stored = nc.alloc_semaphore("stored")
        setup(nc, m, d, sem, s)
        if phases > 1:
            cross_attention(nc, m, sem, s)
            cross_output(nc, m, d, sem, s)
            nc.clear_and_free_semaphores(made[:])
            nc.all_engine_barrier()
            made.clear()
        if phases > 2:
            self_attention(nc, m, d, sem, s)
        if phases > 3:
            feed_forward(nc, m, d, sem, s)
        if phases > 4:
            beyond = nc.values_load(m.over_i[0:1, 0:1], min_val=0, max_val=N,
                                    skip_runtime_bounds_check_because="a count of tokens less 128, not below 0")
            with nc.If(beyond > 0):
                nc.clear_and_free_semaphores(made[:])
                nc.all_engine_barrier()
                overflow(nc, m, d, sem)
        store(nc, m, out, stored)


_NAMES = {"x": "x", "ctx_1024": "ctx", "L0_xattn_w_sim": "w_sim", "L0_xattn_b_sim": "b_sim", "L0_xattn_W_qv": "W_qv",
          "L0_xattn_b_qv": "b_qv", "L0_attn_Wq": "Wq", "L0_attn_bq": "bq", "L0_attn_Wk": "Wk", "L0_attn_bk": "bk",
          "L0_attn_Wv": "Wv", "L0_attn_bv": "bv", "L0_attn_Wo": "Wo", "L0_attn_bo": "bo", "L0_ffn_gate_w": "gate_w",
          "L0_ffn_sh_gate": "sh_gate", "L0_ffn_sh_up": "sh_up", "L0_ffn_sh_down": "sh_down",
          "L0_ffn_rt_gate": "rt_gate", "L0_ffn_rt_up": "rt_up", "L0_ffn_rt_down": "rt_down"}


def kernel(**inputs):
    import concourse.bacc as bacc
    from concourse.bass_utils import run_bass_kernel_spmd

    nc = bacc.Bacc("TRN2", target_bir_lowering=False, num_devices=1)
    arrays = {_NAMES[k]: np.ascontiguousarray(v) for k, v in inputs.items()}
    arrays["consts"] = constants()
    arrays = {f"in_{k}": v for k, v in arrays.items()}
    d = {k[3:]: nc.dram_tensor(k, v.shape, mybir.dt.from_np(v.dtype), kind="ExternalInput").ap() for k, v in arrays.items()}
    out = nc.dram_tensor("out", (1, N, D), F32, kind="ExternalOutput").ap()
    perceiver_block(nc, d, out)
    r = run_bass_kernel_spmd(nc, [arrays], core_ids=[0])
    return r.results[0]["out"]
```

```python
from contextlib import ExitStack

import numpy as np

import concourse.bass as bass
from concourse import mybir

F32 = mybir.dt.float32
F32R = mybir.dt.float32r
I32 = mybir.dt.int32
ALU = mybir.AluOpType
ACT = mybir.ActivationFunctionType
AX = mybir.AxisListType.X

P = 128
N = 512
D = 512
NT = N // P
DC = D // P
CTX = 8192
CB = 512
JT = CB // P
BLOCKS = CTX // CB
UNITS = BLOCKS * NT
STEP = 2 * NT
HEADS, KV, HD = 16, 4, 64
QT = HEADS * HD // P
INNER = 1024
IC = INNER // P
E = 8
EPS = 1e-5
FAR = 3e38
HIDDEN = -1e30
ATT_SCALE = HD ** -0.5

C_IDENT, C_EPS, C_ZERO = 0, P, P + 1
C_HEAD = P + 2
C_ROT, C_MASK, C_TRI, C_ONES, C_IOTA = (C_HEAD + k * P for k in range(5))
C_COS = C_HEAD + 5 * P
C_SIN = C_COS + N
C_PREF = C_SIN + N
C_ALL = C_PREF + E

R_W1, R_W2, R_W3, R_BQ, R_BK = 0, DC, 2 * DC, 3 * DC, 3 * DC + QT
ROWS = R_BK + 2


def constants():
    c = np.zeros((P, C_ALL), np.float32)
    i = np.arange(P)
    c[i, C_IDENT + i] = 1.0
    first = i % HD < HD // 2
    c[i[first] + HD // 2, C_ROT + i[first]] = -1.0
    c[i[~first] - HD // 2, C_ROT + i[~first]] = 1.0
    c[:, C_MASK:C_MASK + P] = np.where(i[None, :] > i[:, None], HIDDEN, 0.0)
    c[:, C_TRI:C_TRI + P] = i[:, None] < i[None, :]
    c[:, C_ONES:C_ONES + P] = 1.0
    c[:, C_IOTA:C_IOTA + P] = i[None, :]
    freq = np.float32(1.0) / np.float32(10000.0) ** (np.arange(0, HD, 2, dtype=np.float32) / np.float32(HD))
    angle = np.arange(N, dtype=np.float32)[None, :] * freq[i % (HD // 2)][:, None]
    c[:, C_COS:C_COS + N] = np.cos(angle)
    c[:, C_SIN:C_SIN + N] = np.sin(angle)
    c[:, C_PREF:C_PREF + E] = E - np.arange(E)[None, :]
    c[:, C_EPS] = EPS
    return c


class Memory:

    def __init__(self, nc, ctx):
        base = (nc.sbuf_base + 31) // 32 * 32
        self.nc = nc

        def at(name, kb, shape, dt=F32):
            return nc.alloc_sbuf_tensor_at(name, shape, dt, offset=base + int(kb * 1024))

        self.ps = ctx.enter_context(nc.psum_tensor("banks", [P, 8, 512], F32))
        self.x = at("x_res", 0, [P, NT, D])
        self.h = at("h_norm", 8, [P, NT, D])
        self.hT = at("hT", 16, [P, DC, N])
        self.c = at("consts", 40, [P, C_ALL])
        self.small_at = 47.5 * 1024

        def small(name, shape, dt=F32):
            size = int(np.prod(shape[1:])) * 4
            t = nc.alloc_sbuf_tensor_at(name, shape, dt, offset=base + int(self.small_at))
            self.small_at += (size + 31) // 32 * 32
            assert self.small_at <= 50 * 1024
            return t

        self.wT = small("wT", [P, ROWS])
        self.stats = small("ln_stats", [P, NT, 6])
        self.mv = small("ln_mean_var", [P, NT, 2])
        self.sd = small("ln_sd", [P, NT])
        self.rstd = small("ln_rstd", [P, NT])
        self.e1 = small("enc_w1", [P, NT])
        self.negm = small("neg_max", [P, 2, NT])
        self.mx = small("block_max", [P, 2 * NT])
        self.alpha = small("alpha", [P, 2 * NT])
        self.rowsum = small("row_sum", [P, 2 * NT])
        self.den = small("denominator", [P, NT])
        self.rden = small("inv_denominator", [P, NT])
        self.bsim = small("b_sim", [P, 1])
        self.mcol = small("token_max", [P, NT])
        self.r1 = small("token_scalars", [P, 4])
        self.hc = small("hc_bar", [P, DC])
        self.amx = small("att_max", [P, 4, 4])
        self.anb = small("att_bias", [P, 4, 4])
        self.ars = small("att_sum", [P, 4, 4])
        self.arl = small("att_inv", [P, 4, 4])
        self.gw = small("gate_w", [P, DC, E])
        self.lg = small("logits", [P, NT, E])
        self.top = small("top", [P, NT])
        self.eq = small("is_top", [P, NT, E])
        self.first = small("first_top", [P, NT])
        self.onehot = small("onehot", [P, NT + 1, E])
        self.score = small("score", [P, NT])
        self.tmp8 = small("rank_of_own", [P, NT, E])
        self.rank = small("rank", [P, NT])
        self.cnt = small("counts", [P, E])
        self.over = small("overflow", [P, 1])
        self.over_i = small("overflow_int", [P, 1], I32)
        self.bqv = at("b_qv_all", 198, [P, D])
        self.bo = at("b_o_all", 200, [P, D])
        self.bv = at("b_v_all", 202, [P, KV * HD])
        self.rows = at("rows", 203, [ROWS, P])
        self.w1all = at("w1_all", 203.5, [P, D])
        self.mrow = at("token_weights_all", 203.5, [P, N])
        self.junk = at("products_of_sums", 205.5, [P, N])
        self.hTh = at("hT_hi", 24, [P, DC, N], F32R)
        self.hTl = at("hT_lo", 32, [P, DC, N], F32R)
        self.gh = at("g_hi", 24, [P, DC, N], F32R)
        self.gl = at("g_lo", 32, [P, DC, N], F32R)
        self.raw = [at(f"ctx_raw{s}", 50 + 8 * s, [P, JT, D]) for s in range(2)]
        self.nh = [at(f"ctx_hi{s}", 66 + 8 * s, [P, JT, D], F32R) for s in range(2)]
        self.nl = [at(f"ctx_lo{s}", 82 + 8 * s, [P, JT, D], F32R) for s in range(2)]
        self.th = [at(f"ctxT_hi{s}", 98 + 8 * s, [P, DC, CB], F32R) for s in range(2)]
        self.tl = [at(f"ctxT_lo{s}", 114 + 8 * s, [P, DC, CB], F32R) for s in range(2)]
        self.p = [at(f"probs{s}", 130 + 2 * s, [P, CB]) for s in range(2)]
        self.pth = [at(f"probsT_hi{s}", 134 + 2 * s, [P, CB], F32R) for s in range(2)]
        self.ptl = [at(f"probsT_lo{s}", 138 + 2 * s, [P, CB], F32R) for s in range(2)]
        self.o = at("attended", 142, [P, NT, D])
        self.g = at("g_whole", 142, [P, DC, N])

        def weight(name, kb, shape, hi_kb=None):
            hi_kb = kb + int(np.prod(shape[1:])) * 4 // 1024 if hi_kb is None else hi_kb
            return at(name, kb, shape), at(name + "_hi", hi_kb, shape, F32R), at(name + "_lo", kb, shape, F32R)

        self.w23, self.w23h, self.w23l = weight("w_qv23", 150, [P, 2, DC, D])
        self.w1, self.w1h, self.w1l = weight("w_qv1", 182, [P, DC, D], 82)
        self.w4 = at("w_qv4", 190, [P, DC, D])
        self.hqTh = at("hqT_hi", 50, [P, DC, N], F32R)
        self.hqTl = at("hqT_lo", 58, [P, DC, N], F32R)
        self.ehTh = at("enc_hqT_hi", 66, [P, DC, N], F32R)
        self.ehTl = at("enc_hqT_lo", 74, [P, DC, N], F32R)
        self.ehT = at("enc_hqT", 90, [P, DC, N])
        self.wq, self.wqh, self.wql = weight("w_q", 98, [P, DC, HEADS * HD])
        self.wkv, self.wkvh, self.wkvl = weight("w_kv", 130, [P, 2, DC, KV * HD])
        self.wo, self.woh, self.wol = weight("w_o", 154, [P, QT, D])
        self.k2h = at("k_hi_twice", 8, [P, KV, N], F32R)
        self.k2l = at("k_lo_twice", 16, [P, KV, N], F32R)
        self.q2 = at("q_hi_lo", 50, [P, HEADS, N], F32R)
        self.qb = [at(f"q_biased{s}", 82 + 2 * s, [P, N]) for s in range(2)]
        self.qc = [at(f"q_cos{s}", 86 + 2 * s, [P, N]) for s in range(2)]
        self.qs = [at(f"q_sin{s}", 90 + 2 * s, [P, N]) for s in range(2)]
        self.qbh = [at(f"q_biased_hi{s}", 146 + 4 * s, [P, N], F32R) for s in range(2)]
        self.qbl = [at(f"q_biased_lo{s}", 148 + 4 * s, [P, N], F32R) for s in range(2)]
        self.rot = at("rotation", 94, [P, P], F32R)
        self.v = at("values", 186, [P, NT, (KV + 1) * HD])
        self.ap = [at(f"att_probs{s}", 191 + 4 * s, [P, 2, N]) for s in range(2)]
        self.apt = [at(f"att_probsT{s}", 199 + 4 * s, [P, 2, N]) for s in range(2)]
        self.ao = at("att_out", 24, [P, NT, HEADS * HD])
        self.aoTh = [at(f"att_outT_hi{s}", 191 + 8 * s, [P, QT, P], F32R) for s in range(2)]
        self.aoTl = [at(f"att_outT_lo{s}", 195 + 8 * s, [P, QT, P], F32R) for s in range(2)]
        self.piece = [weight(f"piece{s}", kb, [P, 4, 512]) for s, kb in enumerate((82, 98, 114, 130, 50, 66))]
        self.sacth = at("sh_act_hi", 154, [P, IC, N], F32R)
        self.sactl = at("sh_act_lo", 170, [P, IC, N], F32R)
        self.sil = [at(f"silu{s}", 186 + 2 * s, [P, 512]) for s in range(2)]
        self.lgt = at("logits_turned", 190, [E, N])
        self.xsh = at("xs_hi", 24, [P, NT, D], F32R)
        self.xsl = at("xs_lo", 32, [P, NT, D], F32R)
        self.sel = at("select", 146, [P, NT, 4, P], F32R)
        self.xg = [at("gatheredT0", 16, [P, DC, 4 * P]), at("gatheredT1", 190, [P, DC, 4 * P])]
        self.selT = at("selectT", 170, [P, E, N], F32R)
        self.act = at("act", 186, [P, INNER])
        self.actTh = [at(f"actT_hi{s}", 154 + 8 * s, [P, INNER], F32R) for s in range(2)]
        self.actTl = [at(f"actT_lo{s}", 158 + 8 * s, [P, INNER], F32R) for s in range(2)]
        self.xgh = [at(f"gatheredT_hi{s}", 198 + 4 * s, [P, DC, P], F32R) for s in range(2)]
        self.xgl = [at(f"gatheredT_lo{s}", 200 + 4 * s, [P, DC, P], F32R) for s in range(2)]
        self.yh = at("y_hi", 24, [P, 4, D], F32R)
        self.yl = at("y_lo", 32, [P, 4, D], F32R)
        self.wg = at("over_gate", 50, [P, DC, INNER])
        self.wu = at("over_up", 66, [P, DC, INNER])
        self.wd = at("over_down", 82, [P, IC, D])
        self.osel = at("over_select", 146, [P, NT, P], F32R)
        self.oselT = at("over_selectT", 170, [P, N], F32R)
        self.oxg = at("over_gatheredT", 154, [P, DC, P])
        self.oact = at("over_act", 98, [P, INNER])
        self.oactT = at("over_actT", 102, [P, INNER])
        self.oyh = at("over_y_hi", 106, [P, D], F32R)
        self.oyl = at("over_y_lo", 108, [P, D], F32R)

    def const(self, col, n=1, rows=P):
        return self.c[0:rows, col:col + n]


class Norm:

    def __init__(self, m, sem, tag, whole, parts, banks):
        self.m, self.whole, self.parts, self.banks = m, whole, parts, banks
        self.stats = sem(f"{tag}_stats")
        self.var = sem(f"{tag}_var")
        self.sd = sem(f"{tag}_sd")
        self.rstd = sem(f"{tag}_rstd")
        self.h = sem(f"{tag}_h")
        self.turned = sem(f"{tag}_turned")
        self.hT = sem(f"{tag}_hT")
        self.hTl = sem(f"{tag}_hT_lo") if parts else None

    def turned_tile(self, t):
        return self.m.ps[:, self.banks[t], :].rearrange("p (c n) -> p c n", c=DC)

    def vector_normalize(self, dve, t):
        m = self.m
        dve.bn_stats(m.stats[:, t, :], m.x[:, t, :]).then_inc(self.stats, 1)
        dve.wait_ge(self.stats, t + 1)
        dve.bn_aggr(m.mv[:, t, :], m.stats[:, t, :]).then_inc(self.var, 1)
        dve.wait_ge(self.sd, t + 1)
        dve.reciprocal(m.rstd[:, t:t + 1], m.sd[:, t:t + 1]).then_inc(self.rstd, 1)
        dve.wait_ge(self.rstd, t + 1)
        dve.tensor_scalar(m.h[:, t, :], m.x[:, t, :], m.mv[:, t, 0:1], m.rstd[:, t:t + 1],
                          ALU.subtract, ALU.mult).then_inc(self.h, 1)

    def vector_lo(self, dve, t):
        m, tok = self.m, slice(t * P, (t + 1) * P)
        dve.wait_ge(self.hT, t + 1)
        dve.tensor_tensor(m.hTl[:, :, tok], self.turned_tile(t), m.hTh[:, :, tok].bitcast(F32),
                          ALU.subtract).then_inc(self.hTl, 1)

    def scalar_root(self, act, t):
        m = self.m
        act.wait_ge(self.var, t + 1)
        act.activation(m.sd[:, t:t + 1], m.mv[:, t, 1:2], ACT.Sqrt, bias=m.const(C_EPS)).then_inc(self.sd, 1)

    def scalar_keep(self, act, t):
        m = self.m
        act.wait_ge(self.turned, t + 1)
        for dst in [m.hT] * self.whole + [m.hTh] * self.parts:
            last = act.activation(dst[:, :, t * P:(t + 1) * P], self.turned_tile(t), ACT.Copy)
        last.then_inc(self.hT, 1)

    def scalar(self, act):
        self.scalar_root(act, 0)
        for t in range(NT):
            if t + 1 < NT:
                self.scalar_root(act, t + 1)
            self.scalar_keep(act, t)

    def tensor(self, pe, t):
        m = self.m
        pe.wait_ge(self.h, t + 1)
        if self.banks[t] in self.banks[:t]:
            pe.wait_ge(self.hT, t - 1)
        for c in range(DC):
            last = pe.transpose(m.ps[:, self.banks[t], c * P:(c + 1) * P], m.h[:, t, c * P:(c + 1) * P],
                                m.const(C_IDENT, P))
        last.then_inc(self.turned, 1)


def product(pe, out, lhs, rhs, first, last):
    pe.matmul(out, lhs[0], rhs[0], start=first, stop=False)
    pe.matmul(out, lhs[0], rhs[1], start=False, stop=False)
    return pe.matmul(out, lhs[1], rhs[0], start=False, stop=last)


def need(eng, sem, base, n):
    if not isinstance(base, int) or base + n > 0:
        eng.wait_ge(sem, base + n)


def cross_attention(nc, m, d, sem, s):
    ct_turned, ct_hi, ct_lo = sem("ctxT_turned"), sem("ctxT_hi_made"), sem("ctxT_lo_made")
    n_hi, n_lo = sem("ctx_hi_made"), sem("ctx_lo_made")
    scored, maxed, negm_made = sem("scored"), sem("block_maxed"), sem("negm_made")
    alpha_made, exp_made = sem("alpha_made"), sem("exp_made")
    pt_turned, pt_hi, pt_lo = sem("probsT_turned"), sem("probsT_hi_made"), sem("probsT_lo_made")
    attended, den_made, merged = sem("attended_made"), sem("den_made"), sem("merged")
    w23_hi, e1_made = sem("w23_hi_made"), sem("e1_made")
    ln = Norm(m, sem, "ln0", True, False, [6, 7, 6, 7])
    head_loaded, consts_loaded, x_loaded = sem("head_loaded"), sem("consts_loaded"), [sem(f"x_loaded{k}") for k in range(2)]
    rows_loaded, rows_turned, wT_ready = sem("rows_loaded"), sem("rows_turned"), sem("wT_ready")
    g_whole, g_hi, g_lo = sem("g_whole_made"), sem("g_hi_made"), sem("g_lo_made")
    cleared = sem("sums_cleared")
    s.ctx_loaded = [sem(f"ctx_loaded{k}") for k in range(2)]
    s.w23_loaded, s.w14_loaded, s.bias_loaded = sem("w23_loaded"), sem("w14_loaded"), sem("bias_loaded")
    s.ctx = d["ctx"].rearrange("o (b p t) d -> (o b) p t d", p=P, t=JT)
    S_BANK, PT_BANK, CT_BANK, O_BANK = 0, 2, 4, 6
    AHEAD_S, AHEAD_CT, AHEAD_N = 2, 6, 4
    ps = m.ps
    ident = m.const(C_IDENT, P)
    loops = UNITS // STEP

    def loaded(eng, base, n):
        slot, use = n // JT % 2, n // JT // 2 + 1
        eng.wait_ge(s.ctx_loaded[slot], base * 2 + 16 * use)

    def turns(eng, unit, prologue):
        prologue()
        for k in range(STEP):
            unit(0, k, False)
        with eng.Fori(STEP, UNITS - STEP, STEP) as base:
            for k in range(STEP):
                unit(base, k, False)
        for k in range(STEP):
            unit(UNITS - STEP, k, True)

    with nc.Block() as block:
        @block.sync
        def _(sp):
            def load(base, block_index, slot, k):
                need(sp, ct_turned, base, JT * (k + 1))
                need(sp, n_lo, base, JT * (k + 1))
                sp.dma_start(m.raw[slot][:, :, :], s.ctx[block_index]).then_inc(s.ctx_loaded[slot], 16)

            x_tiles = d["x"].rearrange("o (t p) d -> p (o t) d", p=P)
            sp.dma_start(m.x[:, 0:2, :], x_tiles[:, 0:2, :]).then_inc(x_loaded[0], 16)
            sp.dma_start(m.c[:, 0:C_HEAD], d["consts"][:, 0:C_HEAD]).then_inc(head_loaded, 16)
            sp.dma_start(m.rows[0:3 * DC, :], d["w_sim"].rearrange("(a p) -> a p", p=P)).then_inc(rows_loaded, 16)
            sp.dma_start(m.rows[R_BQ:R_BK, :], d["bq"].rearrange("(a p) -> a p", p=P)).then_inc(rows_loaded, 16)
            sp.dma_start(m.rows[R_BK:ROWS, :], d["bk"].rearrange("(a p) -> a p", p=P)).then_inc(rows_loaded, 16)
            sp.dma_start(m.raw[0][:, :, :], s.ctx[0]).then_inc(s.ctx_loaded[0], 16)
            sp.dma_start(m.x[:, 2:4, :], x_tiles[:, 2:4, :]).then_inc(x_loaded[1], 16)
            sp.dma_start(m.raw[1][:, :, :], s.ctx[1]).then_inc(s.ctx_loaded[1], 16)
            for k in range(2):
                load(0, 2 + k, k, k)
            sp.dma_start(m.c[:, C_HEAD:], d["consts"][:, C_HEAD:]).then_inc(consts_loaded, 16)
            sp.dma_start(m.w1all[:, :], d["w_sim"][0:D].partition_broadcast(P)).then_inc(s.bias_loaded, 16)
            sp.dma_start(m.bqv[:, :], d["b_qv"].partition_broadcast(P)).then_inc(s.bias_loaded, 16)
            sp.dma_start(m.bo[:, :], d["bo"].partition_broadcast(P)).then_inc(s.bias_loaded, 16)
            sp.dma_start(m.bv[:, :], d["bv"].partition_broadcast(P)).then_inc(s.bias_loaded, 16)
            sp.dma_start(m.bsim[:, :], d["b_sim"].partition_broadcast(P)).then_inc(s.bias_loaded, 16)
            sp.dma_start(m.gw[:, :, :], d["gate_w"].rearrange("(c p) e -> p c e", p=P)).then_inc(s.bias_loaded, 16)
            wqv = d["W_qv"].rearrange("(a c p) n -> a p c n", p=P, a=4)
            for k in range(2):
                sp.dma_start(m.w23[:, k, :, :], wqv[1 + k]).then_inc(s.w23_loaded, 16)
            sp.dma_start(m.w1[:, :, :], wqv[0]).then_inc(s.w14_loaded, 16)
            sp.dma_start(m.w4[:, :, :], wqv[3]).then_inc(s.w14_loaded, 16)
            with sp.Fori(1, loops - 1) as turn:
                for k in range(2):
                    load(turn * STEP, turn * 2 + 2 + k, k, k)

        @block.gpsimd
        def _(pool):
            zeros = m.const(C_ZERO).to_broadcast([P, D])

            def split(base, n):
                slot = n // JT % 2
                loaded(pool, base, n)
                need(pool, attended, base, n // JT * JT - JT)
                raw, hi, lo = m.raw[slot][:, n % JT, :], m.nh[slot][:, n % JT, :], m.nl[slot][:, n % JT, :]
                pool.tensor_tensor(hi, raw, zeros, ALU.add).then_inc(n_hi, 1)
                need(pool, n_hi, base, n + 1)
                pool.tensor_tensor(lo, raw, hi.bitcast(F32), ALU.subtract).then_inc(n_lo, 1)

            def split_weights(part, c):
                raw, hi, lo = m.w23[:, part, c, :], m.w23h[:, part, c, :], m.w23l[:, part, c, :]
                n = part * DC + c
                pool.tensor_tensor(hi, raw, zeros, ALU.add).then_inc(w23_hi, 1)
                pool.wait_ge(w23_hi, n + 1)
                pool.tensor_tensor(lo, raw, hi.bitcast(F32), ALU.subtract)

            def unit(base, k, last):
                if not last or k + AHEAD_N < STEP:
                    split(base, k + AHEAD_N)
                if last:
                    if k == 0:
                        pool.wait_ge(s.w23_loaded, 32)
                    split_weights(k // DC, k % DC)

            def prologue():
                pool.wait_ge(head_loaded, 16)
                for n in range(AHEAD_N):
                    split(0, n)

            turns(pool, unit, prologue)

        @block.tensor
        def _(pe):
            def turn_ctx(base, n):
                slot, bank = n // JT % 2, CT_BANK + n % 2
                loaded(pe, base, n)
                need(pe, ct_lo, base, n - 1)
                for c in range(DC):
                    last = pe.transpose(ps[:, bank, c * P:(c + 1) * P], m.raw[slot][:, n % JT, c * P:(c + 1) * P], ident)
                last.then_inc(ct_turned, 1)

            def score(base, v):
                slot, i, bank = v // NT % 2, v % NT, S_BANK + v % 2
                need(pe, ct_lo, base, v // NT * JT + JT)
                if isinstance(base, int) and base == 0 and v < NT:
                    pe.wait_ge(g_lo, v + 1)
                need(pe, exp_made, base, v - 1)
                tok = slice(i * P, (i + 1) * P)
                for c in range(DC):
                    pe.matmul(ps[:, bank, :], m.gh[:, c, tok], m.th[slot][:, c, :], start=c == 0, stop=False)
                    pe.matmul(ps[:, bank, :], m.gh[:, c, tok], m.tl[slot][:, c, :], start=False, stop=False)
                    last = pe.matmul(ps[:, bank, :], m.gl[:, c, tok], m.th[slot][:, c, :], start=False, stop=c == DC - 1)
                last.then_inc(scored, 1)

            def turn_probs(base, u):
                need(pe, exp_made, base, u + 1)
                need(pe, pt_lo, base, u - 1)
                for j in range(JT):
                    last = pe.transpose(ps[:, PT_BANK + u % 2, j * P:(j + 1) * P], m.p[u % 2][:, j * P:(j + 1) * P], ident)
                last.then_inc(pt_turned, 1)

            def attend(base, u):
                slot, bank, b = u // NT % 2, O_BANK + u % 2, u % 2
                need(pe, pt_lo, base, u + 1)
                need(pe, n_lo, base, u // NT * JT + JT)
                need(pe, merged, base, u - 1)
                for j in range(JT):
                    col = slice(j * P, (j + 1) * P)
                    pe.matmul(ps[:, bank, :], m.pth[b][:, col], m.nh[slot][:, j, :], start=j == 0, stop=False)
                    pe.matmul(ps[:, bank, :], m.pth[b][:, col], m.nl[slot][:, j, :], start=False, stop=False)
                    last = pe.matmul(ps[:, bank, :], m.ptl[b][:, col], m.nh[slot][:, j, :], start=False, stop=j == JT - 1)
                last.then_inc(attended, 1)

            def unit(base, k, last):
                if not last or k < STEP - 1:
                    turn_probs(base, k)
                if last and k == STEP - 2:
                    turn_probs(base, k + 1)
                if not last or k + AHEAD_CT < STEP:
                    turn_ctx(base, k + AHEAD_CT)
                if not last or k + AHEAD_S < STEP:
                    score(base, k + AHEAD_S)
                attend(base, k)

            def prologue():
                pe.wait_ge(head_loaded, 16)
                ln.tensor(pe, 0)
                pe.wait_ge(rows_loaded, 48)
                pe.transpose(ps[:, PT_BANK, 0:ROWS], m.rows[:, :], m.const(C_IDENT, ROWS, ROWS)).then_inc(rows_turned, 1)
                ln.tensor(pe, 1)
                for n in range(JT):
                    turn_ctx(0, n)
                score(0, 0)
                score(0, 1)
                ln.tensor(pe, 2)
                ln.tensor(pe, 3)
                for n in range(JT, AHEAD_CT):
                    turn_ctx(0, n)
                pe.wait_ge(ln.hT, NT)

            turns(pe, unit, prologue)

        @block.scalar
        def _(act):
            def ctx_hi(base, n):
                need(act, ct_turned, base, n + 1)
                need(act, scored, base, n // JT * NT - NT)
                act.activation(m.th[n // JT % 2][:, :, n % JT * P:(n % JT + 1) * P],
                               ps[:, CT_BANK + n % 2, :].rearrange("p (c n) -> p c n", c=DC),
                               ACT.Copy).then_inc(ct_hi, 1)

            def exps(base, v):
                i, new, b = v % NT, v // NT % 2, v % STEP
                need(act, negm_made, base, v + 1)
                act.activation(m.alpha[:, b:b + 1], m.negm[:, 1 - new, i:i + 1], ACT.Exp, scale=-1.0,
                               bias=m.negm[:, new, i:i + 1]).then_inc(alpha_made, 1)
                need(act, pt_turned, base, v - 1)
                act.activation(m.p[v % 2][:, :], ps[:, S_BANK + v % 2, :], ACT.Exp, bias=m.negm[:, new, i:i + 1],
                               accum_out=m.rowsum[:, b:b + 1]).then_inc(exp_made, 1)

            def probs_hi(base, u):
                need(act, pt_turned, base, u + 1)
                need(act, attended, base, u - 1)
                act.activation(m.pth[u % 2][:, :], ps[:, PT_BANK + u % 2, :], ACT.Copy).then_inc(pt_hi, 1)

            def unit(base, k, last):
                probs_hi(base, k)
                if not last or k + AHEAD_CT < STEP:
                    ctx_hi(base, k + AHEAD_CT)
                if not last or k + AHEAD_S < STEP:
                    exps(base, k + AHEAD_S)

            def prologue():
                act.wait_ge(head_loaded, 16)
                ln.scalar_root(act, 0)
                ln.scalar_root(act, 1)
                ln.scalar_keep(act, 0)
                act.wait_ge(rows_turned, 1)
                act.activation(m.wT[:, :], ps[:, PT_BANK, 0:ROWS], ACT.Copy).then_inc(wT_ready, 1)
                ln.scalar_keep(act, 1)
                for n in range(JT):
                    ctx_hi(0, n)
                ln.scalar_root(act, 2)
                ln.scalar_root(act, 3)
                ln.scalar_keep(act, 2)
                ln.scalar_keep(act, 3)
                for n in range(JT, AHEAD_CT):
                    ctx_hi(0, n)
                act.wait_ge(cleared, 2)
                exps(0, 0)
                exps(0, 1)

            turns(act, unit, prologue)

        @block.vector
        def _(dve):
            def ctx_lo(base, n):
                slot, col = n // JT % 2, slice(n % JT * P, (n % JT + 1) * P)
                need(dve, ct_hi, base, n + 1)
                dve.tensor_tensor(m.tl[slot][:, :, col], ps[:, CT_BANK + n % 2, :].rearrange("p (c n) -> p c n", c=DC),
                                  m.th[slot][:, :, col].bitcast(F32), ALU.subtract).then_inc(ct_lo, 1)

            def maxes(base, v):
                i, new, b = v % NT, v // NT % 2, v % STEP
                need(dve, scored, base, v + 1)
                dve.tensor_reduce(m.mx[:, b:b + 1], ps[:, S_BANK + v % 2, :], AX, ALU.max).then_inc(maxed, 1)
                need(dve, maxed, base, v + 1)
                dve.scalar_tensor_tensor(m.negm[:, new, i:i + 1], m.mx[:, b:b + 1], -1.0, m.negm[:, 1 - new, i:i + 1],
                                         ALU.mult, ALU.min).then_inc(negm_made, 1)

            def probs_lo(base, u):
                need(dve, pt_hi, base, u + 1)
                dve.tensor_tensor(m.ptl[u % 2][:, :], ps[:, PT_BANK + u % 2, :], m.pth[u % 2][:, :].bitcast(F32),
                                  ALU.subtract).then_inc(pt_lo, 1)

            def merge(base, u):
                i, b = u % NT, u % STEP
                need(dve, attended, base, u + 1)
                need(dve, exp_made, base, u + 1)
                need(dve, merged, base, u - NT + 1)
                if isinstance(base, int) and base == 0 and u < NT:
                    dve.tensor_copy(m.o[:, i, :], ps[:, O_BANK + u % 2, :]).then_inc(merged, 1)
                else:
                    dve.scalar_tensor_tensor(m.o[:, i, :], m.o[:, i, :], m.alpha[:, b:b + 1], ps[:, O_BANK + u % 2, :],
                                             ALU.mult, ALU.add).then_inc(merged, 1)
                need(dve, den_made, base, u - NT + 1)
                dve.scalar_tensor_tensor(m.den[:, i:i + 1], m.den[:, i:i + 1], m.alpha[:, b:b + 1],
                                         m.rowsum[:, b:b + 1], ALU.mult, ALU.add).then_inc(den_made, 1)

            def unit(base, k, last):
                probs_lo(base, k)
                if not isinstance(base, int) or base + k > 0:
                    merge(base, k - 1) if k else merge(base, -1)
                if not last or k + AHEAD_CT < STEP:
                    ctx_lo(base, k + AHEAD_CT)
                if not last or k + AHEAD_S < STEP:
                    maxes(base, k + AHEAD_S)

            def make_g(t):
                tok = slice(t * P, (t + 1) * P)
                dve.wait_ge(ln.hT, t + 1)
                for c in range(DC):
                    dve.tensor_scalar(m.g[:, c, tok], m.hT[:, c, tok], m.wT[:, R_W3 + c:R_W3 + c + 1],
                                      m.wT[:, R_W2 + c:R_W2 + c + 1], ALU.mult, ALU.add).then_inc(g_whole, 1)
                dve.wait_ge(g_whole, DC * (t + 1))
                dve.tensor_copy(m.gh[:, :, tok], m.g[:, :, tok]).then_inc(g_hi, 1)
                dve.wait_ge(g_hi, t + 1)
                dve.tensor_tensor(m.gl[:, :, tok], m.g[:, :, tok], m.gh[:, :, tok].bitcast(F32), ALU.subtract).then_inc(g_lo, 1)

            def prologue():
                dve.memset(m.den[:, :], 0.0).then_inc(cleared, 1)
                dve.memset(m.negm[:, 1, :], FAR).then_inc(cleared, 1)
                dve.wait_ge(x_loaded[0], 16)
                ln.vector_normalize(dve, 0)
                ln.vector_normalize(dve, 1)
                dve.wait_ge(wT_ready, 1)
                make_g(0)
                for n in range(JT):
                    ctx_lo(0, n)
                make_g(1)
                dve.wait_ge(x_loaded[1], 16)
                ln.vector_normalize(dve, 2)
                ln.vector_normalize(dve, 3)
                dve.wait_ge(cleared, 2)
                maxes(0, 0)
                for n in range(JT, AHEAD_CT):
                    ctx_lo(0, n)
                make_g(2)
                maxes(0, 1)
                make_g(3)
                dve.wait_ge(g_lo, NT)

            def token_sums():
                dve.wait_ge(s.bias_loaded, 96)
                dve.wait_ge(consts_loaded, 16)
                for t in range(NT):
                    if t:
                        dve.wait_ge(e1_made, t)
                    dve.tensor_tensor_reduce(out=m.junk[:, :], in0=m.h[:, t, :], in1=m.w1all[:, :], scale=1.0, scalar=0.0,
                                             op0=ALU.mult, op1=ALU.add, accum_out=m.e1[:, t:t + 1]).then_inc(e1_made, 1)

            turns(dve, unit, prologue)
            token_sums()
            merge(UNITS - STEP, STEP - 1)


def cross_output(nc, m, d, sem, s):
    ln = Norm(m, sem, "ln1", False, True, [5, 6, 7, 0])
    mcol0, mcol, mrow, rmax, rexp, rinv, hc_sum, hc = (sem(x) for x in (
        "mcol_sum", "mcol_made", "mrow_turned", "row_max", "row_exp", "row_inv", "hc_summed", "hc_made"))
    rden, hq, hq_turned, xb, fed, x1 = (sem(x) for x in (
        "rden_made", "hq_made", "hq_turned", "x_biased", "fed", "x1_made"))
    enc_hi, enc_lo, hqT_hi, hqT_lo, eh_whole, eh_hi, eh_lo, w14, w14_hi, w14_lo = (sem(x) for x in (
        "encT_hi_made", "encT_lo_made", "hqT_hi_made", "hqT_lo_made", "ehT_made", "ehT_hi_made", "ehT_lo_made",
        "w14_made", "w14_hi_made", "w14_lo_made"))
    wkv_loaded, wq_loaded, wkv_hi, wq_hi = (sem(x) for x in ("wkv_loaded", "wq_loaded", "wkv_hi_made", "wq_hi_made"))
    ROW_BANK = 4
    ps = m.ps
    out_bank = ln.banks
    encT, hqT, ehT = (m.hTh, m.hTl), (m.hqTh, m.hqTl), (m.ehTh, m.ehTl)

    def turned_tile(t):
        return ps[:, t, :].rearrange("p (c n) -> p c n", c=DC)

    with nc.Block() as block:
        @block.sync
        def _(sp):
            sp.dma_start(m.wkv[:, 0, :, :], d["Wk"].rearrange("(c p) n -> p c n", p=P)).then_inc(wkv_loaded, 16)
            sp.dma_start(m.wkv[:, 1, :, :], d["Wv"].rearrange("(c p) n -> p c n", p=P)).then_inc(wkv_loaded, 16)
            sp.dma_start(m.wq[:, :, :], d["Wq"].rearrange("(c p) n -> p c n", p=P)).then_inc(wq_loaded, 16)

        @block.tensor
        def _(pe):
            pe.wait_ge(mcol, 1)
            for t in range(NT):
                last = pe.matmul(ps[:, ROW_BANK, t * P:(t + 1) * P], m.mcol[:, t:t + 1].to_broadcast([P, P]),
                                 m.const(C_IDENT, P), start=True, stop=True)
            last.then_inc(mrow, 1)
            for t in range(NT):
                pe.wait_ge(hq, t + 1)
                for c in range(DC):
                    last = pe.transpose(ps[:, t, c * P:(c + 1) * P], m.o[:, t, c * P:(c + 1) * P], m.const(C_IDENT, P))
                last.then_inc(hq_turned, 1)

            def feed(t, lhs, rhs, start, stop):
                tok = slice(t * P, (t + 1) * P)
                for c in range(DC):
                    last = product(pe, ps[:, out_bank[t], :], (lhs[0][:, c, tok], lhs[1][:, c, tok]),
                                   (rhs[0][:, c, :], rhs[1][:, c, :]), start and c == 0, stop and c == DC - 1)
                return last

            for t in range(NT):
                pe.wait_ge(hqT_hi, t + 1)
                pe.wait_ge(hqT_lo, t + 1)
                if t == NT - 1:
                    pe.wait_ge(eh_whole, 1)
                feed(t, hqT, (m.w23h[:, 0, :, :], m.w23l[:, 0, :, :]), True, False)
            for t in range(NT):
                pe.wait_ge(eh_hi, t + 1)
                pe.wait_ge(eh_lo, t + 1)
                feed(t, ehT, (m.w23h[:, 1, :, :], m.w23l[:, 1, :, :]), False, False)
            pe.wait_ge(enc_hi, NT)
            pe.wait_ge(enc_lo, NT)
            pe.wait_ge(w14_hi, DC)
            pe.wait_ge(w14_lo, DC)
            for t in range(NT):
                feed(t, encT, (m.w1h, m.w1l), False, True).then_inc(fed, 1)
                if t:
                    ln.tensor(pe, t - 1)
            ln.tensor(pe, NT - 1)

        @block.scalar
        def _(act):
            for c in range(DC):
                act.activation(m.hTh[:, c, :], m.hT[:, c, :], ACT.Copy).then_inc(enc_hi, 1)
            for t in range(NT):
                act.wait_ge(hq_turned, t + 1)
                act.activation(m.hqTh[:, :, t * P:(t + 1) * P], turned_tile(t), ACT.Copy).then_inc(hqT_hi, 1)
            act.wait_ge(rmax, 2)
            act.activation(m.mrow[:, :], ps[:, ROW_BANK, :], ACT.Exp, bias=m.r1[:, 1:2],
                           accum_out=m.r1[:, 2:3]).then_inc(rexp, 1)
            for t in range(NT):
                act.wait_ge(eh_whole, t + 1)
                act.activation(m.ehTh[:, :, t * P:(t + 1) * P], m.ehT[:, :, t * P:(t + 1) * P], ACT.Copy).then_inc(eh_hi, 1)
            act.wait_ge(wkv_loaded, 32)
            for k in range(2):
                act.activation(m.wkvh[:, k, :, :], m.wkv[:, k, :, :], ACT.Copy).then_inc(wkv_hi, 1)
            for c in range(DC):
                act.wait_ge(w14, c + 1)
                act.activation(m.w1h[:, c, :], m.w1[:, c, :], ACT.Copy).then_inc(w14_hi, 1)
            act.wait_ge(wq_loaded, 16)
            for c in range(DC):
                act.activation(m.wqh[:, c, :], m.wq[:, c, :], ACT.Copy).then_inc(wq_hi, 1)
            ln.scalar(act)

        @block.gpsimd
        def _(pool):
            for c in range(DC):
                pool.wait_ge(enc_hi, c + 1)
                pool.tensor_tensor(m.hTl[:, c, :], m.hT[:, c, :], m.hTh[:, c, :].bitcast(F32), ALU.subtract).then_inc(enc_lo, 1)
            pool.wait_ge(s.bias_loaded, 96)
            for t in range(NT):
                pool.tensor_tensor(m.x[:, t, :], m.x[:, t, :], m.bqv[:, :], ALU.add).then_inc(xb, 1)
            for k in range(2):
                pool.wait_ge(wkv_hi, k + 1)
                pool.tensor_tensor(m.wkvl[:, k, :, :], m.wkv[:, k, :, :], m.wkvh[:, k, :, :].bitcast(F32), ALU.subtract)
            for c in range(DC):
                pool.wait_ge(wq_hi, c + 1)
                pool.tensor_tensor(m.wql[:, c, :], m.wq[:, c, :], m.wqh[:, c, :].bitcast(F32), ALU.subtract)

        @block.vector
        def _(dve):
            dve.scalar_tensor_tensor(m.mcol[:, :], m.negm[:, 1, :], -1.0, m.e1[:, :], ALU.mult, ALU.add).then_inc(mcol0, 1)
            dve.reciprocal(m.rden[:, :], m.den[:, :]).then_inc(rden, 1)
            dve.wait_ge(mcol0, 1)
            dve.wait_ge(s.bias_loaded, 96)
            dve.tensor_scalar(m.mcol[:, :], m.mcol[:, :], m.bsim[:, 0:1], None, ALU.add).then_inc(mcol, 1)
            dve.wait_ge(rden, 1)
            for t in range(NT):
                dve.tensor_scalar(m.o[:, t, :], m.o[:, t, :], m.rden[:, t:t + 1], None, ALU.mult).then_inc(hq, 1)
            dve.wait_ge(mrow, 1)
            dve.tensor_reduce(m.r1[:, 0:1], ps[:, ROW_BANK, :], AX, ALU.max).then_inc(rmax, 1)
            dve.wait_ge(rmax, 1)
            dve.tensor_scalar(m.r1[:, 1:2], m.r1[:, 0:1], -1.0, None, ALU.mult).then_inc(rmax, 1)
            for t in range(NT):
                tok = slice(t * P, (t + 1) * P)
                dve.wait_ge(hqT_hi, t + 1)
                dve.tensor_tensor(m.hqTl[:, :, tok], turned_tile(t), m.hqTh[:, :, tok].bitcast(F32), ALU.subtract).then_inc(hqT_lo, 1)
            for t in range(NT):
                tok = slice(t * P, (t + 1) * P)
                dve.tensor_tensor(m.ehT[:, :, tok], m.hT[:, :, tok], turned_tile(t), ALU.mult).then_inc(eh_whole, 1)
            for t in range(NT):
                tok = slice(t * P, (t + 1) * P)
                dve.wait_ge(eh_hi, t + 1)
                dve.tensor_tensor(m.ehTl[:, :, tok], m.ehT[:, :, tok], m.ehTh[:, :, tok].bitcast(F32), ALU.subtract).then_inc(eh_lo, 1)
            dve.wait_ge(rexp, 1)
            dve.reciprocal(m.r1[:, 3:4], m.r1[:, 2:3]).then_inc(rinv, 1)
            for c in range(DC):
                if c:
                    dve.wait_ge(hc_sum, c)
                dve.tensor_tensor_reduce(out=m.junk[:, :], in0=m.hT[:, c, :], in1=m.mrow[:, :], scale=1.0, scalar=0.0,
                                         op0=ALU.mult, op1=ALU.add, accum_out=m.hc[:, c:c + 1]).then_inc(hc_sum, 1)
            dve.wait_ge(hc_sum, DC)
            dve.wait_ge(rinv, 1)
            dve.tensor_scalar(m.hc[:, :], m.hc[:, :], m.r1[:, 3:4], None, ALU.mult).then_inc(hc, 1)
            dve.wait_ge(hc, 1)
            dve.wait_ge(s.w14_loaded, 32)
            for c in range(DC):
                dve.scalar_tensor_tensor(m.w1[:, c, :], m.w4[:, c, :], m.hc[:, c:c + 1], m.w1[:, c, :],
                                         ALU.mult, ALU.add).then_inc(w14, 1)
            for c in range(DC):
                dve.wait_ge(w14_hi, c + 1)
                dve.tensor_tensor(m.w1l[:, c, :], m.w1[:, c, :], m.w1h[:, c, :].bitcast(F32), ALU.subtract).then_inc(w14_lo, 1)
            for t in range(NT):
                dve.wait_ge(fed, t + 1)
                dve.wait_ge(xb, t + 1)
                dve.tensor_tensor(m.x[:, t, :], m.x[:, t, :], ps[:, out_bank[t], :], ALU.add).then_inc(x1, 1)
                dve.wait_ge(x1, t + 1)
                ln.vector_normalize(dve, t)
                if t:
                    ln.vector_lo(dve, t - 1)
            ln.vector_lo(dve, NT - 1)


class Pieces:
    SLOTS = 6
    SHARED = -1

    def __init__(self, m, d, sem):
        self.m, self.d = m, d
        self.order = [(self.SHARED, name, half) for name, half in (
            ("gate", 0), ("up", 0), ("gate", 1), ("up", 1), ("down", 0), ("down", 1))]
        for e in range(E):
            self.order += [(e, "gate", 0), (e, "up", 0), (e, "gate", 1), (e, "up", 1)]
            if e:
                self.order += [(e - 1, "down", 0), (e - 1, "down", 1)]
        self.order += [(E - 1, "down", 0), (E - 1, "down", 1)]
        self.loaded = [sem(f"piece_loaded{k}") for k in range(self.SLOTS)]
        self.hi_made = [sem(f"piece_hi_made{k}") for k in range(self.SLOTS)]
        self.lo_made = [sem(f"piece_lo_made{k}") for k in range(self.SLOTS)]

    def number(self, e, name, half):
        return self.order.index((e, name, half))

    def load(self, sp, n):
        e, name, half = self.order[n]
        w = self.d["sh_" + name] if e == self.SHARED else self.d["rt_" + name][e]
        if name == "down":
            w = w[half * 4 * P:(half + 1) * 4 * P, :].rearrange("(c p) n -> p c n", p=P)
        else:
            w = w[:, half * 512:(half + 1) * 512].rearrange("(c p) n -> p c n", p=P)
        sp.dma_start(self.m.piece[n % self.SLOTS][0][:, :, :], w).then_inc(self.loaded[n % self.SLOTS], 16)

    def raw_loaded(self, eng, n):
        eng.wait_ge(self.loaded[n % self.SLOTS], 16 * (n // self.SLOTS + 1))
        return self.m.piece[n % self.SLOTS][0], self.m.piece[n % self.SLOTS][1]

    def scalar_hi(self, act, n):
        raw, hi = self.raw_loaded(act, n)
        act.activation(hi[:, :, :], raw[:, :, :], ACT.Copy).then_inc(self.hi_made[n % self.SLOTS], 4)

    def vector_hi(self, dve, n):
        raw, hi = self.raw_loaded(dve, n)
        dve.tensor_copy(hi[:, :, :], raw[:, :, :]).then_inc(self.hi_made[n % self.SLOTS], 4)

    def pool_hi(self, pool, n, zeros):
        raw, hi = self.raw_loaded(pool, n)
        for c in range(4):
            pool.tensor_tensor(hi[:, c, :], raw[:, c, :], zeros, ALU.add).then_inc(self.hi_made[n % self.SLOTS], 1)

    def lo(self, eng, n):
        raw, hi, lo = self.m.piece[n % self.SLOTS]
        eng.wait_ge(self.hi_made[n % self.SLOTS], 4 * (n // self.SLOTS + 1))
        eng.tensor_tensor(lo[:, :, :], raw[:, :, :], hi[:, :, :].bitcast(F32),
                          ALU.subtract).then_inc(self.lo_made[n % self.SLOTS], 1)

    def wait(self, pe, n):
        raw, hi, lo = self.m.piece[n % self.SLOTS]
        pe.wait_ge(self.lo_made[n % self.SLOTS], n // self.SLOTS + 1)
        return hi, lo


def self_attention(nc, m, d, sem, s):
    ln = Norm(m, sem, "ln2", True, True, [4, 5, 6, 7])
    projected, biased, rotated, cosed, sined, summed, q_hi, k_hi, split_done = (sem(x) for x in (
        "projected", "q_biased_made", "q_rotated", "q_cosed", "q_sined", "rotary_made", "q_hi_made", "k_hi_made",
        "qk_lo_made"))
    v_ps, v_made, v_pad = sem("v_projected"), sem("v_made"), sem("v_padded")
    scored, masked, maxed, bias_made, exped = (sem(x) for x in (
        "att_scored", "att_masked", "att_maxed", "att_bias_made", "att_exp_made"))
    turned, pt0, pt1, valued, inv, out_made = (sem(x) for x in (
        "att_turned", "att_pt0_made", "att_pt1_made", "att_valued", "att_inv_made", "att_out_made"))
    o_turned, oT_hi, oT_lo, wo_done, xb, x2 = (sem(x) for x in (
        "out_turned", "outT_hi_made", "outT_lo_made", "wo_done", "x1_biased", "x2_made"))
    rot_made, biased_hi, biased_lo = sem("rotation_made"), sem("q_biased_hi_made"), sem("q_biased_lo_made")
    wo_loaded, wo_hi, wo_lo = sem("wo_loaded"), sem("wo_hi_made"), sem("wo_lo_made")
    PROJ_BANK, ROT_BANK, V_BANK = 2, 6, 4
    ps = m.ps
    ident = m.const(C_IDENT, P)
    units = [(t, h, n) for t in range(NT) for n in [4 if t < 2 else 2] for h in range(0, HEADS, n)]
    AU = len(units)

    def exps_through(u):
        return sum(n for _, _, n in units[:u + 1])

    def outputs_through(t):
        return sum(unit[0] <= t for unit in units)

    def head_place(u, k):
        t, _, n = units[u]
        return k // (n // 2), k % (n // 2) * (t + 1) * P

    tiles = [("k", c) for c in range(KV * HD // P)] + [("q", c) for c in range(QT)]
    pieces = s.pieces = Pieces(m, d, sem)

    def out_turned(t):
        return ps[:, t % 2 * 2:t % 2 * 2 + 2, :].rearrange("p a (c n) -> p (a c) n", c=4)

    with nc.Block() as block:
        @block.sync
        def _(sp):
            sp.dma_start(m.wo[:, :, :], d["Wo"].rearrange("(c p) n -> p c n", p=P)).then_inc(wo_loaded, 16)
            sp.wait_ge(projected, len(tiles))
            sp.wait_ge(v_ps, NT)
            for n in (1, 2, 3):
                pieces.load(sp, n)
            sp.wait_ge(split_done, len(tiles))
            pieces.load(sp, 0)
            sp.wait_ge(scored, AU)
            for n in (4, 5):
                pieces.load(sp, n)

        @block.gpsimd
        def _(pool):
            zeros = m.const(C_ZERO).to_broadcast([P, D])
            for j in range(len(tiles)):
                pool.wait_ge(biased_hi, j + 1)
                if j >= 2:
                    pool.wait_ge(rotated, j - 1)
                pool.tensor_tensor(m.qbl[j % 2][:, :], m.qb[j % 2][:, :], m.qbh[j % 2][:, :].bitcast(F32),
                                   ALU.subtract).then_inc(biased_lo, 1)
                if j >= 2:
                    pool.wait_ge(split_done, j - 1)
                pool.tensor_tensor(m.qc[j % 2][:, :], m.qb[j % 2][:, :], m.const(C_COS, N), ALU.mult).then_inc(cosed, 1)
                if j < NT:
                    pool.tensor_tensor(m.x[:, j, :], m.x[:, j, :], m.bo[:, :], ALU.add).then_inc(xb, 1)
            pool.wait_ge(wo_loaded, 16)
            for c in range(QT):
                pool.tensor_tensor(m.woh[:, c, :], m.wo[:, c, :], zeros, ALU.add).then_inc(wo_hi, 1)
            for c in range(QT):
                pool.wait_ge(wo_hi, c + 1)
                pool.tensor_tensor(m.wol[:, c, :], m.wo[:, c, :], m.woh[:, c, :].bitcast(F32), ALU.subtract).then_inc(wo_lo, 1)
            for n in (1, 2, 3, 0, 4, 5):
                pieces.pool_hi(pool, n, zeros)
                pieces.lo(pool, n)

        @block.tensor
        def _(pe):
            def rotate(j):
                pe.wait_ge(biased_lo, j + 1)
                if j >= 2:
                    pe.wait_ge(sined, j - 1)
                else:
                    pe.wait_ge(rot_made, 1)
                pe.matmul(ps[:, ROT_BANK + j % 2, :], m.rot[:, :], m.qbh[j % 2][:, :], start=True, stop=False)
                pe.matmul(ps[:, ROT_BANK + j % 2, :], m.rot[:, :], m.qbl[j % 2][:, :], start=False, stop=True).then_inc(rotated, 1)

            def score(u):
                t, first, n = units[u]
                pe.wait_ge(split_done, 2 + (first + n) // 2)
                if u >= 2:
                    pe.wait_ge(exped, exps_through(u - 2))
                elif u:
                    pe.wait_ge(biased_hi, len(tiles))
                for k in range(n):
                    i, col = head_place(u, k)
                    g, bank = (first + k) // (HEADS // KV), u % 2 * 2 + i
                    q, w = m.q2[:, first + k, t * P:(t + 1) * P], (t + 1) * P
                    pe.matmul(ps[:, bank, col:col + w], q, m.k2h[:, g, 0:w], start=True, stop=False)
                    last = pe.matmul(ps[:, bank, col:col + w], q, m.k2l[:, g, 0:w], start=False, stop=True)
                last.then_inc(scored, 1)

            for j, (kind, c) in enumerate(tiles):
                hi, lo = (m.wkvh[:, 0, :, :], m.wkvl[:, 0, :, :]) if kind == "k" else (m.wqh, m.wql)
                if j >= 2:
                    pe.wait_ge(biased_hi, j - 1)
                for dc in range(DC):
                    last = product(pe, ps[:, PROJ_BANK + j % 2, :], (hi[:, dc, c * P:(c + 1) * P], lo[:, dc, c * P:(c + 1) * P]),
                                   (m.hTh[:, dc, :], m.hTl[:, dc, :]), dc == 0, dc == DC - 1)
                last.then_inc(projected, 1)
                if j:
                    rotate(j - 1)
                if 1 <= j <= NT:
                    t = j - 1
                    if t >= 2:
                        pe.wait_ge(v_made, t - 1)
                    for dc in range(DC):
                        tok = slice(t * P, (t + 1) * P)
                        last = product(pe, ps[:, V_BANK + t % 2, 0:KV * HD], (m.hTh[:, dc, tok], m.hTl[:, dc, tok]),
                                       (m.wkvh[:, 1, dc, :], m.wkvl[:, 1, dc, :]), dc == 0, dc == DC - 1)
                    last.then_inc(v_ps, 1)
                if j == len(tiles) - 2:
                    score(0)
            score(1)
            rotate(len(tiles) - 1)

            def turn(u):
                t, _, n = units[u]
                pe.wait_ge(exped, exps_through(u))
                if u == 0:
                    pe.wait_ge(v_made, NT)
                if u >= 1:
                    pe.wait_ge(pt0, u)
                    pe.wait_ge(pt1, u)
                for i in range(2):
                    for k in range(n // 2 * (t + 1)):
                        last = pe.transpose(ps[:, 4 + i, k * P:(k + 1) * P], m.ap[u % 2][:, i, k * P:(k + 1) * P], ident)
                last.then_inc(turned, 1)

            def value(u):
                t, first, n = units[u]
                if u == 0:
                    pe.wait_ge(v_pad, 1)
                    pe.wait_ge(sined, len(tiles))
                pe.wait_ge(pt0, u + 1)
                pe.wait_ge(pt1, u + 1)
                if u >= 2:
                    pe.wait_ge(out_made, u - 1)
                for h in range(n):
                    i, col = head_place(u, h)
                    g = (first + h) // (HEADS // KV)
                    for k in range(t + 1):
                        last = pe.matmul(ps[:, 6 + u % 2, h * P:(h + 1) * P], m.apt[u % 2][:, i, col + k * P:col + (k + 1) * P],
                                         m.v[:, k, g * HD:g * HD + P], start=k == 0, stop=k == t)
                last.then_inc(valued, 1)

            def turn_out(t):
                if t >= 2:
                    pe.wait_ge(oT_lo, t - 1)
                else:
                    pe.wait_ge(exped, exps_through(AU - 2 + t))
                pe.wait_ge(out_made, outputs_through(t))
                for c in range(QT):
                    bank = t % 2 * 2 + c // 4
                    last = pe.transpose(ps[:, bank, c % 4 * P:(c % 4 + 1) * P], m.ao[:, t, c * P:(c + 1) * P], ident)
                last.then_inc(o_turned, 1)

            for u in range(AU):
                turn(u)
                if u + 2 < AU:
                    score(u + 2)
                if u == AU - 1:
                    turn_out(0)
                    turn_out(1)
                if u >= 1:
                    value(u - 1)
            value(AU - 1)
            pe.wait_ge(wo_lo, QT)
            turn_out(2)
            for t in range(NT):
                pe.wait_ge(oT_lo, t + 1)
                pe.wait_ge(out_made, AU)
                for c in range(QT):
                    last = product(pe, ps[:, 4 + t, :], (m.aoTh[t % 2][:, c, :], m.aoTl[t % 2][:, c, :]),
                                   (m.woh[:, c, :], m.wol[:, c, :]), c == 0, c == QT - 1)
                last.then_inc(wo_done, 1)
                if t == 0:
                    turn_out(3)
                else:
                    ln.tensor(pe, t - 1)
            ln.tensor(pe, NT - 1)

        @block.scalar
        def _(act):
            def bias(j):
                kind, c = tiles[j]
                col = (R_BK if kind == "k" else R_BQ) + c
                act.wait_ge(projected, j + 1)
                if j >= 2:
                    act.wait_ge(rotated, j - 1)
                    act.wait_ge(cosed, j - 1)
                act.activation(m.qb[j % 2][:, :], ps[:, PROJ_BANK + j % 2, :], ACT.Identity, bias=m.wT[:, col:col + 1]).then_inc(biased, 1)
                act.activation(m.qbh[j % 2][:, :], ps[:, PROJ_BANK + j % 2, :], ACT.Identity, bias=m.wT[:, col:col + 1]).then_inc(biased_hi, 1)

            def split_hi(j):
                kind, c = tiles[j]
                act.wait_ge(summed, j + 1)
                src = m.qc[j % 2]
                for i in range(2):
                    own = slice(i * HD, (i + 1) * HD)
                    other = slice((1 - i) * HD, (2 - i) * HD)
                    if kind == "q":
                        act.activation(m.q2[own, 2 * c + i, :], src[own, :], ACT.Copy).then_inc(q_hi, 1)
                    else:
                        act.activation(m.k2h[own, 2 * c + i, :], src[own, :], ACT.Copy).then_inc(k_hi, 1)
                        act.activation(m.k2h[other, 2 * c + i, :], src[own, :], ACT.Copy).then_inc(k_hi, 1)

            act.activation(m.rot[:, :], m.const(C_ROT, P), ACT.Copy).then_inc(rot_made, 1)
            for j in range(len(tiles)):
                bias(j)
                if j:
                    split_hi(j - 1)

            def exps(u):
                t, _, n = units[u]
                act.wait_ge(bias_made, u + 1)
                if u >= 2:
                    act.wait_ge(turned, u - 1)
                if u >= 4:
                    act.wait_ge(inv, u - 3)
                for k in range(n):
                    (i, col), w = head_place(u, k), (t + 1) * P
                    act.activation(m.ap[u % 2][:, i, col:col + w], ps[:, u % 2 * 2 + i, col:col + w], ACT.Exp,
                                   scale=ATT_SCALE, bias=m.anb[:, u % 4, k:k + 1],
                                   accum_out=m.ars[:, u % 4, k:k + 1]).then_inc(exped, 1)

            def move0(u):
                w = units[u][2] // 2 * (units[u][0] + 1) * P
                act.wait_ge(turned, u + 1)
                if u >= 2:
                    act.wait_ge(valued, u - 1)
                act.activation(m.apt[u % 2][:, 0, 0:w], ps[:, 4, 0:w], ACT.Copy).then_inc(pt0, 1)

            exps(0)
            split_hi(len(tiles) - 1)
            exps(1)
            for u in range(AU):
                move0(u)
                if u + 2 < AU:
                    exps(u + 2)
            def out_hi(t):
                act.wait_ge(o_turned, t + 1)
                if t == 1:
                    act.wait_ge(valued, AU)
                if t >= 2:
                    act.wait_ge(wo_done, t - 1)
                act.activation(m.aoTh[t % 2][:, :, :], out_turned(t), ACT.Copy).then_inc(oT_hi, 1)

            out_hi(0)
            out_hi(1)
            out_hi(2)
            ln.scalar_root(act, 0)
            out_hi(3)
            ln.scalar_root(act, 1)
            for t in range(NT):
                ln.scalar_keep(act, t)
                if t + 2 < NT:
                    ln.scalar_root(act, t + 2)

        @block.vector
        def _(dve):
            dve.memset(m.v[:, :, KV * HD:], 0.0).then_inc(v_pad, 1)

            def rotary(j):
                b = j % 2
                dve.wait_ge(rotated, j + 1)
                if j >= 2:
                    dve.wait_ge(summed, j - 1)
                dve.tensor_tensor(m.qs[b][:, :], ps[:, ROT_BANK + b, :], m.const(C_SIN, N), ALU.mult).then_inc(sined, 1)
                dve.wait_ge(cosed, j + 1)
                dve.wait_ge(sined, j + 1)
                dve.tensor_tensor(m.qc[b][:, :], m.qc[b][:, :], m.qs[b][:, :], ALU.add).then_inc(summed, 1)

            def split_lo(j):
                kind, c = tiles[j]
                src = m.qc[j % 2]
                dve.wait_ge(summed, j + 1)
                for i in range(2):
                    own = slice(i * HD, (i + 1) * HD)
                    other = slice((1 - i) * HD, (2 - i) * HD)
                    if kind == "q":
                        dve.wait_ge(q_hi, 2 * (j - 2) + i + 1)
                        last = dve.tensor_tensor(m.q2[other, 2 * c + i, :], src[own, :],
                                                 m.q2[own, 2 * c + i, :].bitcast(F32), ALU.subtract)
                    else:
                        dve.wait_ge(k_hi, 4 * j + 2 * i + 2)
                        hi = m.k2h[own, 2 * c + i, :].bitcast(F32)
                        dve.tensor_tensor(m.k2l[own, 2 * c + i, :], src[own, :], hi, ALU.subtract)
                        last = dve.tensor_tensor(m.k2l[other, 2 * c + i, :], src[own, :], hi, ALU.subtract)
                last.then_inc(split_done, 1)

            def maxes(u):
                (t, _, n), bank, slot = units[u], u % 2 * 2, u % 4
                w = (t + 1) * P
                scores = ps[:, bank:bank + 2, 0:n // 2 * w].rearrange("p b (h w) -> p b h w", w=w)
                dve.wait_ge(scored, u + 1)
                mask = m.const(C_MASK, P).unsqueeze(1).unsqueeze(1).to_broadcast([P, 2, n // 2, P])
                dve.tensor_tensor(scores[:, :, :, t * P:w], scores[:, :, :, t * P:w], mask, ALU.add).then_inc(masked, 1)
                dve.wait_ge(masked, u + 1)
                if u >= 4:
                    dve.wait_ge(exped, exps_through(u - 4))
                    dve.wait_ge(bias_made, u - 3)
                dve.tensor_reduce(m.amx[:, slot, 0:n].rearrange("p (b h) -> p b h", b=2), scores, AX, ALU.max).then_inc(maxed, 1)
                dve.wait_ge(maxed, u + 1)
                dve.tensor_scalar(m.anb[:, slot, 0:n], m.amx[:, slot, 0:n], -ATT_SCALE, None, ALU.mult).then_inc(bias_made, 1)

            for j in range(len(tiles)):
                rotary(j)
                if j:
                    split_lo(j - 1)
                if j == len(tiles) - 2:
                    dve.wait_ge(xb, NT)
                    maxes(0)
                if 1 <= j <= NT:
                    t = j - 1
                    dve.wait_ge(v_ps, t + 1)
                    dve.tensor_tensor(m.v[:, t, 0:KV * HD], ps[:, V_BANK + t % 2, 0:KV * HD], m.bv[:, :], ALU.add).then_inc(v_made, 1)
            def move1(u):
                w = units[u][2] // 2 * (units[u][0] + 1) * P
                dve.wait_ge(turned, u + 1)
                if u >= 2:
                    dve.wait_ge(valued, u - 1)
                dve.tensor_copy(m.apt[u % 2][:, 1, 0:w], ps[:, 5, 0:w]).then_inc(pt1, 1)

            def invert(u):
                n = units[u][2]
                dve.wait_ge(exped, exps_through(u))
                if u >= 4:
                    dve.wait_ge(out_made, u - 3)
                dve.reciprocal(m.arl[:, u % 4, 0:n], m.ars[:, u % 4, 0:n]).then_inc(inv, 1)

            def output(u):
                t, first, n = units[u]
                dve.wait_ge(valued, u + 1)
                dve.wait_ge(inv, u + 1)
                dve.tensor_tensor(m.ao[:, t, first * HD:(first + n) * HD].rearrange("p (i n) -> p i n", i=n),
                                  ps[:, 6 + u % 2, 0:n * P].rearrange("p (i n) -> p i n", i=n)[:, :, 0:HD],
                                  m.arl[:, u % 4, 0:n].unsqueeze(2).to_broadcast([P, n, HD]), ALU.mult).then_inc(out_made, 1)

            maxes(1)
            split_lo(len(tiles) - 1)
            for u in range(AU):
                invert(u)
                move1(u)
                if u + 2 < AU:
                    maxes(u + 2)
                if u >= 1:
                    output(u - 1)
            output(AU - 1)

            def out_lo(t):
                dve.wait_ge(oT_hi, t + 1)
                dve.tensor_tensor(m.aoTl[t % 2][:, :, :], out_turned(t), m.aoTh[t % 2][:, :, :].bitcast(F32),
                                  ALU.subtract).then_inc(oT_lo, 1)

            out_lo(0)
            out_lo(1)
            for t in range(NT):
                dve.wait_ge(wo_done, t + 1)
                if t + 2 < NT:
                    out_lo(t + 2)
                dve.wait_ge(xb, t + 1)
                dve.tensor_tensor(m.x[:, t, :], m.x[:, t, :], ps[:, 4 + t, :], ALU.add).then_inc(x2, 1)
                dve.wait_ge(x2, t + 1)
                ln.vector_normalize(dve, t)
                if t:
                    ln.vector_lo(dve, t - 1)
            ln.vector_lo(dve, NT - 1)


def feed_forward(nc, m, d, sem, s):
    lgT_ps, lgT, lg_ps, lg, top, eq, cand, first, onehot, th, score, rank_ps, own, rank, cnt, over, over_i = (
        sem(x) for x in ("lgT_summed", "lgT_made", "lg_turned", "lg_made", "top_made", "eq_made", "cand_made",
                         "first_made", "onehot_made", "tanh_made", "score_made", "rank_summed", "own_rank_made",
                         "rank_made", "counts_made", "over_made", "over_int_made"))
    xs, xs_hi, xs_lo = sem("xs_made"), sem("xs_hi_made"), sem("xs_lo_made")
    sh_in, sh_sil, sh_act, sh_hi, sh_lo, sh_out, x3 = (sem(x) for x in (
        "sh_projected", "sh_silu_made", "sh_act_made", "sh_act_hi_made", "sh_act_lo_made", "sh_down_done", "x3_made"))
    sel, selT_ps, selT, xg_ps, xg = (sem(x) for x in ("sel_made", "sel_turned", "selT_made", "gathered", "xg_made"))
    xg_hi, xg_lo = sem("xg_hi_made"), sem("xg_lo_made")
    gu, sil, act_made, a_ps, actT_hi, actT_lo, y_ps, y_hi, y_lo, put, added = (sem(x) for x in (
        "gu_done", "silu_made", "act_made", "act_turned", "actT_hi_made", "actT_lo_made", "y_done", "y_hi_made",
        "y_lo_made", "put_back", "put_added"))
    first_used = sem("first_of_pair_used")
    pieces = s.pieces
    count = len(pieces.order)
    BY_POOL = 3
    BY_VECTOR = 6
    ps = m.ps
    ident = m.const(C_IDENT, P)
    HALF = INNER // 2

    with nc.Block() as block:
        @block.sync
        def _(sp):
            for n in range(pieces.SLOTS, count):
                before = n - pieces.SLOTS
                e, name, half = pieces.order[before]
                if before % 2 == 0:
                    sp.wait_ge(first_used, before // 2 + 1)
                elif e == pieces.SHARED:
                    sp.wait_ge(sh_out if name == "down" else sh_in, 4 * (half + 1) if name == "up" else NT)
                elif name == "up":
                    sp.wait_ge(gu, 2 * e + half + 1)
                else:
                    sp.wait_ge(y_ps, e + 1)
                pieces.load(sp, n)

        @block.gpsimd
        def _(pool):
            zeros = m.const(C_ZERO).to_broadcast([P, DC, P])

            def split_tokens(e):
                own = m.xg[e // 4][:, :, e % 4 * P:(e % 4 + 1) * P]
                pool.wait_ge(xg, DC * (e // 4 + 1))
                if e >= 2:
                    pool.wait_ge(gu, 2 * (e - 1))
                pool.tensor_tensor(m.xgh[e % 2][:, :, :], own, zeros, ALU.add).then_inc(xg_hi, 1)
                pool.wait_ge(xg_hi, e + 1)
                pool.tensor_tensor(m.xgl[e % 2][:, :, :], own, m.xgh[e % 2][:, :, :].bitcast(F32),
                                   ALU.subtract).then_inc(xg_lo, 1)

            for n in range(pieces.SLOTS, count):
                if n == 2 * pieces.SLOTS - 1:
                    split_tokens(0)
                    split_tokens(1)
                if n % BY_POOL == BY_POOL - 1:
                    pieces.lo(pool, n)
                for e in range(2, E):
                    if n == pieces.number(e - 1, "gate", 0) + 4:
                        split_tokens(e)

        @block.tensor
        def _(pe):
            for c in range(DC):
                last = pe.matmul(ps[0:E, 4, :], m.gw[:, c, :], m.hT[:, c, :], start=c == 0, stop=c == DC - 1)
            last.then_inc(lgT_ps, 1)

            def shared_in(k):
                if k >= 2:
                    pe.wait_ge(sh_act, k - 1)
                    pe.wait_ge(sh_sil, k - 1)
                for name, bank in (("gate", k % 2), ("up", 2 + k % 2)):
                    n = pieces.number(pieces.SHARED, name, k // 4)
                    hi, lo = pieces.wait(pe, n)
                    col = slice(k % 4 * P, (k % 4 + 1) * P)
                    for c in range(DC):
                        last = product(pe, ps[:, bank, :], (hi[:, c, col], lo[:, c, col]), (m.hTh[:, c, :], m.hTl[:, c, :]),
                                       c == 0, c == DC - 1)
                    if k % 4 == 3 and name == "gate":
                        last.then_inc(first_used, 1)
                last.then_inc(sh_in, 1)

            shared_in(0)
            pe.wait_ge(lgT, 1)
            for t in range(NT):
                last = pe.transpose(ps[:, 5, t * E:(t + 1) * E], m.lgt[:, t * P:(t + 1) * P], m.const(C_IDENT, E, E))
            last.then_inc(lg_ps, 1)
            shared_in(1)
            shared_in(2)
            pe.wait_ge(onehot, 2)
            pe.matmul(ps[:, 6, 0:(NT + 1) * E], m.const(C_TRI, P), m.onehot[:, :, :], start=True, stop=False)
            for s in range(1, NT + 1):
                last = pe.matmul(ps[:, 6, s * E:(NT + 1) * E], m.const(C_ONES, P), m.onehot[:, 0:NT + 1 - s, :],
                                 start=False, stop=s == NT)
            last.then_inc(rank_ps, 1)
            for k in range(3, IC):
                shared_in(k)
            pe.wait_ge(cnt, 1)

            def gather(half):
                pe.wait_ge(sel, 16 * (half + 1))
                for c in range(DC):
                    bank = 6 + c % 2 if half else c
                    if half:
                        pe.wait_ge(selT, 4)
                        if c >= 2:
                            pe.wait_ge(xg, DC + c - 1)
                    for t in range(NT):
                        for part in (m.xsh, m.xsl):
                            last = pe.matmul(ps[:, bank, :], part[:, t, c * P:(c + 1) * P], m.sel[:, t, :, :],
                                             start=t == 0 and part is m.xsh, stop=t == NT - 1 and part is m.xsl)
                    last.then_inc(xg_ps, 1)

            def turn_sel(half):
                for q in range(4):
                    if q >= 2:
                        pe.wait_ge(selT, 4 * half + q - 1)
                    elif half:
                        pe.wait_ge(xg, 2 * DC - 1 + q)
                    else:
                        pe.wait_ge(x3, 3 + q)
                    for t in range(NT):
                        last = pe.transpose(ps[:, 6 + q % 2, t * P:(t + 1) * P], m.sel[:, t, q, :].bitcast(F32), ident)
                    last.then_inc(selT_ps, 1)

            for half in range(2):
                n = pieces.number(pieces.SHARED, "down", half)
                hi, lo = pieces.wait(pe, n)
                for t in range(NT):
                    tok = slice(t * P, (t + 1) * P)
                    for k in range(4):
                        row = 4 * half + k
                        pe.wait_ge(sh_hi, row + 1)
                        pe.wait_ge(sh_lo, row + 1)
                        last = product(pe, ps[:, 4 + t, :], (m.sacth[:, row, tok], m.sactl[:, row, tok]),
                                       (hi[:, k, :], lo[:, k, :]), half == 0 and k == 0, half == 1 and k == 3)
                    if half:
                        last.then_inc(sh_out, 1)
                    elif t == NT - 1:
                        last.then_inc(first_used, 1)
                if half == 0:
                    pe.wait_ge(xs_lo, NT)
                    pe.wait_ge(sh_act, IC)
                    gather(0)

            def gate_up(e, half):
                if half == 0:
                    pe.wait_ge(xg_lo, e + 1)
                if e:
                    pe.wait_ge(act_made, 2 * (e - 1) + half + 1)
                for name, bank in (("gate", 2 * half), ("up", 2 * half + 1)):
                    hi, lo = pieces.wait(pe, pieces.number(e, name, half))
                    for c in range(DC):
                        last = product(pe, ps[:, bank, :], (m.xgh[e % 2][:, c, :], m.xgl[e % 2][:, c, :]),
                                       (hi[:, c, :], lo[:, c, :]), c == 0, c == DC - 1)
                    if name == "gate":
                        last.then_inc(first_used, 1)
                last.then_inc(gu, 1)

            def turn_act(e, half):
                n = 2 * e + half
                pe.wait_ge(act_made, n + 1)
                if n:
                    pe.wait_ge(actT_lo, n)
                for k in range(4):
                    last = pe.transpose(ps[:, 4, k * P:(k + 1) * P], m.act[:, (4 * half + k) * P:(4 * half + k + 1) * P], ident)
                last.then_inc(a_ps, 1)

            def down(e):
                pe.wait_ge(actT_lo, 2 * e + 2)
                if e:
                    pe.wait_ge(y_lo, e)
                for half in range(2):
                    hi, lo = pieces.wait(pe, pieces.number(e, "down", half))
                    for k in range(4):
                        row = slice((4 * half + k) * P, (4 * half + k + 1) * P)
                        last = product(pe, ps[:, 5, :], (m.actTh[e % 2][:, row], m.actTl[e % 2][:, row]),
                                       (hi[:, k, :], lo[:, k, :]), half == 0 and k == 0, half == 1 and k == 3)
                    if half == 0:
                        last.then_inc(first_used, 1)
                last.then_inc(y_ps, 1)

            last_bank = [6, 7, 0, 1]

            def put_back(half, t, bank, experts):
                for q in experts:
                    pe.wait_ge(y_lo, 4 * half + q + 1)
                    for part in (m.yh, m.yl):
                        last = pe.matmul(ps[:, bank, :], m.selT[:, 4 * half + q, t * P:(t + 1) * P], part[:, q, :],
                                         start=q == 0 and part is m.yh, stop=q == 3 and part is m.yl)
                if experts[-1] == 3:
                    last.then_inc(put, 1)

            for e in range(E):
                gate_up(e, 0)
                if e:
                    turn_act(e - 1, 1)
                else:
                    turn_sel(0)
                gate_up(e, 1)
                turn_act(e, 0)
                if e == 0:
                    gather(1)
                    turn_sel(1)
                if e == 5:
                    for t in range(NT):
                        if t >= 2:
                            pe.wait_ge(added, t - 1)
                        put_back(0, t, 6 + t % 2, range(4))
                if e:
                    down(e - 1)
            turn_act(E - 1, 1)
            pe.wait_ge(added, NT)
            for t in range(NT):
                put_back(1, t, last_bank[t], range(3))
            down(E - 1)
            for t in range(NT):
                put_back(1, t, last_bank[t], range(3, 4))

        @block.scalar
        def _(act):
            def hi_of_act(n):
                e, half = n // 2, n % 2
                act.wait_ge(a_ps, n + 1)
                if e >= 2:
                    act.wait_ge(y_ps, e - 1)
                act.activation(m.actTh[e % 2][:, half * HALF:(half + 1) * HALF], ps[:, 4, :], ACT.Copy).then_inc(actT_hi, 1)

            def hi_of_y(e):
                act.wait_ge(y_ps, e + 1)
                if e >= 4:
                    act.wait_ge(put, NT)
                act.activation(m.yh[:, e % 4, :], ps[:, 5, :], ACT.Copy).then_inc(y_hi, 1)

            def split(before, end):
                for n in range(before, min(end, count)):
                    if n % BY_VECTOR:
                        pieces.scalar_hi(act, n)

            act.wait_ge(lgT_ps, 1)
            act.activation(m.lgt[:, :], ps[0:E, 4, :], ACT.Copy).then_inc(lgT, 1)

            def shared_silu(k):
                act.wait_ge(sh_in, k + 1)
                if k >= 2:
                    act.wait_ge(sh_lo, k - 1)
                if k < 2:
                    act.wait_ge(lg_ps, 1)
                act.activation(m.sil[k % 2][:, :], ps[:, k % 2, :], ACT.Silu).then_inc(sh_sil, 1)

            shared_silu(0)
            shared_silu(1)
            act.wait_ge(top, 1)
            act.activation(m.score[:, :], m.top[:, :], ACT.Tanh, scale=0.5).then_inc(th, 1)
            for k in range(2, IC):
                shared_silu(k)
                if k == 5:
                    split(6, 8)
            act.wait_ge(sh_in, IC)
            for t in range(NT):
                act.wait_ge(xs, t + 1)
                act.activation(m.xsh[:, t, :], m.h[:, t, :], ACT.Copy).then_inc(xs_hi, 1)
            split(8, 10)

            def keep_gathered(half):
                for c in range(DC):
                    act.wait_ge(xg_ps, half * DC + c + 1)
                    act.activation(m.xg[half][:, c, :], ps[:, 6 + c % 2 if half else c, :], ACT.Copy).then_inc(xg, 1)

            keep_gathered(0)
            split(10, 11)
            for e in range(E):
                for half in range(2):
                    n, q = 2 * e + half, pieces.number(e, "gate", half)
                    if n:
                        split(q + 4, q + 5)
                    act.wait_ge(gu, n + 1)
                    if e:
                        act.wait_ge(a_ps, n - 1)
                    act.activation(m.act[:, half * HALF:(half + 1) * HALF], ps[:, 2 * half, :], ACT.Silu).then_inc(sil, 1)
                    if n:
                        hi_of_act(n - 1)
                    if n == 1:
                        keep_gathered(1)
                    split(q + 5, q + 6)
                if e:
                    q = pieces.number(e - 1, "down", 0)
                    split(q + 4, q + 5)
                    hi_of_y(e - 1)
                    split(q + 5, q + 6)
            hi_of_act(2 * E - 1)
            hi_of_y(E - 1)

        @block.vector
        def _(dve):
            def shared_act(k):
                dve.wait_ge(sh_sil, k + 1)
                own = m.sil[k % 2][:, :]
                dve.tensor_tensor(own, own, ps[:, 2 + k % 2, :], ALU.mult).then_inc(sh_act, 1)
                dve.wait_ge(sh_act, k + 1)
                dve.tensor_copy(m.sacth[:, k, :], own).then_inc(sh_hi, 1)
                dve.wait_ge(sh_hi, k + 1)
                dve.tensor_tensor(m.sactl[:, k, :], own, m.sacth[:, k, :].bitcast(F32), ALU.subtract).then_inc(sh_lo, 1)

            dve.wait_ge(lg_ps, 1)
            dve.tensor_copy(m.lg[:, :, :], ps[:, 5, 0:NT * E].rearrange("p (t e) -> p t e", t=NT)).then_inc(lg, 1)
            dve.wait_ge(lg, 1)
            dve.tensor_reduce(m.top[:, :], m.lg[:, :, :], AX, ALU.max).then_inc(top, 1)
            dve.wait_ge(top, 1)
            wide = [P, NT, E]
            dve.tensor_tensor(m.eq[:, :, :], m.lg[:, :, :], m.top[:, :].unsqueeze(2).to_broadcast(wide), ALU.is_equal).then_inc(eq, 1)
            dve.wait_ge(eq, 1)
            dve.tensor_tensor(m.tmp8[:, :, :], m.eq[:, :, :], m.const(C_PREF, E).unsqueeze(1).to_broadcast(wide), ALU.mult).then_inc(cand, 1)
            dve.wait_ge(cand, 1)
            dve.tensor_reduce(m.first[:, :], m.tmp8[:, :, :], AX, ALU.max).then_inc(first, 1)
            dve.wait_ge(first, 1)
            dve.memset(m.onehot[:, NT, :], 0.0).then_inc(onehot, 1)
            dve.tensor_tensor(m.onehot[:, 0:NT, :], m.tmp8[:, :, :], m.first[:, :].unsqueeze(2).to_broadcast(wide), ALU.is_equal).then_inc(onehot, 1)
            shared_act(0)
            dve.wait_ge(th, 1)
            dve.tensor_scalar(m.score[:, :], m.score[:, :], 0.5, 0.5, ALU.mult, ALU.add).then_inc(score, 1)
            dve.wait_ge(score, 1)
            for t in range(NT):
                dve.tensor_scalar(m.h[:, t, :], m.h[:, t, :], m.score[:, t:t + 1], None, ALU.mult).then_inc(xs, 1)
            shared_act(1)
            shared_act(2)
            dve.wait_ge(rank_ps, 1)
            dve.wait_ge(onehot, 2)
            dve.tensor_tensor(m.tmp8[:, :, :], ps[:, 6, 0:NT * E].rearrange("p (t e) -> p t e", t=NT), m.onehot[:, 0:NT, :], ALU.mult).then_inc(own, 1)
            dve.tensor_reduce(m.over[:, :], ps[:, 6, NT * E:(NT + 1) * E], AX, ALU.max).then_inc(cnt, 1)
            dve.wait_ge(own, 1)
            dve.tensor_reduce(m.rank[:, :], m.tmp8[:, :, :], AX, ALU.add).then_inc(rank, 1)
            dve.wait_ge(cnt, 1)
            dve.tensor_scalar(m.over[:, :], m.over[:, :], -float(P), 0.0, ALU.add, ALU.max).then_inc(over, 1)
            dve.wait_ge(over, 1)
            dve.tensor_copy(m.over_i[:, :], m.over[:, :]).then_inc(over_i, 1)
            def split(before, end):
                for n in range(before, min(end, count)):
                    if n % BY_VECTOR == 0:
                        pieces.vector_hi(dve, n)
                    if n % BY_POOL != BY_POOL - 1:
                        pieces.lo(dve, n)

            def select(half):
                if half:
                    dve.wait_ge(xg_ps, DC)
                    dve.wait_ge(selT_ps, 4)
                for t in range(NT):
                    for q in range(4):
                        dve.tensor_scalar(m.sel[:, t, q, :], m.const(C_IOTA, P), m.rank[:, t:t + 1],
                                          m.onehot[:, t, 4 * half + q:4 * half + q + 1], ALU.is_equal, ALU.mult).then_inc(sel, 1)

            def move_sel(half):
                for q in range(4):
                    e = 4 * half + q
                    dve.wait_ge(selT_ps, e + 1)
                    dve.tensor_copy(m.selT[:, e, :], ps[:, 6 + q % 2, :]).then_inc(selT, 1)

            dve.wait_ge(rank, 1)
            for k in range(3, IC):
                shared_act(k)
                if k == 4:
                    select(0)
                if k == 5:
                    split(6, 8)
            for t in range(NT):
                dve.wait_ge(xs_hi, t + 1)
                dve.tensor_tensor(m.xsl[:, t, :], m.h[:, t, :], m.xsh[:, t, :].bitcast(F32), ALU.subtract).then_inc(xs_lo, 1)
            split(8, 10)
            for t in range(NT):
                dve.wait_ge(sh_out, t + 1)
                dve.tensor_tensor(m.x[:, t, :], m.x[:, t, :], ps[:, 4 + t, :], ALU.add).then_inc(x3, 1)
            split(10, 12)

            def act_of(n):
                e, half = n // 2, n % 2
                a = m.act[:, half * HALF:(half + 1) * HALF]
                dve.wait_ge(sil, n + 1)
                dve.tensor_tensor(a, a, ps[:, 2 * half + 1, :], ALU.mult).then_inc(act_made, 1)

            def lo_of_act(n):
                e, half = n // 2, n % 2
                own = slice(half * HALF, (half + 1) * HALF)
                dve.wait_ge(actT_hi, n + 1)
                dve.tensor_tensor(m.actTl[e % 2][:, own], ps[:, 4, :], m.actTh[e % 2][:, own].bitcast(F32),
                                  ALU.subtract).then_inc(actT_lo, 1)

            def lo_of_y(e):
                dve.wait_ge(y_hi, e + 1)
                dve.tensor_tensor(m.yl[:, e % 4, :], ps[:, 5, :], m.yh[:, e % 4, :].bitcast(F32), ALU.subtract).then_inc(y_lo, 1)

            def add_back(half):
                for t in range(NT):
                    n = 4 * half + t
                    dve.wait_ge(put, n + 1)
                    dve.wait_ge(added, n - 3) if n >= 4 else dve.wait_ge(x3, t + 1)
                    bank = (6, 7, 0, 1)[t] if half else 6 + t % 2
                    dve.tensor_tensor(m.x[:, t, :], m.x[:, t, :], ps[:, bank, :], ALU.add).then_inc(added, 1)

            for e in range(E):
                for half in range(2):
                    n, q = 2 * e + half, pieces.number(e, "gate", half)
                    if n:
                        split(q + 4, q + 5)
                    act_of(n)
                    if n == 0:
                        move_sel(0)
                        select(1)
                    if n:
                        lo_of_act(n - 1)
                        if n == 1:
                            move_sel(1)
                        split(q + 5, q + 6)
                if e:
                    q = pieces.number(e - 1, "down", 0)
                    if e == 5:
                        add_back(0)
                    split(q + 4, q + 5)
                    lo_of_y(e - 1)
                    split(q + 5, q + 6)
            lo_of_act(2 * E - 1)
            lo_of_y(E - 1)
            add_back(1)


def overflow(nc, m, d, sem):
    loaded, moved, sel, selT_ps, selT, xg_ps, xg, gu, sil, act_made, a_ps, actT, y_ps, y_hi, y_lo, put, added, xs_hi, xs_lo = (
        sem("over_" + x) for x in ("loaded", "rank_moved", "sel", "selT_ps", "selT", "xg_ps", "xg", "gu", "silu", "act",
                                   "act_turned", "actT", "y", "y_hi", "y_lo", "put", "added", "xs_hi", "xs_lo"))
    ps = m.ps
    ident = m.const(C_IDENT, P)
    ROUNDS = (N - 1) // P
    HALF = INNER // 2

    def rounds(eng, body):
        with eng.Fori(0, ROUNDS) as tile:
            with eng.Fori(0, E) as e:
                body(tile, e, tile * E + e)

    with nc.Block() as block:
        @block.gpsimd
        def _(pool):
            pool.memset(m.over[:, :], 0.0).then_inc(added, 1)

        @block.sync
        def _(sp):
            def body(tile, e, n):
                sp.wait_ge(added, n * NT + 1)
                for w, name in ((m.wg, "rt_gate"), (m.wu, "rt_up"), (m.wd, "rt_down")):
                    sp.dma_start(w[:, :, :], d[name][e].rearrange("(c p) n -> p c n", p=P)).then_inc(loaded, 16)

            rounds(sp, body)

        @block.tensor
        def _(pe):
            pe.wait_ge(xs_lo, 1)

            def body(tile, e, n):
                pe.wait_ge(sel, n * NT + NT)
                for t in range(NT):
                    last = pe.transpose(ps[:, 0, t * P:(t + 1) * P], m.osel[:, t, :].bitcast(F32), ident)
                last.then_inc(selT_ps, 1)
                for c in range(DC):
                    for t in range(NT):
                        for part in (m.xsh, m.xsl):
                            last = pe.matmul(ps[:, 1, c * P:(c + 1) * P], part[:, t, c * P:(c + 1) * P], m.osel[:, t, :],
                                             start=t == 0 and part is m.xsh, stop=t == NT - 1 and part is m.xsl)
                last.then_inc(xg_ps, 1)
                pe.wait_ge(xg, n + 1)
                pe.wait_ge(loaded, n * 48 + 48)
                for half in range(2):
                    for w, bank in ((m.wg, 2 + 2 * half), (m.wu, 3 + 2 * half)):
                        for c in range(DC):
                            last = pe.matmul(ps[:, bank, :], m.oxg[:, c, :], w[:, c, half * HALF:(half + 1) * HALF],
                                             start=c == 0, stop=c == DC - 1)
                    last.then_inc(gu, 1)
                pe.wait_ge(act_made, n * 2 + 2)
                for k in range(IC):
                    last = pe.transpose(ps[:, 6 + k // 4, k % 4 * P:(k % 4 + 1) * P], m.oact[:, k * P:(k + 1) * P], ident)
                last.then_inc(a_ps, 1)
                pe.wait_ge(actT, n + 1)
                for k in range(IC):
                    last = pe.matmul(ps[:, 0, :], m.oactT[:, k * P:(k + 1) * P], m.wd[:, k, :], start=k == 0, stop=k == IC - 1)
                last.then_inc(y_ps, 1)
                pe.wait_ge(y_lo, n + 1)
                for t in range(NT):
                    for part in (m.oyh, m.oyl):
                        last = pe.matmul(ps[:, 2 + t, :], m.oselT[:, t * P:(t + 1) * P], part[:, :],
                                         start=part is m.oyh, stop=part is m.oyl)
                last.then_inc(put, 1)

            rounds(pe, body)

        @block.scalar
        def _(act):
            act.activation(m.xsh[:, :, :], m.h[:, :, :], ACT.Copy).then_inc(xs_hi, 1)

            def body(tile, e, n):
                act.wait_ge(selT_ps, n + 1)
                act.activation(m.oselT[:, :], ps[:, 0, :], ACT.Copy).then_inc(selT, 1)
                act.wait_ge(xg_ps, n + 1)
                act.activation(m.oxg[:, :, :], ps[:, 1, :].rearrange("p (c n) -> p c n", c=DC), ACT.Copy).then_inc(xg, 1)
                for half in range(2):
                    act.wait_ge(gu, n * 2 + half + 1)
                    act.activation(m.oact[:, half * HALF:(half + 1) * HALF], ps[:, 2 + 2 * half, :], ACT.Silu).then_inc(sil, 1)
                act.wait_ge(a_ps, n + 1)
                act.activation(m.oactT[:, :], ps[:, 6:8, :], ACT.Copy).then_inc(actT, 1)
                act.wait_ge(y_ps, n + 1)
                act.activation(m.oyh[:, :], ps[:, 0, :], ACT.Copy).then_inc(y_hi, 1)

            rounds(act, body)

        @block.vector
        def _(dve):
            dve.tensor_scalar(m.rank[:, :], m.rank[:, :], -float(P), None, ALU.add).then_inc(moved, 1)
            dve.wait_ge(xs_hi, 1)
            dve.tensor_tensor(m.xsl[:, :, :], m.h[:, :, :], m.xsh[:, :, :].bitcast(F32), ALU.subtract).then_inc(xs_lo, 1)

            def body(tile, e, n):
                dve.wait_ge(added, n * NT + 1)
                dve.wait_ge(moved, tile + 1)
                for t in range(NT):
                    dve.tensor_scalar(m.osel[:, t, :], m.const(C_IOTA, P), m.rank[:, t:t + 1], m.onehot[:, t, bass.ds(e, 1)],
                                      ALU.is_equal, ALU.mult).then_inc(sel, 1)
                for half in range(2):
                    dve.wait_ge(sil, n * 2 + half + 1)
                    a = m.oact[:, half * HALF:(half + 1) * HALF]
                    dve.tensor_tensor(a, a, ps[:, 3 + 2 * half, :], ALU.mult).then_inc(act_made, 1)
                dve.wait_ge(y_hi, n + 1)
                dve.tensor_tensor(m.oyl[:, :], ps[:, 0, :], m.oyh[:, :].bitcast(F32), ALU.subtract).then_inc(y_lo, 1)
                dve.wait_ge(put, n + 1)
                for t in range(NT):
                    dve.tensor_tensor(m.x[:, t, :], m.x[:, t, :], ps[:, 2 + t, :], ALU.add).then_inc(added, 1)

            with dve.Fori(0, ROUNDS) as tile:
                with dve.Fori(0, E) as e:
                    body(tile, e, tile * E + e)
                dve.wait_ge(sel, (tile + 1) * E * NT)
                dve.tensor_scalar(m.rank[:, :], m.rank[:, :], -float(P), None, ALU.add).then_inc(moved, 1)


def store(nc, m, out, stored):
    with nc.Block() as block:
        @block.sync
        def _(sp):
            sp.dma_start(out.rearrange("o (t p) d -> p (o t) d", p=P), m.x[:, :, :]).then_inc(stored, 16)
            sp.wait_ge(stored, 16)


class Signals:
    pass


def perceiver_block(nc, d, out, phases=6):
    with ExitStack() as ctx:
        m = Memory(nc, ctx)
        s = Signals()

        made = []

        def sem(name):
            made.append(nc.alloc_semaphore(name))
            return made[-1]

        stored = nc.alloc_semaphore("stored")
        if phases > 1:
            cross_attention(nc, m, d, sem, s)
            cross_output(nc, m, d, sem, s)
            nc.clear_and_free_semaphores(made[:])
            nc.all_engine_barrier()
            made.clear()
        if phases > 2:
            self_attention(nc, m, d, sem, s)
        if phases > 3:
            feed_forward(nc, m, d, sem, s)
        if phases > 4:
            beyond = nc.values_load(m.over_i[0:1, 0:1], min_val=0, max_val=N,
                                    skip_runtime_bounds_check_because="a count of tokens less 128, not below 0")
            with nc.If(beyond > 0):
                nc.clear_and_free_semaphores(made[:])
                nc.all_engine_barrier()
                overflow(nc, m, d, sem)
        store(nc, m, out, stored)


_NAMES = {"x": "x", "ctx_1024": "ctx", "L0_xattn_w_sim": "w_sim", "L0_xattn_b_sim": "b_sim", "L0_xattn_W_qv": "W_qv",
          "L0_xattn_b_qv": "b_qv", "L0_attn_Wq": "Wq", "L0_attn_bq": "bq", "L0_attn_Wk": "Wk", "L0_attn_bk": "bk",
          "L0_attn_Wv": "Wv", "L0_attn_bv": "bv", "L0_attn_Wo": "Wo", "L0_attn_bo": "bo", "L0_ffn_gate_w": "gate_w",
          "L0_ffn_sh_gate": "sh_gate", "L0_ffn_sh_up": "sh_up", "L0_ffn_sh_down": "sh_down",
          "L0_ffn_rt_gate": "rt_gate", "L0_ffn_rt_up": "rt_up", "L0_ffn_rt_down": "rt_down"}


def kernel(**inputs):
    import concourse.bacc as bacc
    from concourse.bass_utils import run_bass_kernel_spmd

    nc = bacc.Bacc("TRN2", target_bir_lowering=False, num_devices=1)
    arrays = {_NAMES[k]: np.ascontiguousarray(v) for k, v in inputs.items()}
    arrays["consts"] = constants()
    arrays = {f"in_{k}": v for k, v in arrays.items()}
    d = {k[3:]: nc.dram_tensor(k, v.shape, mybir.dt.from_np(v.dtype), kind="ExternalInput").ap() for k, v in arrays.items()}
    out = nc.dram_tensor("out", (1, N, D), F32, kind="ExternalOutput").ap()
    perceiver_block(nc, d, out)
    r = run_bass_kernel_spmd(nc, [arrays], core_ids=[0])
    return r.results[0]["out"]
```
